# Optimizing a Trainium2 kernel written in Bass

```python
import numpy as np
import jax
import jax.numpy as jnp

def _softmax(x, axis=-1):
    return jax.nn.softmax(x, axis=axis)

def _gelu(x):
    return jax.nn.gelu(x, approximate=True)

def _silu(x):
    return jax.nn.silu(x)

def _sigmoid(x):
    return jax.nn.sigmoid(x)

def _layernorm(x, axis=-1, eps=1e-05):
    m = jnp.mean(x, axis=axis, keepdims=True)
    v = jnp.var(x, axis=axis, keepdims=True)
    return (x - m) / jnp.sqrt(v + eps)

def _scatter_add(tgt, idx, src, axis=0):
    return tgt.at[idx].add(src)

def _segment_sum(src, seg, n):
    return jax.ops.segment_sum(src, seg, n)
kernel_name = 'mk_vit_tower_d2_tok_img1024_r4_9ea8b9'

def setup_inputs(seed: int=0):
    np.random.seed(seed)
    _w = jnp.asarray

    def _rec_inputs():
        import jax
        import jax.numpy as jnp
        _rk = jax.random.key(seed)
        x = -7.10856e-05 + 0.999911 * jax.random.normal(jax.random.fold_in(_rk, 1), (2, 1024, 256, 4), jnp.float32)
        return x
    x = _rec_inputs()

    def _L0_tok_setup():
        import jax, jax.numpy as jnp
        import numpy as np
        B, T, D, DV = (4, 1024, 256, 4)
        K = 4
        C = D * DV
        key = jax.random.key(seed)
        k1, k2, k3 = jax.random.split(key, 3)
        x = jax.random.normal(k1, (B, T, D, DV), dtype=jnp.float32)
        conv_w = jax.random.normal(k2, (C, K), dtype=jnp.float32) * (1.0 / np.sqrt(K))
        conv_b = jax.random.normal(k3, (C,), dtype=jnp.float32) * 0.02
        read = jnp.full((DV,), 1.0 / DV, dtype=jnp.float32)
        return {'x': x, 'conv_w': conv_w, 'conv_b': conv_b, 'read': read}
    _L0_tok_all = _L0_tok_setup()
    _L0_tok_in = {k: v for k, v in _L0_tok_all.items() if k in ('conv_w', 'conv_b', 'read')}
    del _L0_tok_all

    def _L0_attn_setup():
        import jax, jax.numpy as jnp
        import numpy as np
        D_MODEL = 256
        N_HEADS = 16
        D_HEAD = 64
        ROTARY_DIM = 64
        ROTARY_BASE = 10000.0
        ATTN_SCALE = 8.0

        def _rope_sin_cos(n_pos, rotary_dim):
            pos = jnp.arange(n_pos, dtype=jnp.float32)
            dim = jnp.arange(rotary_dim // 2, dtype=jnp.float32)
            freq = ROTARY_BASE ** (dim / (rotary_dim / 2))
            freq = jnp.concatenate([freq, freq])
            angles = pos[:, None] / freq[None, :]
            return (jnp.sin(angles), jnp.cos(angles))

        def _apply_rotary(x, sin, cos):
            n = x.shape[-1] // 2
            x_flip = jnp.concatenate([-x[..., n:], x[..., :n]], axis=-1)
            return x * cos[None, :, None, :] + x_flip * sin[None, :, None, :]
        key = jax.random.key(seed)
        ks = jax.random.split(key, 9)
        std = 0.02
        x = jax.random.normal(ks[0], (2, 512, D_MODEL), dtype=jnp.float32)
        W_Q = jax.random.normal(ks[1], (N_HEADS, D_MODEL, D_HEAD), dtype=jnp.float32) * std
        W_K = jax.random.normal(ks[2], (N_HEADS, D_MODEL, D_HEAD), dtype=jnp.float32) * std
        W_V = jax.random.normal(ks[3], (N_HEADS, D_MODEL, D_HEAD), dtype=jnp.float32) * std
        W_O = jax.random.normal(ks[4], (N_HEADS, D_HEAD, D_MODEL), dtype=jnp.float32) * std
        b_Q = jnp.zeros((N_HEADS, D_HEAD), dtype=jnp.float32)
        b_K = jnp.zeros((N_HEADS, D_HEAD), dtype=jnp.float32)
        b_V = jnp.zeros((N_HEADS, D_HEAD), dtype=jnp.float32)
        b_O = jnp.zeros((D_MODEL,), dtype=jnp.float32)
        return {'x': x, 'W_Q': W_Q, 'b_Q': b_Q, 'W_K': W_K, 'b_K': b_K, 'W_V': W_V, 'b_V': b_V, 'W_O': W_O, 'b_O': b_O}
    _L0_attn_all = _L0_attn_setup()
    _L0_attn_in = {k: v for k, v in _L0_attn_all.items() if k in ('W_Q', 'b_Q', 'W_K', 'b_K', 'W_V', 'b_V', 'W_O', 'b_O')}
    del _L0_attn_all

    def _L0_ffn_setup():
        import jax, jax.numpy as jnp
        import numpy as np
        B, S, D, F, E = (4, 512, 256, 1024, 8)
        key = jax.random.key(seed)
        ks = jax.random.split(key, 7)
        s1 = 1.0 / np.sqrt(D)
        s2 = 1.0 / np.sqrt(F)
        x = jax.random.normal(ks[0], (B, S, D), dtype=jnp.float32)
        W1 = jax.random.uniform(ks[1], (E, D, F), jnp.float32, -s1, s1)
        b1 = jax.random.uniform(ks[2], (E, F), jnp.float32, -s1, s1)
        W2 = jax.random.uniform(ks[3], (E, F, D), jnp.float32, -s2, s2)
        b2 = jax.random.uniform(ks[4], (E, D), jnp.float32, -s2, s2)
        Wr = jax.random.uniform(ks[5], (D, E), jnp.float32, -s1, s1)
        br = jax.random.uniform(ks[6], (E,), jnp.float32, -s1, s1)
        return {'x': x, 'W1': W1, 'b1': b1, 'W2': W2, 'b2': b2, 'Wr': Wr, 'br': br}
    _L0_ffn_all = _L0_ffn_setup()
    _L0_ffn_in = {k: v for k, v in _L0_ffn_all.items() if k in ('W1', 'b1', 'W2', 'b2', 'Wr', 'br')}
    del _L0_ffn_all

    def _L1_attn_setup():
        import jax, jax.numpy as jnp
        import numpy as np
        EPS = 1e-08

        def elu_feature_map(x):
            return jax.nn.elu(x) + 1.0
        key = jax.random.key(seed)
        ks = jax.random.split(key, 5)
        B, S, D = (2, 1024, 256)
        scale = 1.0 / np.sqrt(D).astype(np.float32)
        x = jax.random.normal(ks[0], (B, S, D), dtype=jnp.float32)
        Wq = jax.random.normal(ks[1], (D, D), dtype=jnp.float32) * scale
        Wk = jax.random.normal(ks[2], (D, D), dtype=jnp.float32) * scale
        Wv = jax.random.normal(ks[3], (D, D), dtype=jnp.float32) * scale
        Wo = jax.random.normal(ks[4], (D, D), dtype=jnp.float32) * scale
        return {'x': x, 'Wq': Wq, 'Wk': Wk, 'Wv': Wv, 'Wo': Wo}
    _L1_attn_all = _L1_attn_setup()
    _L1_attn_in = {k: v for k, v in _L1_attn_all.items() if k in ('Wq', 'Wk', 'Wv', 'Wo')}
    del _L1_attn_all

    def _L1_ffn_setup():
        import jax, jax.numpy as jnp
        import numpy as np
        B, L, C1, C2, K, K_IN = (4, 256, 256, 256, 32, 32)
        BN_EPS = 1e-05

        def _gated_bottleneck(x2d, conv_w, conv_b, gamma, beta, lin_w, lin_b):
            n = x2d.shape[0]
            g = conv_w.shape[0]
            xc = jnp.einsum('ngf,gf->ng', x2d.reshape(n, g, 4), conv_w) + conv_b
            mean = jnp.mean(xc, axis=0)
            var = jnp.mean((xc - mean) ** 2, axis=0)
            xn = (xc - mean) * jax.lax.rsqrt(var + BN_EPS) * gamma + beta
            xa = jax.nn.gelu(xn, approximate=False)
            return xa @ lin_w.T + lin_b
        key = jax.random.key(seed)
        ks = jax.random.split(key, 8)
        g = C1 // 4
        w_std = (2.0 / C2) ** 0.5
        lin_std = (1.0 / g) ** 0.5
        return {'x': jax.random.normal(ks[0], (B, L, C1), jnp.float32), 'weight': jax.random.normal(ks[1], (C1, C2), jnp.float32) * w_std, 'bias': jnp.zeros((C2,), jnp.float32), 'so_conv_w': jax.random.normal(ks[2], (g, 4), jnp.float32) * 0.5, 'so_conv_b': jnp.zeros((g,), jnp.float32), 'so_gamma': jnp.ones((g,), jnp.float32), 'so_beta': jnp.zeros((g,), jnp.float32), 'so_lin_w': jax.random.normal(ks[3], (C2, g), jnp.float32) * lin_std, 'so_lin_b': jnp.zeros((C2,), jnp.float32), 'si_conv_w': jax.random.normal(ks[4], (g, 4), jnp.float32) * 0.5, 'si_conv_b': jnp.zeros((g,), jnp.float32), 'si_gamma': jnp.ones((g,), jnp.float32), 'si_beta': jnp.zeros((g,), jnp.float32), 'si_lin_w': jax.random.normal(ks[5], (C1, g), jnp.float32) * lin_std, 'si_lin_b': jnp.zeros((C1,), jnp.float32)}
    _L1_ffn_all = _L1_ffn_setup()
    _L1_ffn_in = {k: v for k, v in _L1_ffn_all.items() if k in ('weight', 'bias', 'so_conv_w', 'so_conv_b', 'so_gamma', 'so_beta', 'so_lin_w', 'so_lin_b', 'si_conv_w', 'si_conv_b', 'si_gamma', 'si_beta', 'si_lin_w', 'si_lin_b')}
    del _L1_ffn_all
    return {'x': x, 'L0_tok_conv_w': _L0_tok_in['conv_w'], 'L0_tok_conv_b': _L0_tok_in['conv_b'], 'L0_tok_read': _L0_tok_in['read'], 'L0_attn_W_Q': _L0_attn_in['W_Q'], 'L0_attn_b_Q': _L0_attn_in['b_Q'], 'L0_attn_W_K': _L0_attn_in['W_K'], 'L0_attn_b_K': _L0_attn_in['b_K'], 'L0_attn_W_V': _L0_attn_in['W_V'], 'L0_attn_b_V': _L0_attn_in['b_V'], 'L0_attn_W_O': _L0_attn_in['W_O'], 'L0_attn_b_O': _L0_attn_in['b_O'], 'L0_ffn_W1': _L0_ffn_in['W1'], 'L0_ffn_b1': _L0_ffn_in['b1'], 'L0_ffn_W2': _L0_ffn_in['W2'], 'L0_ffn_b2': _L0_ffn_in['b2'], 'L0_ffn_Wr': _L0_ffn_in['Wr'], 'L0_ffn_br': _L0_ffn_in['br'], 'L1_attn_Wq': _L1_attn_in['Wq'], 'L1_attn_Wk': _L1_attn_in['Wk'], 'L1_attn_Wv': _L1_attn_in['Wv'], 'L1_attn_Wo': _L1_attn_in['Wo'], 'L1_ffn_weight': _L1_ffn_in['weight'], 'L1_ffn_bias': _L1_ffn_in['bias'], 'L1_ffn_so_conv_w': _L1_ffn_in['so_conv_w'], 'L1_ffn_so_conv_b': _L1_ffn_in['so_conv_b'], 'L1_ffn_so_gamma': _L1_ffn_in['so_gamma'], 'L1_ffn_so_beta': _L1_ffn_in['so_beta'], 'L1_ffn_so_lin_w': _L1_ffn_in['so_lin_w'], 'L1_ffn_so_lin_b': _L1_ffn_in['so_lin_b'], 'L1_ffn_si_conv_w': _L1_ffn_in['si_conv_w'], 'L1_ffn_si_conv_b': _L1_ffn_in['si_conv_b'], 'L1_ffn_si_gamma': _L1_ffn_in['si_gamma'], 'L1_ffn_si_beta': _L1_ffn_in['si_beta'], 'L1_ffn_si_lin_w': _L1_ffn_in['si_lin_w'], 'L1_ffn_si_lin_b': _L1_ffn_in['si_lin_b']}

def reference(x, L0_tok_conv_w, L0_tok_conv_b, L0_tok_read, L0_attn_W_Q, L0_attn_b_Q, L0_attn_W_K, L0_attn_b_K, L0_attn_W_V, L0_attn_b_V, L0_attn_W_O, L0_attn_b_O, L0_ffn_W1, L0_ffn_b1, L0_ffn_W2, L0_ffn_b2, L0_ffn_Wr, L0_ffn_br, L1_attn_Wq, L1_attn_Wk, L1_attn_Wv, L1_attn_Wo, L1_ffn_weight, L1_ffn_bias, L1_ffn_so_conv_w, L1_ffn_so_conv_b, L1_ffn_so_gamma, L1_ffn_so_beta, L1_ffn_so_lin_w, L1_ffn_so_lin_b, L1_ffn_si_conv_w, L1_ffn_si_conv_b, L1_ffn_si_gamma, L1_ffn_si_beta, L1_ffn_si_lin_w, L1_ffn_si_lin_b):
    import jax
    import jax.numpy as jnp

    def _L0_tok_ref(x, conv_w, conv_b, read):
        import jax, jax.numpy as jnp
        import numpy as np
        B, T, D, DV = (4, 1024, 256, 4)
        K = 4
        C = D * DV
        Bb, Tt, d, dv = x.shape
        c = d * dv
        x_flat = x.reshape(Bb, Tt, c)
        k = conv_w.shape[1]
        x_pad = jnp.pad(x_flat, ((0, 0), (k - 1, 0), (0, 0)))
        acc = conv_b
        for j in range(k):
            acc = acc + x_pad[:, j:j + Tt, :] * conv_w[:, j]
        x_conv = acc.reshape(Bb, Tt, d, dv)
        return jnp.einsum('btdv,v->btd', x_conv, read)

    def _L0_attn_ref(x, W_Q, b_Q, W_K, b_K, W_V, b_V, W_O, b_O):
        import jax, jax.numpy as jnp
        import numpy as np
        D_MODEL = 256
        N_HEADS = 16
        D_HEAD = 64
        ROTARY_DIM = 64
        ROTARY_BASE = 10000.0
        ATTN_SCALE = 8.0

        def _rope_sin_cos(n_pos, rotary_dim):
            pos = jnp.arange(n_pos, dtype=jnp.float32)
            dim = jnp.arange(rotary_dim // 2, dtype=jnp.float32)
            freq = ROTARY_BASE ** (dim / (rotary_dim / 2))
            freq = jnp.concatenate([freq, freq])
            angles = pos[:, None] / freq[None, :]
            return (jnp.sin(angles), jnp.cos(angles))

        def _apply_rotary(x, sin, cos):
            n = x.shape[-1] // 2
            x_flip = jnp.concatenate([-x[..., n:], x[..., :n]], axis=-1)
            return x * cos[None, :, None, :] + x_flip * sin[None, :, None, :]
        B, S, _ = x.shape
        q = jnp.einsum('bsd,hdk->bshk', x, W_Q) + b_Q
        k = jnp.einsum('bsd,hdk->bshk', x, W_K) + b_K
        v = jnp.einsum('bsd,hdk->bshk', x, W_V) + b_V
        sin, cos = _rope_sin_cos(S, ROTARY_DIM)
        q = _apply_rotary(q, sin, cos)
        k = _apply_rotary(k, sin, cos)
        scores = jnp.einsum('bqhd,bkhd->bhqk', q, k) / ATTN_SCALE
        causal = jnp.tril(jnp.ones((S, S), dtype=bool))
        scores = jnp.where(causal[None, None], scores, -jnp.inf)
        pattern = jax.nn.softmax(scores, axis=-1)
        pattern = jnp.where(jnp.isnan(pattern), jnp.zeros_like(pattern), pattern)
        z = jnp.einsum('bhqk,bkhd->bqhd', pattern, v)
        out = jnp.einsum('bqhd,hdm->bqm', z, W_O) + b_O
        return out

    def _L0_ffn_ref(x, W1, b1, W2, b2, Wr, br):
        import jax, jax.numpy as jnp
        import numpy as np
        B, S, D, F, E = (4, 512, 256, 1024, 8)
        b, s, d = x.shape
        e = Wr.shape[1]
        logits = x @ Wr + br
        idx = jnp.argmax(logits, axis=-1)
        probs = jax.nn.softmax(logits, axis=-1)
        gates = jnp.take_along_axis(probs, idx[..., None], axis=-1)[..., 0]
        xf = x.reshape(-1, d)
        idxf = idx.reshape(-1)
        gf = gates.reshape(-1)
        out = jnp.zeros_like(xf)
        for ei in range(e):
            h = jax.nn.gelu(xf @ W1[ei] + b1[ei], approximate=False)
            y = h @ W2[ei] + b2[ei]
            mask = (idxf == ei).astype(xf.dtype)
            out = out + y * (gf * mask)[:, None]
        return out.reshape(b, s, d)

    def _L1_attn_ref(x, Wq, Wk, Wv, Wo):
        import jax, jax.numpy as jnp
        import numpy as np
        EPS = 1e-08

        def elu_feature_map(x):
            return jax.nn.elu(x) + 1.0
        B, S, D = x.shape
        H = 16
        Dh = D // H

        def proj(W):
            return (x @ W.T).reshape(B, S, H, Dh)
        q = elu_feature_map(proj(Wq))
        k = elu_feature_map(proj(Wk))
        v = proj(Wv)
        q_t = jnp.moveaxis(q, 1, 0)
        k_t = jnp.moveaxis(k, 1, 0)
        v_t = jnp.moveaxis(v, 1, 0)

        def step(carry, qkv):
            kv_sum, k_sum = carry
            q_i, k_i, v_i = qkv
            kv_sum = kv_sum + jnp.einsum('bhd,bhe->bhde', k_i, v_i)
            k_sum = k_sum + k_i
            num = jnp.einsum('bhd,bhde->bhe', q_i, kv_sum)
            den = jnp.sum(q_i * k_sum, axis=-1, keepdims=True)
            out_i = num / (den + EPS)
            return ((kv_sum, k_sum), out_i)
        kv0 = jnp.zeros((B, H, Dh, Dh), dtype=x.dtype)
        ks0 = jnp.zeros((B, H, Dh), dtype=x.dtype)
        _, out = jax.lax.scan(step, (kv0, ks0), (q_t, k_t, v_t))
        out = jnp.moveaxis(out, 0, 1).reshape(B, S, D)
        return out @ Wo.T

    def _L1_ffn_ref(x, weight, bias, so_conv_w, so_conv_b, so_gamma, so_beta, so_lin_w, so_lin_b, si_conv_w, si_conv_b, si_gamma, si_beta, si_lin_w, si_lin_b):
        import jax, jax.numpy as jnp
        import numpy as np
        B, L, C1, C2, K, K_IN = (4, 256, 256, 256, 32, 32)
        BN_EPS = 1e-05

        def _gated_bottleneck(x2d, conv_w, conv_b, gamma, beta, lin_w, lin_b):
            n = x2d.shape[0]
            g = conv_w.shape[0]
            xc = jnp.einsum('ngf,gf->ng', x2d.reshape(n, g, 4), conv_w) + conv_b
            mean = jnp.mean(xc, axis=0)
            var = jnp.mean((xc - mean) ** 2, axis=0)
            xn = (xc - mean) * jax.lax.rsqrt(var + BN_EPS) * gamma + beta
            xa = jax.nn.gelu(xn, approximate=False)
            return xa @ lin_w.T + lin_b
        b, l, c1 = x.shape
        c2 = weight.shape[1]
        x2d = x.reshape(b * l, c1)
        bi = jnp.arange(b)[:, None, None]
        li = jnp.arange(l)[None, :, None]
        score_out = jax.nn.softmax(_gated_bottleneck(x2d, so_conv_w, so_conv_b, so_gamma, so_beta, so_lin_w, so_lin_b).reshape(b, l, c2), axis=-1)
        s_v_out, s_i_out = jax.lax.top_k(score_out, K)
        full = jnp.einsum('blc,co->blo', x, weight)
        out_k = jnp.take_along_axis(full, s_i_out, axis=-1) * s_v_out
        out_branch = jnp.zeros((b, l, c2), x.dtype).at[bi, li, s_i_out].add(out_k)
        score_in = jax.nn.softmax(_gated_bottleneck(x2d, si_conv_w, si_conv_b, si_gamma, si_beta, si_lin_w, si_lin_b).reshape(b, l, c1), axis=-1)
        s_v_in, s_i_in = jax.lax.top_k(score_in, K_IN)
        x_gated = jnp.take_along_axis(x, s_i_in, axis=-1) * s_v_in
        x_sparse = jnp.zeros((b, l, c1), x.dtype).at[bi, li, s_i_in].add(x_gated)
        in_branch = jnp.einsum('blc,co->blo', x_sparse, weight)
        return out_branch + in_branch + bias
    h = _L0_tok_ref(x, L0_tok_conv_w, L0_tok_conv_b, L0_tok_read)
    h = h + _L0_attn_ref(_layernorm(h, axis=-1), L0_attn_W_Q, L0_attn_b_Q, L0_attn_W_K, L0_attn_b_K, L0_attn_W_V, L0_attn_b_V, L0_attn_W_O, L0_attn_b_O)
    h = h + _L0_ffn_ref(_layernorm(h, axis=-1), L0_ffn_W1, L0_ffn_b1, L0_ffn_W2, L0_ffn_b2, L0_ffn_Wr, L0_ffn_br)
    h = h + _L1_attn_ref(_layernorm(h, axis=-1), L1_attn_Wq, L1_attn_Wk, L1_attn_Wv, L1_attn_Wo)
    h = h + _L1_ffn_ref(_layernorm(h, axis=-1), L1_ffn_weight, L1_ffn_bias, L1_ffn_so_conv_w, L1_ffn_so_conv_b, L1_ffn_so_gamma, L1_ffn_so_beta, L1_ffn_so_lin_w, L1_ffn_so_lin_b, L1_ffn_si_conv_w, L1_ffn_si_conv_b, L1_ffn_si_gamma, L1_ffn_si_beta, L1_ffn_si_lin_w, L1_ffn_si_lin_b)
    return h

_drawn_inputs = setup_inputs


def setup_inputs(seed=0):
    import zlib

    import numpy as np

    out = dict(_drawn_inputs(seed))
    spreads = {'L0_tok_read': (0.25, 0.2),
     'L0_attn_b_Q': (0.0, 0.8),
     'L0_attn_b_K': (0.0, 0.8),
     'L0_attn_b_V': (0.0, 0.1),
     'L0_attn_b_O': (0.0, 0.1),
     'L1_ffn_bias': (0.0, 0.1),
     'L1_ffn_so_conv_b': (0.0, 0.8),
     'L1_ffn_so_gamma': (1.0, 0.6),
     'L1_ffn_so_beta': (0.0, 0.8),
     'L1_ffn_so_lin_b': (0.0, 0.8),
     'L1_ffn_si_conv_b': (0.0, 0.8),
     'L1_ffn_si_gamma': (1.0, 0.6),
     'L1_ffn_si_beta': (0.0, 0.8),
     'L1_ffn_si_lin_b': (0.0, 0.8)}
    factors = {'L0_attn_W_Q': 8.0,
     'L0_attn_W_K': 8.0,
     'L0_ffn_b1': 7.913,
     'L0_ffn_b2': 5.425,
     'L1_attn_Wq': 3.147,
     'L1_ffn_weight': 4.123,
     'L1_ffn_so_conv_w': 6.887,
     'L1_ffn_so_lin_w': 6.411,
     'L1_ffn_si_conv_w': 6.826,
     'L1_ffn_si_lin_w': 6.467}
    for name, (base, spread) in spreads.items():
        noise = np.random.default_rng([zlib.crc32(name.encode()), seed]).standard_normal(out[name].shape)
        drawn = base * np.exp(spread * noise) if base else spread * noise
        out[name] = jnp.asarray(drawn.astype(out[name].dtype))
    for name, factor in factors.items():
        out[name] = (out[name] * factor).astype(out[name].dtype)
    return out
```

```python
import concourse.bass as bass
from concourse import mybir
from contextlib import ExitStack
import numpy as np

STAGE = 4

B, T, D, DV, TAPS = 2, 1024, 256, 4, 4
C = D * DV
N = B * T
TILES = N // 128
KC = D // 128
HEADS, DH = 16, 64
PAIRS = HEADS // 2
SCALE = 8.0
NEG = -1.0e30
EPS = 1e-5
EXPERTS, FF = 8, 1024
SLOT_TILES = TILES + EXPERTS - 1
LHEADS, LDH = 16, 16
GROUPS = D // 4
TOPK = 32


def shape_constants():
    p = np.arange(128)
    parts = {}
    parts["ident"] = np.eye(128)
    parts["causal_add"] = np.where(p[None, :] <= p[:, None], 0.0, NEG)
    parts["causal_mul"] = (p[:, None] <= p[None, :]).astype(float)
    parts["before"] = (p[:, None] < p[None, :]).astype(float)
    parts["ones"] = np.ones((128, 128))
    tile_of, expert = np.arange(128) // 8, np.arange(128) % 8
    parts["expert"] = np.broadcast_to(expert, (128, 128))
    parts["expert_plus"] = np.broadcast_to(expert + EXPERTS, (128, 128))
    parts["k128"] = np.broadcast_to(128 * (np.arange(128) % 16), (128, 128))
    parts["slot_tile"] = np.broadcast_to(np.arange(SLOT_TILES * EXPERTS) // EXPERTS, (128, SLOT_TILES * EXPERTS))
    parts["own_head"] = (p[:, None] // 16 == np.arange(136)[None, :] // 17).astype(float)
    parts["odd_head"] = (p[:, None] // 16 % 2 == np.arange(2)[None, :]).astype(float)
    parts["group4"] = (p[:, None] // 4 == np.arange(32)[None, :]).astype(float)
    arrays, where, at = [], {}, 0
    for name, a in parts.items():
        where[name] = (at, at + a.shape[1])
        at += a.shape[1]
        arrays.append(a)
    s = p % 64
    dim = (s % 32) // 16 * 32 + s // 32 * 16 + s % 16
    f = np.arange(32, dtype=np.float32)
    freq = (np.float32(10000.0) ** (f / np.float32(32))).astype(np.float32)
    angles = (np.arange(T, dtype=np.float32)[None, :] / freq[dim % 32][:, None]).astype(np.float32)
    sign = np.where(dim < 32, -1.0, 1.0)[:, None]
    rope = np.concatenate([np.cos(angles), sign * np.sin(angles)], axis=1)
    return (np.concatenate(arrays, axis=1).astype(np.float32), where, rope.astype(np.float32))


def build(nc, ins, where, out):
    f32, f16, bf16 = mybir.dt.float32, mybir.dt.float16, mybir.dt.bfloat16
    ALU, ACT, AX = mybir.AluOpType, mybir.ActivationFunctionType, mybir.AxisListType
    ctx = ExitStack()
    with ctx:
        def sem(name):
            return ctx.enter_context(nc.semaphore(name))

        def psum(name, cols):
            return ctx.enter_context(nc.psum_tensor(name, [128, cols], f32))

        banks = psum("banks", 8 * 512)

        def bank(b, n=1):
            return banks[:, b * 512:(b + n) * 512]

        def sb(name, shape, dt=f32, stack=ctx):
            return stack.enter_context(nc.sbuf_tensor(name, shape, dt))

        nconst = ins["consts"].shape[1]
        cst = sb("cst", [128, nconst])

        def const(name):
            a, b = where[name]
            return cst[:, a:b]

        H = sb("H", [128, TILES, D])
        mask16 = sb("mask16", [128, 128], bf16)
        ident16 = sb("ident16", [128, 128], bf16)
        eps = sb("eps", [128, 1])
        stats = sb("stats", [128, TILES, 6])
        mv = sb("mv", [128, TILES, 2])
        std = sb("std", [128, TILES])
        rstd = sb("rstd", [128, TILES])
        xn = sb("xn", [128, 2, D])
        XN = sb("XN", [128, TILES, D])
        xnT = sb("xnT", [128, KC, N])

        with ExitStack() as st:
            x_in = sb("x_in", [128, 2, C], stack=st)
            x_hi = sb("x_hi", [128, 2, 8, 131], f16, st)
            x_lo = sb("x_lo", [128, 2, 8, 131], f16, st)
            conv_w = sb("conv_w", [128, 8, TAPS], stack=st)
            conv_b = sb("conv_b", [128, 8], stack=st)
            read = sb("read", [128, 1], stack=st)
            taps32 = sb("taps32", [128, 8, TAPS, 32], stack=st)
            taps_hi = sb("taps_hi", [128, 8, TAPS, 32], f16, st)
            taps_lo = sb("taps_lo", [128, 8, TAPS, 32], f16, st)
            bias32 = sb("bias32", [128, 8, 32], stack=st)
            conv_bias = sb("conv_bias", [128, D], stack=st)
        with ExitStack() as st:
            rope = sb("rope", [128, 2, T], stack=st)
            w_in = sb("w_in", [128, 2, KC, 128], stack=st)
            w_qk = sb("w_qk", [128, 2, KC, 128], stack=st)
            w_v = sb("w_v", [128, KC, 128], stack=st)
            w_o = sb("w_o", [128, D], stack=st)
            b_in = sb("b_in", [128, 2, PAIRS], stack=st)
            b_v = sb("b_v", [128, PAIRS], stack=st)
            b_o = sb("b_o", [128, D], stack=st)
            qf = sb("qf", [128, 2, 512], stack=st)
            q_swap = sb("q_swap", [128, 512], stack=st)
            q_sin = sb("q_sin", [128, 512], stack=st)
            q_cos = sb("q_cos", [128, 2, 512], stack=st)
            q_rot = sb("q_rot", [128, 2, 512], stack=st)
            hi = sb("hi", [128, 2, N], f16, st)
            lo_q = sb("lo_q", [128, N], f16, st)
            lo_k = sb("lo_k", [128, 2, N], f16, st)
            Q2 = sb("Q2", [128, 2, 2, N], f16, st)
            K2 = sb("K2", [128, 2, 2, N], f16, st)
            V = sb("V", [128, 2, TILES, 128], stack=st)
            neg_max = sb("neg_max", [128, 4], stack=st)
            row_sum = sb("row_sum", [128, 4], stack=st)
            inv_sum = sb("inv_sum", [128, 4], stack=st)
            P = sb("P", [128, 2, T], stack=st)
            PT = sb("PT", [128, 4, 512], stack=st)
            z = sb("z", [128, 2, 128], stack=st)
            zT = sb("zT", [128, N], stack=st)

        with ExitStack() as st:
            W1 = sb("W1", [128, EXPERTS, KC, FF], stack=st)
            W2 = sb("W2", [128, EXPERTS, FF // 128, D], stack=st)
            w_r = sb("w_r", [128, KC, EXPERTS], stack=st)
            b_r = sb("b_r", [128, EXPERTS], stack=st)
            b_1 = sb("b_1", [128, EXPERTS * 8], stack=st)
            b_2 = sb("b_2", [1, EXPERTS * D], stack=st)
            logit = sb("logit", [128, TILES, EXPERTS], stack=st)
            top = sb("top", [128, TILES], stack=st)
            pick = sb("pick", [128, TILES, EXPERTS], stack=st)
            cand = sb("cand", [128, TILES, EXPERTS], stack=st)
            gate = sb("gate", [128, TILES], stack=st)
            scan = sb("scan", [128, 2, TILES, EXPERTS], stack=st)
            tot = sb("tot", [128, TILES, EXPERTS], stack=st)
            more = sb("more", [128, EXPERTS, TILES], stack=st)
            ntile = sb("ntile", [128, EXPERTS], stack=st)
            cum = sb("cum", [128, 2, EXPERTS], stack=st)
            start = sb("start", [128, EXPERTS], stack=st)
            past = sb("past", [128, SLOT_TILES, EXPERTS], stack=st)
            posf = sb("posf", [128, TILES], stack=st)
            pos = sb("pos", [128, TILES], mybir.dt.uint32, st)
            expf = sb("expf", [128, SLOT_TILES], stack=st)
            expi = sb("expi", [128, SLOT_TILES], mybir.dt.int32, st)
            xs = sb("xs", [128, 2, D], stack=st)
            xsT = sb("xsT", [128, 2, KC, 128], stack=st)
            hid = xnT[:, 0, 0:FF]
            gelT = xnT[:, 1, 0:FF].rearrange("p (f t) -> p f t", f=8)
            ys = sb("ys", [128, 2, D], stack=st)
        with ExitStack() as st:
            wl_in = sb("wl_in", [128, 4, 2, D], stack=st)
            wlT = sb("wlT", [128, KC, 4, D], stack=st)
            xT = sb("xT", [128, 2, KC, 128], stack=st)
            eT = sb("eT", [128, 512], stack=st)
            ek = sb("ek", [128, D], stack=st)
            qkT = sb("qkT", [128, 2, 4, 128], stack=st)
            kz = sb("kz", [128, 2, 2, KC, 128], stack=st)
            ktok = sb("ktok", [128, 2, D], stack=st)
            vaug = sb("vaug", [128, 2, LHEADS, 17], stack=st)
            AT = sb("AT", [128, LHEADS, 128], stack=st)
            state = sb("state", [128, B, 272], stack=st)
            sdel = sb("sdel", [128, 272], stack=st)
            den = sb("den", [128, LHEADS], stack=st)
            o = sb("o", [128, D], stack=st)
            oT = sb("oT", [128, KC, 128], stack=st)
        with ExitStack() as st:
            wg = sb("wg", [128, KC, D], stack=st)
            cwc = sb("cwc", [128, 2, KC], stack=st)
            gcols = sb("gcols", [128, 3], stack=st)
            lin_in = sb("lin_in", [128, 2, 128], stack=st)
            linT = sb("linT", [128, 2, D], stack=st)
            lin_b = sb("lin_b", [128, 2, D], stack=st)
            bias_g = sb("bias_g", [128, D], stack=st)
            CW = sb("CW", [128, KC, 128], stack=st)
            xc = sb("xc", [128, N], stack=st)
            xa = sb("xa", [128, N], stack=st)
            bst = sb("bst", [128, 4, 6], stack=st)
            bmv = sb("bmv", [128, 2], stack=st)
            bstd = sb("bstd", [128, 1], stack=st)
            bsc = sb("bsc", [128, 3], stack=st)
            xat = sb("xat", [128, 2, 128], stack=st)
            xgt = sb("xgt", [128, 2, KC, 128], stack=st)
            L = sb("L", [128, 2, 2, D], stack=st)
            Lr = sb("Lr", [128, 2, 2, D], stack=st)
            m8 = sb("m8", [128, 2, 2, 4, 8], stack=st)
            nmx = sb("nmx", [128, 2, 2], stack=st)
            ef = sb("ef", [128, 2, 2, D], stack=st)
            er = sb("er", [128, 2, 2, D], stack=st)
            esum = sb("esum", [128, 2, 2], stack=st)
            einv = sb("einv", [128, 2, 2], stack=st)
            ob = sb("ob", [128, 2, D], stack=st)
            xg = sb("xg", [128, 2, D], stack=st)
            xgT = sb("xgT", [128, 2, KC, 128], stack=st)
        sorted_x = nc.dram_tensor("sorted_x", (SLOT_TILES * 128, D), f32, kind="Internal").ap()
        sorted_y = nc.dram_tensor("sorted_y", (SLOT_TILES * 128, D), f32, kind="Internal").ap()

        s_passed = {e.engine: sem("s_passed_" + n) for n, e in
                    (("sp", nc.sync), ("act", nc.scalar), ("dve", nc.vector), ("pe", nc.tensor), ("pool", nc.gpsimd))}
        s_cst = sem("s_cst")
        s_x = [sem("s_x0"), sem("s_x1")]
        s_small = sem("s_small")
        s_taps = sem("s_taps")
        s_cbias = sem("s_cbias")
        s_cb = sem("s_cb")
        s_m16 = sem("s_m16")
        s_xT = sem("s_xT")
        s_xhi = sem("s_xhi")
        s_xlo = sem("s_xlo")
        s_conv = sem("s_conv")
        s_h0 = sem("s_h0")
        s_var = sem("s_var")
        s_std = sem("s_std")
        s_xn = sem("s_xn")
        s_xnt = sem("s_xnt")
        s_xnT = sem("s_xnT")
        s_rope = sem("s_rope")
        s_wqk_in = sem("s_wqk_in")
        s_wv = sem("s_wv")
        s_wo = sem("s_wo")
        s_bias = sem("s_bias")
        s_bq = sem("s_bq")
        s_perm = sem("s_perm")
        s_qk = sem("s_qk")
        s_vp = sem("s_vp")
        s_qf = sem("s_qf")
        s_vev = sem("s_vev")
        s_cos = sem("s_cos")
        s_rot = sem("s_rot")
        s_hi = sem("s_hi")
        s_lo = sem("s_lo")
        s_dup = [sem("s_dup0"), sem("s_dup1")]
        s_S = sem("s_S")
        s_mx = sem("s_mx")
        s_P = sem("s_P")
        s_T = sem("s_T")
        s_evD = sem("s_evD")
        s_evA = sem("s_evA")
        s_PV = sem("s_PV")
        s_zn = sem("s_zn")
        s_zt = sem("s_zt")
        s_zT = sem("s_zT")
        s_WO = sem("s_WO")
        s_h1 = sem("s_h1")
        s_out = sem("s_out")
        s_z0 = sem("s_z0"); s_zd = sem("s_zd"); s_w1 = sem("s_w1"); s_w2 = sem("s_w2"); s_rw = sem("s_rw")
        s_lg = sem("s_lg"); s_lgd = sem("s_lgd"); s_lge = sem("s_lge"); s_oh = sem("s_oh"); s_rk = sem("s_rk")
        s_pos = sem("s_pos"); s_sc = sem("s_sc"); s_xs = [sem("s_xs0"), sem("s_xs1")]; s_xst = sem("s_xst")
        s_xsT = sem("s_xsT"); s_hid = sem("s_hid"); s_he = sem("s_he"); s_ht = sem("s_ht"); s_gel = sem("s_gel")
        s_y = sem("s_y"); s_ye = sem("s_ye"); s_ys = [sem("s_ys0"), sem("s_ys1")]; s_g = sem("s_g"); s_h2 = sem("s_h2")
        l_w = sem("l_w"); l_wt = sem("l_wt"); l_wT = sem("l_wT"); l_xt = sem("l_xt"); l_xT = sem("l_xT"); l_xn = sem("l_xn")
        l_A = sem("l_A"); l_Bk = sem("l_Bk"); l_eA = sem("l_eA"); l_eB = sem("l_eB"); l_mA = sem("l_mA"); l_mB = sem("l_mB")
        l_fA = sem("l_fA"); l_fB = sem("l_fB"); l_kz = sem("l_kz"); l_v = sem("l_v"); l_at = sem("l_at"); l_AT = sem("l_AT")
        l_num = sem("l_num"); l_st = sem("l_st"); l_sd = sem("l_sd"); l_o = sem("l_o"); l_ot = sem("l_ot"); l_oT = sem("l_oT")
        l_y = sem("l_y"); l_h3 = sem("l_h3"); l_ini = sem("l_ini")
        g_w = sem("g_w"); g_cw = sem("g_cw"); g_lt = sem("g_lt"); g_lT = sem("g_lT"); g_xc = sem("g_xc"); g_xce = sem("g_xce")
        g_bv = sem("g_bv"); g_bs = sem("g_bs"); g_sc = sem("g_sc"); g_xa = sem("g_xa"); g_cp = sem("g_cp"); g_lg = sem("g_lg")
        g_L = sem("g_L"); g_tk = [sem("g_tk0"), sem("g_tk1")]; g_nm = sem("g_nm"); g_e = sem("g_e"); g_d = sem("g_d"); g_fu = sem("g_fu"); g_ob = sem("g_ob")
        g_xg = sem("g_xg"); g_xt = sem("g_xt"); g_xT = sem("g_xT"); g_in = sem("g_in"); g_h = sem("g_h")

        x_rows = ins["x"].rearrange("b (i p) d v -> b i p (d v)", p=128)
        out_rows = out.rearrange("b (i p) d -> p (b i) d", p=128)
        wq_d = ins["L0_attn_W_Q"].rearrange("(a h) (c p) k -> a p c h k", h=2, p=128)
        wk_d = ins["L0_attn_W_K"].rearrange("(a h) (c p) k -> a p c h k", h=2, p=128)
        wv_d = ins["L0_attn_W_V"].rearrange("(a h) (c p) k -> a p c h k", h=2, p=128)
        wo_d = ins["L0_attn_W_O"].rearrange("(a h) k m -> a (h k) m", h=2)

        STEPS = [(b, qt, h) for b in range(B) for qt in range(8) for h in range(2)]
        PARTS = []
        for g, (b, qt, h) in enumerate(STEPS):
            PARTS.append([(len(sum(PARTS, [])) + j, a, min(a + 4, qt + 1))
                          for j, a in enumerate(range(0, qt + 1, 4))])
        NP = len(sum(PARTS, []))
        NS = len(STEPS)
        FIRST_PROJ, NQK, NV = 1, 8, 4

        def over_pairs(eng, body):
            with eng.Fori(0, PAIRS // 2 - 1) as j:
                for par in range(2):
                    body(2 * j + par, par, False)
            body(PAIRS - 2, 0, False)
            body(PAIRS - 1, 1, True)

        def lin_tile(n, u):
            return (n // 2 if isinstance(n, int) else (n - u) // 2) + 8 * u

        def lin_loop(eng, front, back):
            f = front or (lambda n, u: None)
            k = back or (lambda n, u, i: None)
            f(0, 0)
            with eng.Fori(0, TILES // 2 - 1) as i:
                f(2 * i + 1, 1)
                k(2 * i, 0, i)
                f(2 * i + 2, 0)
                k(2 * i + 1, 1, i)
            f(TILES - 1, 1)
            k(TILES - 2, 0, TILES // 2 - 1)
            k(TILES - 1, 1, TILES // 2 - 1)

        def alone(eng):
            eng.sem_inc(s_passed[eng.engine], 1)

        block = ctx.enter_context(nc.Block())

        @block.sync
        def _(sp):
            sp.dma_start(cst[:], ins["consts"]).then_inc(s_cst, 16)
            sp.dma_start(conv_w[:], ins["L0_tok_conv_w"].rearrange("(c p) j -> p c j", p=128)).then_inc(s_small, 16)
            with nc.allow_non_contiguous_dma(reason="small vectors onto partitions"):
                sp.dma_start(conv_b[:], ins["L0_tok_conv_b"].rearrange("(c p) -> p c", p=128)).then_inc(s_small, 16)
                rd = ins["L0_tok_read"]
                sp.dma_start(read[:], bass.AP(rd.tensor, 0, [[0, 32], [1, 4], [1, 1]])).then_inc(s_small, 16)
            with sp.Fori(0, T // 128) as i:
                for u in range(B):
                    sp.wait_ge(s_xT, 2 * i + u + 1)
                    alone(sp)
                    sp.dma_start(x_in[:, u, :], x_rows[u, i, :, :]).then_inc(s_x[u], 16)
            if STAGE >= 1:
                sp.wait_ge(s_h0, TILES)
                sp.dma_start(rope[:], ins["rope"].rearrange("p (s t) -> p s t", s=2)).then_inc(s_rope, 16)
                with nc.allow_non_contiguous_dma(reason="small vectors onto partitions"):
                    for j, name in enumerate(("L0_attn_b_Q", "L0_attn_b_K")):
                        v = ins[name].rearrange("(a h) (f q r) -> h q f r a", h=2, f=2, q=2)
                        for h in range(2):
                            for q in range(2):
                                for f in range(2):
                                    p0 = h * 64 + q * 32 + f * 16
                                    sp.dma_start(b_in[p0:p0 + 16, j, :], v[h, q, f]).then_inc(s_bias, 16)
                    sp.dma_start(b_v[:], ins["L0_attn_b_V"].rearrange("(a h) k -> (h k) a", h=2)).then_inc(s_bias, 16)
                    bo = ins["L0_attn_b_O"]
                    sp.dma_start(b_o[:], bass.AP(bo.tensor, 0, [[0, 128], [1, D]])).then_inc(s_bias, 16)

                def load_proj(hp):
                    sp.wait_ge(s_perm, hp + 1)
                    alone(sp)
                    for h in range(2):
                        sp.dma_start(w_in[:, 0, :, h * 64:(h + 1) * 64], wq_d[hp, :, :, h, :]).then_inc(s_wqk_in, 16)
                        sp.dma_start(w_in[:, 1, :, h * 64:(h + 1) * 64], wk_d[hp, :, :, h, :]).then_inc(s_wqk_in, 16)
                    sp.wait_ge(s_vp, NV * hp + 1)
                    alone(sp)
                    for h in range(2):
                        sp.dma_start(w_v[:, :, h * 64:(h + 1) * 64], wv_d[hp, :, :, h, :]).then_inc(s_wv, 16)

                def spread(hp, par):
                    sp.wait_ge(s_hi, NQK * hp + NQK)
                    alone(sp)
                    sp.wait_ge(s_lo, NQK * hp + NQK + 1)
                    alone(sp)
                    for h in range(2):
                        own, other = slice(64 * h, 64 * h + 64), slice(64 - 64 * h, 128 - 64 * h)
                        sp.dma_start(Q2[own, par, h, :], hi[own, 0, :]).then_inc(s_dup[par], 16)
                        sp.dma_start(Q2[other, par, h, :], lo_q[own, :]).then_inc(s_dup[par], 16)
                        sp.dma_start(K2[own, par, h, :], hi[own, 1, :]).then_inc(s_dup[par], 16)
                        sp.dma_start(K2[other, par, h, :], hi[own, 1, :]).then_inc(s_dup[par], 16)

                load_proj(0)
                spread(0, 0)

                def pair(hp, par, last):
                    sp.wait_ge(s_WO, NV * 2 * hp + 1)
                    alone(sp)
                    sp.dma_start(w_o[:], wo_d[hp, :, :]).then_inc(s_wo, 16)
                    if not last:
                        load_proj(hp + 1)
                        sp.wait_ge(s_S, NS * hp + 1)
                        alone(sp)
                        spread(hp + 1, 1 - par)

                over_pairs(sp, pair)
                sp.wait_ge(s_h1, 8 * PAIRS + 1)
            if STAGE >= 2:
                with nc.allow_non_contiguous_dma(reason="small vectors onto partitions"):
                    sp.dma_start(w_r[:], ins["L0_ffn_Wr"].rearrange("(c p) e -> p c e", p=128)).then_inc(s_rw, 16)
                    br = ins["L0_ffn_br"]
                    sp.dma_start(b_r[:], bass.AP(br.tensor, 0, [[0, 128], [1, EXPERTS]])).then_inc(s_rw, 16)
                    sp.dma_start(b_1[:].rearrange("p (e f) -> p e f", e=EXPERTS), ins["L0_ffn_b1"].rearrange("e (f p) -> p e f", p=128)).then_inc(s_rw, 16)
                sp.dma_start(b_2[:], ins["L0_ffn_b2"].rearrange("(a e) d -> a (e d)", a=1)).then_inc(s_rw, 16)
                for e in range(EXPERTS):
                    sp.dma_start(W1[:, e, :, :], ins["L0_ffn_W1"][e].rearrange("(c p) f -> p c f", p=128)).then_inc(s_w1, 16)
                for e in range(EXPERTS):
                    sp.dma_start(W2[:, e, :, :], ins["L0_ffn_W2"][e].rearrange("(c p) f -> p c f", p=128)).then_inc(s_w2, 16)
                sp.wait_ge(s_sc, 16 * TILES)

                def load_slots(s, u, k):
                    sp.wait_ge(s_xst, s + 1)
                    alone(sp)
                    sp.dma_start(xs[:, u, :], sorted_x[bass.ts(s, 128), :]).then_inc(s_xs[u], 16)

                def store_slots(s, u, k):
                    sp.wait_ge(s_ye, s + 1)
                    alone(sp)
                    sp.dma_start(sorted_y[bass.ts(s, 128), :], ys[:, u, :]).then_inc(s_ys[u], 16)

                load_slots(0, 0, 0)
                load_slots(1, 1, 0)
                with sp.Fori(0, SLOT_TILES // 2 - 1) as i:
                    for u in range(2):
                        store_slots(2 * i + u, u, 0)
                        load_slots(2 * i + u + 2, u, 0)
                store_slots(SLOT_TILES - 3, 0, 0)
                load_slots(SLOT_TILES - 1, 0, 0)
                store_slots(SLOT_TILES - 2, 1, 0)
                store_slots(SLOT_TILES - 1, 0, 0)
                sp.wait_ge(s_h2, TILES)
            if STAGE >= 3:
                for j, name in enumerate(("Wk", "Wv", "Wq", "Wo")):
                    sp.dma_start(wl_in[:, j, :, :], ins["L1_attn_" + name].rearrange("(c p) d -> p c d", p=128)).then_inc(l_w, 16)
                sp.wait_ge(l_h3, TILES + 1)
            if STAGE >= 4:
                sp.dma_start(wg[:], ins["L1_ffn_weight"].rearrange("(c p) d -> p c d", p=128)).then_inc(g_w, 16)
                with nc.allow_non_contiguous_dma(reason="small vectors onto partitions"):
                    for j, n in enumerate(("so", "si")):
                        sp.dma_start(cwc[:, j, :], ins[f"L1_ffn_{n}_conv_w"].rearrange("(c g) f -> (g f) c", c=KC)).then_inc(g_w, 16)
                        for m, v in enumerate(("conv_b", "gamma", "beta")):
                            sp.dma_start(gcols[64 * j:64 * j + 64, m:m + 1], ins[f"L1_ffn_{n}_{v}"].rearrange("(g a) -> g a", a=1)).then_inc(g_w, 16)
                        sp.dma_start(lin_in[:, :, 64 * j:64 * j + 64], ins[f"L1_ffn_{n}_lin_w"].rearrange("(c p) g -> p c g", p=128)).then_inc(g_w, 16)
                        lb = ins[f"L1_ffn_{n}_lin_b"]
                        sp.dma_start(lin_b[:, j, :], bass.AP(lb.tensor, 0, [[0, 128], [1, D]])).then_inc(g_w, 16)
                    bg = ins["L1_ffn_bias"]
                    sp.dma_start(bias_g[:], bass.AP(bg.tensor, 0, [[0, 128], [1, D]])).then_inc(g_w, 16)
                flat = out.rearrange("b (i p) d -> (b i) p d", p=128)
                with sp.Fori(0, TILES // 2) as i:
                    for u in range(2):
                        sp.wait_ge(g_h, 2 * i + u + 1)
                        alone(sp)
                        sp.dma_start(flat[bass.ds(2 * i + u, 1), :, :].rearrange("a p d -> p (a d)"), H[:, 2 * i + u, :]).then_inc(s_out, 16)
                sp.wait_ge(s_out, 16 * TILES)
                return
            if STAGE >= 1:
                pass
            else:
                sp.wait_ge(s_h0, TILES)
            sp.dma_start(out_rows, H[:]).then_inc(s_out, 16)
            sp.wait_ge(s_out, 16)

        @block.gpsimd
        def _(pool):
            pool.wait_ge(s_cst, 16)
            nc.gpsimd.memset(eps[:], EPS)
            nc.gpsimd.memset(x_hi[:, :, :, 0:3], 0.0)
            nc.gpsimd.memset(x_lo[:, :, :, 0:3], 0.0)
            nc.gpsimd.tensor_scalar(ident16[:], const("ident"), 1.0, 0.0, ALU.mult, ALU.add)
            nc.gpsimd.tensor_scalar(mask16[:], const("causal_add"), 1.0, 0.0, ALU.mult, ALU.add).then_inc(s_m16, 1)
            if STAGE < 1:
                return
            pool.wait_ge(s_rope, 16)
            pool.wait_ge(s_bias, 16 * 18)
            nc.gpsimd.tensor_scalar(b_in[:, 0, :], b_in[:, 0, :], 1.0 / SCALE, 0.0, ALU.mult, ALU.add).then_inc(s_bq, 1)

            def permute(hp):
                pool.wait_ge(s_wqk_in, 64 * hp + 64)
                pool.wait_ge(s_qk, NQK * hp + 1)
                alone(pool)
                for j, sc in enumerate((1.0 / SCALE, 1.0)):
                    src = w_in[:, j, :, :].rearrange("p c (h f q r) -> p (c h) f q r", h=2, f=2, q=2)
                    dst = w_qk[:, j, :, :].rearrange("p c (h q f r) -> p (c h) q f r", h=2, f=2, q=2)
                    for f in range(2):
                        last = nc.gpsimd.tensor_scalar(dst[:, :, :, f, :], src[:, :, f, :, :], sc, 0.0, ALU.mult, ALU.add)
                pool.drain()
                last.then_inc(s_perm, 1)

            def rotate(hp):
                for m in range(NQK + 1):
                    if m < NQK:
                        pool.wait_ge(s_qf, NQK * hp + m + 1)
                        if not isinstance(hp, int) or NQK * hp + m > 0:
                            pool.wait_ge(s_rot, NQK * hp + m)
                        nc.gpsimd.tensor_tensor(q_cos[:, m % 2, :], qf[:, m % 2, :],
                                                rope[:, 0, (m // 2) % 2 * 512:(m // 2) % 2 * 512 + 512],
                                                ALU.mult).then_inc(s_cos, 1)
                    if m >= 1:
                        k = m - 1
                        pool.wait_ge(s_rot, NQK * hp + k + 2)
                        alone(pool)
                        nc.gpsimd.tensor_scalar(hi[:, k % 2, k // 2 * 512:k // 2 * 512 + 512], q_rot[:, k % 2, :],
                                                1.0, 0.0, ALU.mult, ALU.add).then_inc(s_hi, 1)

            permute(0)
            rotate(0)

            def pair(hp, par, last):
                if not last:
                    permute(hp + 1)
                    pool.wait_ge(s_dup[par], 64 * (hp - par) + 128)
                    rotate(hp + 1)

            over_pairs(pool, pair)
            if STAGE < 2:
                return
            pool.wait_ge(s_h1, 8 * PAIRS + 1)
            nc.gpsimd.memset(xs[:, 0, :], 0.0).then_inc(s_z0, 1)
            pool.wait_ge(s_z0, 1)
            for s in range(SLOT_TILES):
                pool.dma_start(sorted_x[s * 128:(s + 1) * 128, :], xs[:, 0, :]).then_inc(s_zd, 16)
            pool.wait_ge(s_zd, 16 * SLOT_TILES)
            pool.wait_ge(s_pos, 1)
            for t in range(TILES):
                pool.indirect_dma_start(out=sorted_x, out_offset=bass.IndirectOffsetOnAxis(pos[:, t:t + 1], 0),
                                        in_=XN[:, t, :], in_offset=None).then_inc(s_sc, 16)
            pool.wait_ge(s_ys[0], 16 * ((SLOT_TILES + 1) // 2))
            pool.wait_ge(s_ys[1], 16 * (SLOT_TILES // 2))
            for t in range(TILES):
                pool.indirect_dma_start(out=XN[:, t, :], out_offset=None, in_=sorted_y,
                                        in_offset=bass.IndirectOffsetOnAxis(pos[:, t:t + 1], 0)).then_inc(s_g, 16)
            if STAGE < 3:
                return
            pool.wait_ge(s_h2, TILES)
            nc.gpsimd.memset(state[:], 0.0)
            nc.gpsimd.memset(vaug[:, :, :, 16:17], 1.0).then_inc(l_ini, 1)

            def lin_front(n, u):
                pool.wait_ge(l_eA, n + 1)
                alone(pool)
                nc.gpsimd.tensor_scalar(eT[:], eT[:], 1.0, 0.0, ALU.min, ALU.add).then_inc(l_mA, 1)
                pool.wait_ge(l_eB, n + 1)
                alone(pool)
                nc.gpsimd.tensor_scalar(ek[:], ek[:], 1.0, 0.0, ALU.min, ALU.add).then_inc(l_mB, 1)
                pool.wait_ge(l_fA, n + 1)
                alone(pool)
                for par in range(2):
                    last = nc.gpsimd.tensor_scalar(kz[:, u, par, :, :], qkT[:, u, 2:4, :], const("odd_head")[:, par:par + 1], 0.0,
                                                   ALU.mult, ALU.add)
                last.then_inc(l_kz, 1)

            lin_loop(pool, lin_front, None)
            if STAGE < 4:
                return
            pool.wait_ge(g_w, 16 * 14)
            nc.gpsimd.memset(CW[:], 0.0)
            nc.gpsimd.memset(linT[:], 0.0)
            pool.drain()
            for c in range(KC):
                for j in range(2):
                    last = nc.gpsimd.tensor_scalar(CW[:, c, 64 * j + 32 * c:64 * j + 32 * c + 32], const("group4"), cwc[:, j, c:c + 1], 0.0,
                                                   ALU.mult, ALU.add)
            last.then_inc(g_cw, 1)
            pool.wait_ge(g_xa, 1)
            with pool.Fori(0, TILES // 2) as i:
                for u in range(2):
                    n = 2 * i + u
                    pool.wait_ge(g_fu, n + 1)
                    alone(pool)
                    nc.gpsimd.tensor_copy(xat[:, u, :], xa[:, bass.ts(n, 128)])
                    nc.gpsimd.tensor_copy(xgt[:, u, :, :], xnT[:, :, bass.ts(n, 128)]).then_inc(g_cp, 1)
                    pool.wait_ge(g_e, n + 1)
                    nc.gpsimd.tensor_tensor(ef[:, u, :, :], ef[:, u, :, :], er[:, u, :, :], ALU.subtract).then_inc(g_d, 1)

        @block.scalar
        def _(act):
            def evac_hi(n, u):
                act.wait_ge(s_xT, n + 3)
                act.wait_ge(s_conv, n + 1)
                nc.scalar.activation(x_hi[:, u, :, 3:131], bank(2 * u, 2).rearrange("p (c t) -> p c t", c=8),
                                     ACT.Copy).then_inc(s_xhi, 1)

            act.sem_inc(s_xT, 2)
            act.sem_inc(s_xnT, 2)
            act.sem_inc(s_qk, 1)
            act.sem_inc(s_perm, 1)
            act.sem_inc(s_vp, 1)
            act.sem_inc(s_rot, 1)
            act.sem_inc(s_lo, 1)
            act.sem_inc(s_S, 1)
            act.sem_inc(s_WO, 1)
            act.sem_inc(s_evD, 1)
            act.sem_inc(s_evA, 1)
            act.sem_inc(s_T, 2)
            act.sem_inc(s_PV, 4)
            act.sem_inc(s_zn, 2)
            act.sem_inc(s_zt, 2)
            act.sem_inc(s_h1, 1)
            act.sem_inc(s_xst, 2)
            act.sem_inc(l_num, 2)
            act.sem_inc(l_at, 1)
            act.sem_inc(l_AT, 2)
            act.sem_inc(l_xt, 2)
            act.sem_inc(l_h3, 1)
            act.sem_inc(l_sd, 2)
            act.sem_inc(l_kz, 2)
            act.sem_inc(l_o, 1)
            act.sem_inc(l_ot, 1)
            act.sem_inc(l_y, 1)
            act.sem_inc(s_he, 1)
            act.sem_inc(s_ye, 0) if False else None
            act.sem_inc(g_fu, 1)
            act.sem_inc(g_in, 2)
            act.sem_inc(g_xt, 1)
            act.sem_inc(g_h, 0) if False else None
            act.sem_inc(s_conv, 2)
            act.wait_ge(s_m16, 1)
            act.drain()
            evac_hi(0, 0)
            def tok(i, u, last):
                act.wait_ge(s_conv, 2 * i + u + 3)
                if not (last):
                    nc.scalar.activation(x_hi[:, u, :, 0:3], x_hi[:, u, :, 128:131], ACT.Copy)
                    act.drain()
            with act.Fori(0, T // 128 - 1) as i:
                evac_hi(2 * i + 1, 1)
                tok(i, 0, False)
                evac_hi(2 * i + 2, 0)
                tok(i, 1, False)
            evac_hi(TILES - 1, 1)
            act.wait_ge(s_var, 1)
            nc.scalar.activation(std[:], mv[:, :, 1], ACT.Sqrt, bias=eps[:, 0:1]).then_inc(s_std, 1)
            if STAGE < 1:
                return

            def evac_tiles(k):
              with act.Fori(0, TILES // 2) as i:
                for u in range(2):
                    act.wait_ge(s_xnt, TILES * (k - 1) + 2 * i + u + 1)
                    alone(act)
                    nc.scalar.activation(xnT[:, :, bass.ts(2 * i + u, 128)],
                                         bank(u)[:, 0:256].rearrange("p (c t) -> p c t", c=KC), ACT.Copy).then_inc(s_xnT, 1)
            evac_tiles(1)
            act.wait_ge(s_bq, 1)

            def evac_qk(hp):
                for m in range(NQK):
                    act.wait_ge(s_qk, NQK * hp + m + 2)
                    if not isinstance(hp, int) or NQK * hp + m > 1:
                        act.wait_ge(s_rot, NQK * hp + m)
                        act.wait_ge(s_cos, NQK * hp + m - 1)
                    alone(act)
                    nc.scalar.activation(qf[:, m % 2, :], bank(m % 4), ACT.Identity,
                                         bias=b_in[:, m % 2, bass.ds(hp, 1)]).then_inc(s_qf, 1)

            def pair(hp, par, last):
                if not last:
                    evac_qk(hp + 1)

                def exps(g):
                    b, qt, h = STEPS[g]
                    w = (qt + 1) * 128
                    act.wait_ge(s_mx, NS * hp + g + 1)
                    act.wait_ge(s_T, NP * hp + (PARTS[g - 2][-1][0] + 1 if g >= 2 else 0) + 2)
                    act.wait_ge(s_zn, NS * hp + g + 2 - 2) if g>=2 else None
                    nc.scalar.activation(P[:, g % 2, 0:w], bank(2 * (g % 2), 2)[:, 0:w], ACT.Exp,
                                         bias=neg_max[:, g % 4:g % 4 + 1],
                                         accum_out=row_sum[:, g % 4:g % 4 + 1]).then_inc(s_P, 1)

                def evac_zT(k):
                    act.wait_ge(s_zt, 16 * hp + k + 3)
                    alone(act)
                    if k == 0:
                        act.wait_ge(s_WO, 8 * hp + 1)
                        alone(act)
                    nc.scalar.activation(zT[:, k * 128:(k + 1) * 128], bank(7)[:, 0:128], ACT.Identity,
                                         bias=b_v[:, bass.ds(hp, 1)]).then_inc(s_zT, 1)

                exps(0)
                for g in range(NS):
                    if g + 1 < NS:
                        exps(g + 1)
                    for f, a, e in PARTS[g]:
                        if f % 2 == 1:
                            act.wait_ge(s_T, NP * hp + f + 3)
                            act.wait_ge(s_PV, NP * hp + f + 1)
                            nc.scalar.activation(PT[:, f % 4, 0:(e - a) * 128], bank(4 + f % 2)[:, 0:(e - a) * 128],
                                                 ACT.Copy).then_inc(s_evA, 1)
                    if g % 2 == 0 and g >= 2:
                        evac_zT(g // 2 - 1)
                evac_zT(NS // 2 - 1)

            evac_qk(0)
            over_pairs(act, pair)
            if STAGE < 2:
                return
            act.wait_ge(s_var, 2)
            nc.scalar.activation(std[:], mv[:, :, 1], ACT.Sqrt, bias=eps[:, 0:1]).then_inc(s_std, 1)
            evac_tiles(2)
            act.wait_ge(s_lgd, 1)
            nc.scalar.activation(cand[:], logit[:], ACT.Exp).then_inc(s_lge, 1)

            def evac_xs(s, u):
                act.wait_ge(s_xst, s + 3)
                nc.scalar.activation(xsT[:, u, :, :], bank(u)[:, 0:256].rearrange("p (c t) -> p c t", c=KC), ACT.Copy).then_inc(s_xsT, 1)

            def gelu(s, u):
                e = act.value_load(expi[0:1, bass.ds(s, 1)], min_val=0, max_val=EXPERTS - 1)
                act.wait_ge(s_ht, s + 1)
                alone(act)
                for f in range(8):
                    last = nc.scalar.activation(gelT[:, f, :], bank(4, 2)[:, f * 128:(f + 1) * 128], ACT.Gelu, bias=b_1[:, bass.ds(8 * e + f, 1)])
                last.then_inc(s_gel, 1)

            act.wait_ge(s_pos, 1)
            act.wait_ge(s_rw, 64)
            evac_xs(0, 0)
            with act.Fori(0, SLOT_TILES // 2) as i:
                evac_xs(2 * i + 1, 1)
                gelu(2 * i, 0)
                evac_xs(2 * i + 2, 0)
                gelu(2 * i + 1, 1)
            gelu(SLOT_TILES - 1, 0)
            if STAGE < 3:
                return
            act.wait_ge(s_var, 3)
            nc.scalar.activation(std[:], mv[:, :, 1], ACT.Sqrt, bias=eps[:, 0:1]).then_inc(s_std, 1)
            for j in range(4):
                act.wait_ge(l_wt, j + 1)
                nc.scalar.activation(wlT[:, :, j, :], bank(j).rearrange("p (c d) -> p c d", c=KC), ACT.Copy).then_inc(l_wT, 1)
            act.wait_ge(l_ini, 1)

            def lin_front(n, u):
                act.wait_ge(l_xt, n + 3)
                nc.scalar.activation(xT[:, u, :, :], bank(7)[:, 0:256].rearrange("p (c t) -> p c t", c=KC), ACT.Copy).then_inc(l_xT, 1)
                act.wait_ge(l_A, n + 1)
                nc.scalar.activation(eT[:], bank(0), ACT.Exp).then_inc(l_eA, 1)
                act.wait_ge(l_Bk, n + 1)
                nc.scalar.activation(vaug[:, u, :, 0:16], bank(1)[:, 256:512].rearrange("p (h d) -> p h d", h=LHEADS), ACT.Copy)
                nc.scalar.activation(ek[:], bank(1)[:, 0:256], ACT.Exp).then_inc(l_eB, 1)

            def lin_back(n, u, i):
                act.wait_ge(l_ot, n + 2)
                nc.scalar.activation(oT[:], bank(5)[:, 0:256].rearrange("p (c t) -> p c t", c=KC), ACT.Copy).then_inc(l_oT, 1)

            lin_loop(act, lin_front, lin_back)
            if STAGE < 4:
                return
            act.wait_ge(s_var, 4)
            nc.scalar.activation(std[:], mv[:, :, 1], ACT.Sqrt, bias=eps[:, 0:1]).then_inc(s_std, 1)
            evac_tiles(3)
            act.wait_ge(g_w, 16 * 14)
            act.wait_ge(g_lt, 1)
            act.wait_ge(g_cw, 1)
            for j in range(2):
                rows = slice(64 * j, 64 * j + 64)
                last = nc.scalar.activation(linT[rows, j, :], bank(2)[rows, 0:256], ACT.Copy)
            last.then_inc(g_lT, 1)
            for m in range(4):
                act.wait_ge(g_xc, m + 1)
                nc.scalar.activation(xc[:, m * 512:(m + 1) * 512], bank(4 + m), ACT.Identity, bias=gcols[:, 0:1]).then_inc(g_xce, 1)
            act.wait_ge(g_bv, 1)
            nc.scalar.activation(bstd[:], bmv[:, 1:2], ACT.Sqrt, bias=eps[:, 0:1]).then_inc(g_bs, 1)
            act.wait_ge(g_sc, 1)
            nc.scalar.activation(xa[:], xc[:], ACT.Gelu, bias=bsc[:, 2:3], scale=bsc[:, 1:2]).then_inc(g_xa, 1)
            with act.Fori(0, TILES // 2) as i:
                for u in range(2):
                    n = 2 * i + u
                    act.wait_ge(g_nm, n + 1)
                    for j in range(2):
                        nc.scalar.activation(ef[:, u, j, :], L[:, u, j, :], ACT.Exp, bias=nmx[:, u, j:j + 1], accum_out=esum[:, u, j:j + 1])
                        last = nc.scalar.activation(er[:, u, j, :], Lr[:, u, j, :], ACT.Exp, bias=nmx[:, u, j:j + 1])
                    last.then_inc(g_e, 1)
                    act.wait_ge(g_xt, n + 2)
                    nc.scalar.activation(xgT[:, u, :, :], bank(4 + u)[:, 0:256].rearrange("p (c t) -> p c t", c=KC), ACT.Copy).then_inc(g_xT, 1)

        @block.vector
        def _(dve):
            dve.wait_ge(s_cst, 16)
            dve.wait_ge(s_small, 48)
            for c in range(8):
                for j in range(TAPS):
                    nc.vector.tensor_scalar(taps32[:, c, j, :], const("group4"), conv_w[:, c, j:j + 1], read[:, 0:1],
                                            ALU.mult, ALU.mult)
                last = nc.vector.tensor_scalar(bias32[:, c, :], const("group4"), conv_b[:, c:c + 1], read[:, 0:1],
                                               ALU.mult, ALU.mult)
            last.then_inc(s_cbias, 1)
            dve.drain()
            nc.vector.tensor_copy(taps_hi[:], taps32[:])
            dve.drain()
            nc.vector.tensor_tensor(taps_lo[:], taps32[:], taps_hi[:], ALU.subtract).then_inc(s_taps, 1)
            dve.wait_ge(s_cb, 1)
            nc.vector.tensor_copy(conv_bias[:], bank(4)[:, 0:256]).then_inc(s_taps, 1)
            dve.wait_ge(s_m16, 1)

            def evac_lo(n, u):
                dve.wait_ge(s_xhi, n + 1)
                nc.vector.tensor_tensor(x_lo[:, u, :, 3:131], bank(2 * u, 2).rearrange("p (c t) -> p c t", c=8),
                                        x_hi[:, u, :, 3:131], ALU.subtract).then_inc(s_xlo, 1)

            def tok(i, u, last):
                dve.wait_ge(s_conv, 2 * i + u + 3)
                if not last:
                    nc.vector.tensor_copy(x_lo[:, u, :, 0:3], x_lo[:, u, :, 128:131])
                nc.vector.tensor_tensor(H[:, 8 * u + i, :], bank(4 + u)[:, 0:256], conv_bias[:], ALU.add).then_inc(s_h0, 1)
                dve.drain()

            evac_lo(0, 0)
            with dve.Fori(0, T // 128 - 1) as i:
                evac_lo(2 * i + 1, 1)
                tok(i, 0, False)
                evac_lo(2 * i + 2, 0)
                tok(i, 1, False)
            evac_lo(TILES - 1, 1)
            tok(T // 128 - 1, 0, True)
            tok(T // 128 - 1, 1, True)

            def layernorm_stats(k):
                with dve.Fori(0, TILES // 2) as i:
                    for u in range(2):
                        nc.vector.bn_stats(stats[:, bass.ds(2 * i + u, 1), :].rearrange("p a s -> p (a s)"), H[:, 2 * i + u, :])
                dve.drain()
                for t in range(TILES):
                    nc.vector.bn_aggr(mv[:, t, :], stats[:, t, :])
                dve.drain()
                nc.vector.tensor_copy(stats[:, 0, 0:1], eps[:, 0:1]).then_inc(s_var, 1)
                dve.wait_ge(s_std, k)
                nc.vector.reciprocal(rstd[:], std[:])
                dve.drain()

            layernorm_stats(1)
            if STAGE < 1:
                return

            def normalise(k, keep):
                with dve.Fori(0, TILES // 2) as i:
                    for u in range(2):
                        args = (H[:, 2 * i + u, :], mv[:, 2 * i + u, 0:1], rstd[:, bass.ds(2 * i + u, 1)], ALU.subtract, ALU.mult)
                        dve.wait_ge(s_xnT, TILES * (k - 1) + 2 * i + u + 1)
                        nc.vector.tensor_scalar(xn[:, u, :], *args).then_inc(s_xn, 1)
                        if keep:
                            nc.vector.tensor_scalar(XN[:, 2 * i + u, :], *args)

            normalise(1, False)

            def rotate(hp):
                for m in range(NQK + 1):
                    if m < NQK:
                        t0 = (m // 2) % 2 * 512
                        dve.wait_ge(s_qf, NQK * hp + m + 1)
                        alone(dve)
                        nc.vector.stream_shuffle(q_swap[:], qf[:, m % 2, :], [(r + 16) % 32 for r in range(32)])
                        dve.drain()
                        nc.vector.tensor_tensor(q_sin[:], q_swap[:], rope[:, 1, t0:t0 + 512], ALU.mult)
                        dve.drain()
                        dve.wait_ge(s_cos, NQK * hp + m + 1)
                        if m >= 2:
                            dve.wait_ge(s_hi, NQK * hp + m - 1)
                        nc.vector.tensor_tensor(q_rot[:, m % 2, :], q_sin[:], q_cos[:, m % 2, :], ALU.add).then_inc(s_rot, 1)
                    if m >= 1:
                        k = m - 1
                        dve.wait_ge(s_hi, NQK * hp + k + 1)
                        dst = lo_q[:] if k % 2 == 0 else lo_k[:, LOP[0], :]
                        nc.vector.tensor_tensor(dst[:, k // 2 * 512:k // 2 * 512 + 512], q_rot[:, k % 2, :],
                                                hi[:, k % 2, k // 2 * 512:k // 2 * 512 + 512], ALU.subtract).then_inc(s_lo, 1)

            def evac_v(hp, par):
                for m in range(NV):
                    dve.wait_ge(s_vp, NV * hp + m + 2)
                    nc.vector.tensor_copy(V[:, par, 4 * m:4 * m + 4, :], bank(m % 4).rearrange("p (t d) -> p t d", t=4)).then_inc(s_vev, 1)

            LOP = [0]
            rotate(0)
            evac_v(0, 0)
            dve.drain()
            nc.vector.tensor_tensor(H[:], H[:], b_o[:].unsqueeze(1).to_broadcast([128, TILES, D]), ALU.add)
            dve.drain()

            def pair(hp, par, last):
                if not last:
                    LOP[0] = 1 - par
                    dve.wait_ge(s_dup[par], 64 * (hp - par) + 128)
                    rotate(hp + 1)
                    evac_v(hp + 1, 1 - par)

                def maximum(g):
                    b, qt, h = STEPS[g]
                    w = (qt + 1) * 128
                    dve.wait_ge(s_S, NS * hp + g + 2)
                    nc.vector.tensor_reduce(neg_max[:, g % 4:g % 4 + 1], bank(2 * (g % 2), 2)[:, 0:w], AX.X, ALU.max,
                                            negate=True).then_inc(s_mx, 1)

                maximum(0)
                for g in range(NS):
                    if g + 1 < NS:
                        maximum(g + 1)
                    for f, a, e in PARTS[g]:
                        if f % 2 == 0:
                            dve.wait_ge(s_T, NP * hp + f + 3)
                            dve.wait_ge(s_PV, NP * hp + f + 1)
                            nc.vector.tensor_copy(PT[:, f % 4, 0:(e - a) * 128], bank(4 + f % 2)[:, 0:(e - a) * 128]).then_inc(s_evD, 1)
                    b, qt, h = STEPS[g]
                    k = g // 2
                    dve.wait_ge(s_P, NS * hp + g + 1)
                    nc.vector.reciprocal(inv_sum[:, g % 4:g % 4 + 1], row_sum[:, g % 4:g % 4 + 1])
                    dve.drain()
                    dve.wait_ge(s_PV, NP * hp + PARTS[g][-1][0] + 1 + 4)
                    if h == 0:
                        dve.wait_ge(s_zt, 16 * hp + k + 1)
                    nc.vector.tensor_scalar(z[:, k % 2, 64 * h:64 * h + 64], bank(6)[:, 64 * h:64 * h + 64],
                                            inv_sum[:, g % 4:g % 4 + 1], None, ALU.mult).then_inc(s_zn, 1)
                for k in range(8):
                    dve.wait_ge(s_WO, 8 * hp + k + 2)
                    hh = H[:, 2 * k:2 * k + 2, :]
                    nc.vector.tensor_tensor(hh, bank(4 + k % 2).rearrange("p (t d) -> p t d", t=2), hh, ALU.add).then_inc(s_h1, 1)
                dve.drain()

            over_pairs(dve, pair)
            if STAGE < 2:
                return
            layernorm_stats(2)
            normalise(2, True)
            dve.drain()
            dve.wait_ge(s_lg, 1)
            dve.wait_ge(s_rw, 64)
            flat = lambda a: a[:].rearrange("p t e -> p (t e)")
            over_e = lambda a: a.unsqueeze(2).to_broadcast([128, TILES, EXPERTS])
            nc.vector.tensor_tensor(logit[:], bank(2)[:, 0:128].rearrange("p (t e) -> p t e", e=EXPERTS),
                                    b_r[:].unsqueeze(1).to_broadcast([128, TILES, EXPERTS]), ALU.add)
            dve.drain()
            nc.vector.tensor_reduce(top[:], logit[:], AX.X, ALU.max)
            dve.drain()
            nc.vector.tensor_tensor(logit[:], logit[:], over_e(top[:]), ALU.subtract).then_inc(s_lgd, 1)
            dve.drain()
            nc.vector.tensor_scalar(flat(pick), flat(logit), 0.0, None, ALU.is_equal)
            dve.wait_ge(s_lge, 1)
            nc.vector.tensor_reduce(posf[:], cand[:], AX.X, ALU.add)
            dve.drain()
            nc.vector.reciprocal(gate[:], posf[:])
            nc.vector.scalar_tensor_tensor(flat(cand), flat(pick), -float(EXPERTS), const("expert_plus"), ALU.mult, ALU.add)
            dve.drain()
            nc.vector.tensor_reduce(top[:], cand[:], AX.X, ALU.min)
            dve.drain()
            nc.vector.tensor_tensor(pick[:], const("expert").rearrange("p (t e) -> p t e", e=EXPERTS), over_e(top[:]), ALU.is_equal).then_inc(s_oh, 1)
            dve.wait_ge(s_rk, 1)
            nc.vector.tensor_copy(flat(tot), bank(4)[:, 0:128])
            nc.vector.tensor_copy(scan[:, 0, :, :].rearrange("p t e -> p (t e)"), bank(4)[:, 0:128])
            dve.drain()
            a, sh = 0, 1
            while sh < TILES:
                nc.vector.tensor_copy(scan[:, 1 - a, 0:sh, :], scan[:, a, 0:sh, :])
                nc.vector.tensor_tensor(scan[:, 1 - a, sh:TILES, :], scan[:, a, sh:TILES, :], scan[:, a, 0:TILES - sh, :], ALU.add)
                dve.drain()
                a, sh = 1 - a, 2 * sh
            count = scan[:, a, TILES - 1, :]
            nc.vector.tensor_tensor(more[:], count.unsqueeze(2).to_broadcast([128, EXPERTS, TILES]),
                                    const("k128").rearrange("p (e k) -> p e k", e=EXPERTS), ALU.is_gt)
            dve.drain()
            nc.vector.tensor_reduce(ntile[:], more[:], AX.X, ALU.add)
            dve.drain()
            nc.vector.tensor_copy(cum[:, 0, :], ntile[:])
            dve.drain()
            c, sh = 0, 1
            while sh < EXPERTS:
                nc.vector.tensor_copy(cum[:, 1 - c, 0:sh], cum[:, c, 0:sh])
                nc.vector.tensor_tensor(cum[:, 1 - c, sh:EXPERTS], cum[:, c, sh:EXPERTS], cum[:, c, 0:EXPERTS - sh], ALU.add)
                dve.drain()
                c, sh = 1 - c, 2 * sh
            nc.vector.tensor_tensor(start[:], cum[:, c, :], ntile[:], ALU.subtract)
            nc.vector.tensor_tensor(past[:], cum[:, c, :].unsqueeze(1).to_broadcast([128, SLOT_TILES, EXPERTS]),
                                    const("slot_tile").rearrange("p (s e) -> p s e", e=EXPERTS), ALU.is_le)
            nc.vector.tensor_tensor(cand[:], scan[:, a, :, :], tot[:], ALU.subtract)
            dve.drain()
            nc.vector.tensor_scalar(start[:], start[:], 128.0, None, ALU.mult)
            nc.vector.tensor_reduce(expf[:], past[:], AX.X, ALU.add)
            nc.vector.tensor_tensor(flat(cand), bank(3)[:, 0:128], flat(cand), ALU.add)
            dve.drain()
            nc.vector.tensor_scalar(expi[:], expf[:], float(EXPERTS - 1), None, ALU.min)
            nc.vector.tensor_tensor(cand[:], cand[:], start[:].unsqueeze(1).to_broadcast([128, TILES, EXPERTS]), ALU.add)
            dve.drain()
            nc.vector.tensor_tensor(cand[:], cand[:], pick[:], ALU.mult)
            dve.drain()
            nc.vector.tensor_reduce(posf[:], cand[:], AX.X, ALU.add)
            dve.drain()
            nc.vector.tensor_copy(pos[:], posf[:])
            dve.drain()
            dve.sem_inc(s_pos, 1)

            def evac_hid(s, u):
                dve.wait_ge(s_hid, s + 1)
                nc.vector.tensor_copy(hid, bank(2, 2)).then_inc(s_he, 1)

            def evac_y(s, u, i):
                dve.wait_ge(s_y, s + 1)
                if not isinstance(i, int) or i >= 1:
                    dve.wait_ge(s_ys[u], 16 * i)
                nc.vector.tensor_copy(ys[:, u, :], bank(6 + u)[:, 0:256]).then_inc(s_ye, 1)

            evac_hid(0, 0)
            evac_hid(1, 1)
            evac_y(0, 0, 0)
            evac_hid(2, 0)
            evac_y(1, 1, 0)
            with dve.Fori(1, SLOT_TILES // 2) as i:
                evac_hid(2 * i + 1, 1)
                evac_y(2 * i, 0, i)
                evac_hid(2 * i + 2, 0)
                evac_y(2 * i + 1, 1, i)
            evac_y(SLOT_TILES - 1, 0, SLOT_TILES // 2)
            for t in range(TILES):
                if t == 0:
                    dve.wait_ge(s_g, 16 * TILES)
                last = nc.vector.scalar_tensor_tensor(H[:, t, :], XN[:, t, :], gate[:, t:t + 1], H[:, t, :], ALU.mult, ALU.add)
                last.then_inc(s_h2, 1)
            dve.drain()
            if STAGE < 3:
                return
            layernorm_stats(3)
            dve.wait_ge(l_ini, 1)

            def lin_front(n, u):
                dve.wait_ge(l_xt, n + 1)
                nc.vector.tensor_scalar(xn[:, u, :], H[:, lin_tile(n, u), :], mv[:, lin_tile(n, u), 0:1],
                                        rstd[:, bass.ds(lin_tile(n, u), 1)], ALU.subtract, ALU.mult).then_inc(l_xn, 1)
                dve.wait_ge(l_mA, n + 1)
                dve.wait_ge(l_kz, n + 1)
                nc.vector.scalar_tensor_tensor(qkT[:, u, :, :].rearrange("p a t -> p (a t)"), bank(0), 0.0, eT[:], ALU.max, ALU.add).then_inc(l_fA, 1)
                dve.wait_ge(l_mB, n + 1)
                nc.vector.scalar_tensor_tensor(ktok[:, u, :], bank(1)[:, 0:256], 0.0, ek[:], ALU.max, ALU.add).then_inc(l_fB, 1)

            def lin_back(n, u, i):
                for r in range(4):
                    dve.wait_ge(l_at, 4 * n + r + 2)
                    for c in range(KC):
                        last = nc.vector.tensor_tensor(AT[:, 8 * c + 2 * r:8 * c + 2 * r + 2, :],
                                                       bank(2 + r % 2)[:, 256 * c:256 * c + 256].rearrange("p (h t) -> p h t", h=2),
                                                       const("causal_mul").unsqueeze(1).to_broadcast([128, 2, 128]), ALU.mult)
                    last.then_inc(l_AT, 1)
                dve.wait_ge(l_st, n + 1)
                nc.vector.tensor_tensor(sdel[:].rearrange("p (c x) -> p c x", c=2), bank(4)[:, 0:272].rearrange("p (c x) -> p c x", c=2),
                                        const("own_head").unsqueeze(1).to_broadcast([128, 2, 136]), ALU.mult)
                dve.wait_ge(l_num, n + 3)
                num = bank(6)[:, 0:272].rearrange("p (h x) -> p h x", x=17)
                nc.vector.tensor_scalar(den[:], num[:, :, 16], 1e-8, None, ALU.add)
                dve.drain()
                nc.vector.tensor_tensor(state[:, u, :], state[:, u, :], sdel[:], ALU.add).then_inc(l_sd, 1)
                nc.vector.reciprocal(den[:], den[:])
                dve.drain()
                nc.vector.tensor_tensor(o[:].rearrange("p (h x) -> p h x", x=16), num[:, :, 0:16],
                                        den[:].unsqueeze(2).to_broadcast([128, LHEADS, 16]), ALU.mult).then_inc(l_o, 1)
                dve.wait_ge(l_y, n + 2)
                hh = H[:, lin_tile(n, u), :]
                nc.vector.tensor_tensor(hh, bank(5)[:, 256:512], hh, ALU.add).then_inc(l_h3, 1)

            lin_loop(dve, lin_front, lin_back)
            dve.drain()
            if STAGE < 4:
                return
            layernorm_stats(4)
            normalise(3, True)
            dve.drain()
            dve.wait_ge(g_w, 16 * 14)
            nc.vector.tensor_tensor(H[:], H[:], bias_g[:].unsqueeze(1).to_broadcast([128, TILES, D]), ALU.add)
            for m in range(4):
                dve.wait_ge(g_xce, m + 1)
                nc.vector.bn_stats(bst[:, m, :], xc[:, m * 512:(m + 1) * 512])
            dve.drain()
            nc.vector.bn_aggr(bmv[:], bst[:].rearrange("p a b -> p (a b)")).then_inc(g_bv, 1)
            dve.wait_ge(g_bs, 1)
            nc.vector.reciprocal(bsc[:, 0:1], bstd[:])
            dve.drain()
            nc.vector.tensor_tensor(bsc[:, 1:2], bsc[:, 0:1], gcols[:, 1:2], ALU.mult)
            dve.drain()
            nc.vector.tensor_tensor(bsc[:, 0:1], bsc[:, 1:2], bmv[:, 0:1], ALU.mult)
            dve.drain()
            nc.vector.tensor_tensor(bsc[:, 2:3], gcols[:, 2:3], bsc[:, 0:1], ALU.subtract).then_inc(g_sc, 1)
            with dve.Fori(0, TILES // 2) as i:
                for u in range(2):
                    n = 2 * i + u
                    dve.wait_ge(g_lg, n + 1)
                    nc.vector.tensor_tensor(L[:, u, :, :], bank(u).rearrange("p (j d) -> p j d", j=2), lin_b[:], ALU.add).then_inc(g_L, 1)
                    for r in range(TOPK // 8):
                        for j in range(2):
                            src = L if r == 0 else Lr
                            if r == 0:
                                dve.wait_ge(g_L, n + 1)
                            else:
                                dve.wait_ge(g_tk[j], 8 * n + 2 * r)
                            alone(dve)
                            nc.vector.max(m8[:, u, j, r, :], src[:, u, j, :]).then_inc(g_tk[j], 1)
                        for j in range(2):
                            src = L if r == 0 else Lr
                            dve.wait_ge(g_tk[j], 8 * n + 2 * r + 1)
                            alone(dve)
                            nc.vector.match_replace(Lr[:, u, j, :], m8[:, u, j, r, :], src[:, u, j, :], NEG).then_inc(g_tk[j], 1)
                        if r == 0:
                            nc.vector.tensor_scalar(nmx[:, u, :], m8[:, u, :, 0, 0], -1.0, None, ALU.mult)
                    dve.drain()
                    dve.sem_inc(g_nm, 1)
                    dve.wait_ge(g_e, n + 1)
                    nc.vector.reciprocal(einv[:, u, :], esum[:, u, :])
                    dve.drain()
                    dve.wait_ge(g_d, n + 1)
                    nc.vector.scalar_tensor_tensor(xg[:, u, :], ef[:, u, 1, :], einv[:, u, 1:2], XN[:, n, :], ALU.mult, ALU.mult).then_inc(g_xg, 1)
                    dve.wait_ge(g_fu, n + 2)
                    nc.vector.scalar_tensor_tensor(ob[:, u, :], ef[:, u, 0, :], einv[:, u, 0:1], bank(2 + u)[:, 0:256], ALU.mult, ALU.mult)
                    dve.drain()
                    nc.vector.tensor_tensor(H[:, n, :], H[:, n, :], ob[:, u, :], ALU.add)
                    dve.drain()
                    dve.wait_ge(g_in, n + 3)
                    nc.vector.tensor_tensor(H[:, n, :], bank(6 + u)[:, 0:256], H[:, n, :], ALU.add).then_inc(g_h, 1)

        @block.tensor
        def _(pe):
            pe.wait_ge(s_cst, 16)
            pe.wait_ge(s_cbias, 1)
            for c in range(8):
                last = nc.tensor.matmul(bank(4)[:, 32 * c:32 * c + 32], const("ones"), bias32[:, c, :], start=True, stop=True)
            last.then_inc(s_cb, 1)
            pe.wait_ge(s_taps, 2)

            def transpose_x(n, i, u):
                pe.wait_ge(s_x[u], 16 * i + 16)
                pe.wait_ge(s_xlo, n - 1) if isinstance(n, int) and n >= 2 else (None if isinstance(n, int) else pe.wait_ge(s_xlo, n - 1))
                for c in range(8):
                    last = nc.tensor.transpose(bank(2 * u, 2)[:, c * 128:(c + 1) * 128], x_in[:, u, c * 128:(c + 1) * 128], const("ident"))
                last.then_inc(s_xT, 1)

            def conv(n, u):
                pe.wait_ge(s_xhi, n + 1)
                pe.wait_ge(s_xlo, n + 1)
                if not isinstance(n, int) or n >= 2:
                    pe.wait_ge(s_h0, n - 1)
                first = True
                for c in range(8):
                    for xs, ws in ((x_hi, taps_hi), (x_hi, taps_lo), (x_lo, taps_hi)):
                        for j in range(TAPS):
                            last = nc.tensor.matmul(bank(4 + u)[:, 32 * c:32 * c + 32], xs[:, u, c, j:j + 128], ws[:, c, j, :],
                                                    start=first, stop=True, skip_group_check=True)
                            first = False
                last.then_inc(s_conv, 1)

            transpose_x(0, 0, 0)
            transpose_x(1, 0, 1)
            conv(0, 0)
            transpose_x(2, 1, 0)
            conv(1, 1)
            with pe.Fori(1, T // 128 - 1) as i:
                transpose_x(2 * i + 1, i, 1)
                conv(2 * i, 0)
                transpose_x(2 * i + 2, i + 1, 0)
                conv(2 * i + 1, 1)
            transpose_x(TILES - 1, T // 128 - 1, 1)
            conv(TILES - 2, 0)
            conv(TILES - 1, 1)
            if STAGE < 1:
                return
            pe.wait_ge(s_h0, TILES)

            def transpose_tiles(k):
                with pe.Fori(0, TILES // 2) as i:
                    for u in range(2):
                        pe.wait_ge(s_xn, TILES * (k - 1) + 2 * i + u + 1)
                        for c in range(KC):
                            last = nc.tensor.transpose(bank(u)[:, c * 128:(c + 1) * 128], xn[:, u, c * 128:(c + 1) * 128], const("ident"))
                        last.then_inc(s_xnt, 1)
            transpose_tiles(1)

            def project(hp):
                pe.wait_ge(s_perm, hp + 2)
                for m in range(NQK):
                    if m >= 4:
                        pe.wait_ge(s_qf, NQK * hp + m - 3)
                    for c in range(KC):
                        last = nc.tensor.matmul(bank(m % 4), w_qk[:, m % 2, c, :], xnT[:, c, m // 2 * 512:m // 2 * 512 + 512],
                                                start=(c == 0), stop=(c == KC - 1))
                    last.then_inc(s_qk, 1)
                pe.wait_ge(s_wv, 32 * hp + 32)
                for m in range(NV):
                    pe.wait_ge(s_qf, NQK * hp + m + 5)
                    for t in range(4):
                        tok = (4 * m + t) * 128
                        for c in range(KC):
                            last = nc.tensor.matmul(bank(m % 4)[:, t * 128:(t + 1) * 128], xnT[:, c, tok:tok + 128], w_v[:, c, :],
                                                    start=(c == 0), stop=(c == KC - 1))
                    last.then_inc(s_vp, 1)

            pe.wait_ge(s_xnT, TILES + 2)
            project(0)

            def pair(hp, par, last_pair):
                if not last_pair:
                    pe.wait_ge(s_vev, NV * hp + NV)
                    project(hp + 1)
                    pe.wait_ge(s_vev, NV * hp + 2 * NV)
                pe.wait_ge(s_dup[par], 64 * (hp - par) + 128)
                pe.wait_ge(s_lo, NQK * hp + NQK + 1)

                def scores(g):
                    b, qt, h = STEPS[g]
                    q0, w = b * T + qt * 128, (qt + 1) * 128
                    own = slice(64 * h, 64 * h + 64)
                    if g >= 2:
                        pe.wait_ge(s_P, NS * hp + g - 1)
                    for a in range(0, w, 512):
                        e = min(a + 512, w)
                        dst = bank(2 * (g % 2), 2)[:, a:e]
                        nc.tensor.matmul(dst, Q2[:, par, h, q0:q0 + 128], K2[:, par, h, b * T + a:b * T + e], start=True, stop=False)
                        last = nc.tensor.matmul(dst, Q2[own, par, h, q0:q0 + 128], lo_k[own, par, b * T + a:b * T + e],
                                                start=False, stop=True)
                        if e == w:
                            last = nc.tensor.matmul(bank(2 * (g % 2), 2)[:, w - 128:w], ident16[:], mask16[:], start=False, stop=True,
                                                    skip_group_check=True)
                    last.then_inc(s_S, 1)

                def transpose_z(k):
                    pe.wait_ge(s_zn, NS * hp + 2 * k + 4)
                    pe.wait_ge(s_zT, 16 * hp + k) if k else None
                    nc.tensor.transpose(bank(7)[:, 0:128], z[:, k % 2, :], const("ident")).then_inc(s_zt, 1)

                scores(0)
                for g in range(NS):
                    b, qt, h = STEPS[g]
                    if g + 1 < NS:
                        scores(g + 1)
                    pe.wait_ge(s_P, NS * hp + g + 1)
                    for f, a, e in PARTS[g]:
                        pe.wait_ge(s_evD if f % 2 == 0 else s_evA, NP // 2 * hp + f // 2 + 1)
                        for j in range(a, e):
                            last = nc.tensor.transpose(bank(4 + f % 2)[:, (j - a) * 128:(j - a + 1) * 128],
                                                       P[:, g % 2, j * 128:(j + 1) * 128], const("ident"))
                        last.then_inc(s_T, 1)
                    if g % 2 == 0 and g >= 2:
                        transpose_z(g // 2 - 1)
                    pe.wait_ge(s_zn, NS * hp + g + 2)
                    for f, a, e in PARTS[g]:
                        pe.wait_ge(s_evD if f % 2 == 0 else s_evA, NP // 2 * hp + f // 2 + 2)
                        for j in range(a, e):
                            last = nc.tensor.matmul(bank(6)[:, 64 * h:64 * h + 64], PT[:, f % 4, (j - a) * 128:(j - a + 1) * 128],
                                                    V[:, par, b * 8 + j, 64 * h:64 * h + 64], start=(j == 0), stop=(j == qt))
                        last.then_inc(s_PV, 1)
                transpose_z(NS // 2 - 1)
                pe.wait_ge(s_wo, 16 * hp + 16)
                for k in range(8):
                    pe.wait_ge(s_zT, 16 * hp + min(2 * k + 2, 16))
                    pe.wait_ge(s_h1, 8 * hp + max(k - 1, 0) + 1) if k >= 2 else None
                    for t in range(2):
                        last = nc.tensor.matmul(bank(4 + k % 2)[:, t * 256:(t + 1) * 256], zT[:, (2 * k + t) * 128:(2 * k + t + 1) * 128],
                                                w_o[:], start=True, stop=True)
                    last.then_inc(s_WO, 1)
                pe.wait_ge(s_h1, 8 * hp + 9)

            over_pairs(pe, pair)
            if STAGE < 2:
                return
            transpose_tiles(2)
            pe.wait_ge(s_xnT, 2 * TILES + 2)
            pe.wait_ge(s_rw, 64)
            for t in range(TILES):
                for c in range(KC):
                    last = nc.tensor.matmul(bank(2)[:, t * 8:(t + 1) * 8], xnT[:, c, t * 128:(t + 1) * 128], w_r[:, c, :],
                                            start=(c == 0), stop=(c == KC - 1))
            last.then_inc(s_lg, 1)
            pe.wait_ge(s_oh, 1)
            nc.tensor.matmul(bank(3)[:, 0:128], const("before"), pick[:].rearrange("p t e -> p (t e)"), start=True, stop=True)
            nc.tensor.matmul(bank(4)[:, 0:128], const("ones"), pick[:].rearrange("p t e -> p (t e)"), start=True, stop=True).then_inc(s_rk, 1)
            pe.wait_ge(s_pos, 1)

            def tr_xs(s, u, i):
                pe.wait_ge(s_xs[u], 16 * i + 16)
                for c in range(KC):
                    last = nc.tensor.transpose(bank(u)[:, c * 128:(c + 1) * 128], xs[:, u, c * 128:(c + 1) * 128], const("ident"))
                last.then_inc(s_xst, 1)

            def up(s, u):
                e = pe.value_load(expi[0:1, bass.ds(s, 1)], min_val=0, max_val=EXPERTS - 1)
                pe.wait_ge(s_xsT, s + 1)
                pe.wait_ge(s_he, s + 1)
                for a in range(2):
                    for c in range(KC):
                        last = nc.tensor.matmul(bank(2 + a), xsT[:, u, c, :], W1[:, bass.ds(e, 1), c, a * 512:(a + 1) * 512].rearrange("p a f -> p (a f)"),
                                                start=(c == 0), stop=(c == KC - 1))
                last.then_inc(s_hid, 1)

            def tr_hid(s, u):
                pe.wait_ge(s_he, s + 2)
                if not isinstance(s, int) or s >= 1:
                    pe.wait_ge(s_gel, s)
                for f in range(8):
                    last = nc.tensor.transpose(bank(4, 2)[:, f * 128:(f + 1) * 128], hid[:, f * 128:(f + 1) * 128], const("ident"))
                last.then_inc(s_ht, 1)

            def down(s, u):
                e = pe.value_load(expi[0:1, bass.ds(s, 1)], min_val=0, max_val=EXPERTS - 1)
                pe.wait_ge(s_gel, s + 1)
                if not isinstance(s, int) or s >= 2:
                    pe.wait_ge(s_ye, s - 1)
                for f in range(8):
                    nc.tensor.matmul(bank(6 + u)[:, 0:256], gelT[:, f, :], W2[:, bass.ds(e, 1), f, :].rearrange("p a f -> p (a f)"), start=(f == 0), stop=False)
                nc.tensor.matmul(bank(6 + u)[:, 0:256], const("ones")[0:1, :], b_2[0:1, bass.ds(e * D, D)], start=False, stop=True).then_inc(s_y, 1)

            pe.wait_ge(s_w1, 128)
            tr_xs(0, 0, 0)
            up(0, 0)
            pe.wait_ge(s_w2, 128)

            def slot(s, u, i, iu):
                tr_xs(s + 1, 1 - u, iu)
                tr_hid(s, u)
                up(s + 1, 1 - u)
                down(s, u)

            slot(0, 0, 0, 0)
            slot(1, 1, 0, 1)
            with pe.Fori(1, SLOT_TILES // 2) as i:
                slot(2 * i, 0, i, i)
                slot(2 * i + 1, 1, i, i + 1)
            tr_hid(SLOT_TILES - 1, 0)
            down(SLOT_TILES - 1, 0)
            if STAGE < 3:
                return
            pe.wait_ge(s_ye, SLOT_TILES)
            pe.wait_ge(l_w, 64)
            for j in range(4):
                for c in range(KC):
                    for oc in range(2):
                        last = nc.tensor.transpose(bank(j)[:, c * 256 + oc * 128:c * 256 + oc * 128 + 128], wl_in[:, j, oc, c * 128:(c + 1) * 128], const("ident"))
                last.then_inc(l_wt, 1)
            pe.wait_ge(l_wT, 4)

            def lin_front(n, u):
                pe.wait_ge(l_xn, n + 1)
                if not isinstance(n, int) or n >= 1:
                    pe.wait_ge(l_xT, n)
                for c in range(KC):
                    last = nc.tensor.transpose(bank(7)[:, c * 128:(c + 1) * 128], xn[:, u, c * 128:(c + 1) * 128], const("ident"))
                last.then_inc(l_xt, 1)
                pe.wait_ge(l_xT, n + 1)
                if not isinstance(n, int) or n >= 1:
                    pe.wait_ge(l_fA, n)
                    pe.wait_ge(l_fB, n)
                for a in range(4):
                    w = (2, 2, 0, 0)[a]
                    for c in range(KC):
                        last = nc.tensor.matmul(bank(0)[:, a * 128:(a + 1) * 128], wlT[:, c, w, a % 2 * 128:a % 2 * 128 + 128], xT[:, u, c, :],
                                                start=(c == 0), stop=(c == KC - 1))
                last.then_inc(l_A, 1)
                for c in range(KC):
                    last = nc.tensor.matmul(bank(1), xT[:, u, c, :], wlT[:, c, 0:2, :].rearrange("p a d -> p (a d)"),
                                            start=(c == 0), stop=(c == KC - 1))
                last.then_inc(l_Bk, 1)

            def lin_back(n, u, i):
                pe.wait_ge(l_kz, n + 3)
                pe.wait_ge(l_fB, n + 1)
                pe.wait_ge(l_eB, n + 1)
                for r in range(4):
                    pe.wait_ge(l_AT, 4 * n + r + 1)
                    for k in range(4):
                        c, par = k // 2, k % 2
                        rows, g = slice(32 * r, 32 * r + 32), r
                        last = nc.tensor.matmul(bank(2 + r % 2)[:, k * 128:k * 128 + 128], kz[rows, u, par, c, :], qkT[rows, u, c, :],
                                                start=True, stop=True, tile_position=(32 * g, 0))
                    last.then_inc(l_at, 1)
                pe.wait_ge(l_sd, n + 1)
                pe.wait_ge(l_o, n + 1)
                for c in range(KC):
                    nc.tensor.matmul(bank(6)[:, c * 136:(c + 1) * 136], qkT[:, u, c, :], state[:, u, c * 136:(c + 1) * 136], start=(c == 0), stop=True, skip_group_check=True)
                pe.wait_ge(l_AT, 4 * n + 6)
                for h in range(LHEADS):
                    last = nc.tensor.matmul(bank(6)[:, h * 17:(h + 1) * 17], AT[:, h, :], vaug[:, u, h, :], start=False, stop=True, skip_group_check=True)
                last.then_inc(l_num, 1)
                pe.wait_ge(l_sd, n + 2)
                for c in range(KC):
                    last = nc.tensor.matmul(bank(4)[:, c * 136:(c + 1) * 136], ktok[:, u, c * 128:(c + 1) * 128],
                                            vaug[:, u, 8 * c:8 * c + 8, :].rearrange("p h x -> p (h x)"), start=True, stop=True)
                last.then_inc(l_st, 1)
                pe.wait_ge(l_o, n + 2)
                pe.wait_ge(l_h3, n + 1)
                for c in range(KC):
                    last = nc.tensor.transpose(bank(5)[:, c * 128:(c + 1) * 128], o[:, c * 128:(c + 1) * 128], const("ident"))
                last.then_inc(l_ot, 1)
                pe.wait_ge(l_oT, n + 1)
                for c in range(KC):
                    last = nc.tensor.matmul(bank(5)[:, 256:512], oT[:, c, :], wlT[:, c, 3, :], start=(c == 0), stop=(c == KC - 1))
                last.then_inc(l_y, 1)

            lin_loop(pe, lin_front, lin_back)
            if STAGE < 4:
                return
            pe.wait_ge(l_h3, TILES + 1)
            transpose_tiles(3)
            pe.wait_ge(g_w, 16 * 14)
            for c in range(2):
                last = nc.tensor.transpose(bank(2)[:, c * 128:(c + 1) * 128], lin_in[:, c, :], const("ident"))
            last.then_inc(g_lt, 1)
            pe.wait_ge(g_cw, 1)
            pe.wait_ge(s_xnT, 3 * TILES + 2)
            for m in range(4):
                for c in range(KC):
                    last = nc.tensor.matmul(bank(4 + m), CW[:, c, :], xnT[:, c, m * 512:(m + 1) * 512], start=(c == 0), stop=(c == KC - 1))
                last.then_inc(g_xc, 1)
            pe.wait_ge(g_lT, 1)
            pe.wait_ge(g_xce, 4)
            def g_front(n, u, first):
                pe.wait_ge(g_cp, n + 1)
                if not first:
                    pe.wait_ge(g_L, n - 1)
                nc.tensor.matmul(bank(u), xat[:, u, :], linT[:].rearrange("p j d -> p (j d)"), start=True, stop=True).then_inc(g_lg, 1)
                if not first:
                    pe.wait_ge(g_h, n - 1)
                for c in range(KC):
                    last = nc.tensor.matmul(bank(2 + u)[:, 0:256], xgt[:, u, c, :], wg[:, c, :], start=(c == 0), stop=(c == KC - 1))
                last.then_inc(g_fu, 1)

            def g_back(n, u):
                pe.wait_ge(g_xg, n + 1)
                for c in range(KC):
                    last = nc.tensor.transpose(bank(4 + u)[:, c * 128:(c + 1) * 128], xg[:, u, c * 128:(c + 1) * 128], const("ident"))
                last.then_inc(g_xt, 1)
                pe.wait_ge(g_xT, n + 1)
                for c in range(KC):
                    last = nc.tensor.matmul(bank(6 + u)[:, 0:256], xgT[:, u, c, :], wg[:, c, :], start=(c == 0), stop=(c == KC - 1))
                last.then_inc(g_in, 1)

            g_front(0, 0, True)
            g_front(1, 1, True)
            g_back(0, 0)
            g_front(2, 0, False)
            g_back(1, 1)
            with pe.Fori(1, TILES // 2 - 1) as i:
                g_front(2 * i + 1, 1, False)
                g_back(2 * i, 0)
                g_front(2 * i + 2, 0, False)
                g_back(2 * i + 1, 1)
            g_front(TILES - 1, 1, False)
            g_back(TILES - 2, 0)
            g_back(TILES - 1, 1)


NAMES = ['x', 'L0_tok_conv_w', 'L0_tok_conv_b', 'L0_tok_read', 'L0_attn_W_Q', 'L0_attn_b_Q', 'L0_attn_W_K', 'L0_attn_b_K', 'L0_attn_W_V', 'L0_attn_b_V', 'L0_attn_W_O', 'L0_attn_b_O',
         'L0_ffn_W1', 'L0_ffn_b1', 'L0_ffn_W2', 'L0_ffn_b2', 'L0_ffn_Wr', 'L0_ffn_br', 'L1_attn_Wq', 'L1_attn_Wk', 'L1_attn_Wv', 'L1_attn_Wo',
         'L1_ffn_weight', 'L1_ffn_bias', 'L1_ffn_so_conv_w', 'L1_ffn_so_conv_b', 'L1_ffn_so_gamma', 'L1_ffn_so_beta', 'L1_ffn_so_lin_w',
         'L1_ffn_so_lin_b', 'L1_ffn_si_conv_w', 'L1_ffn_si_conv_b', 'L1_ffn_si_gamma', 'L1_ffn_si_beta', 'L1_ffn_si_lin_w', 'L1_ffn_si_lin_b']


def kernel(**inputs):
    import concourse.bacc as _bacc
    from concourse.bass_utils import run_bass_kernel_spmd as _run
    nc = _bacc.Bacc("TRN2", target_bir_lowering=False, num_devices=1)
    packed, where, rope = shape_constants()
    arrays = {n: np.ascontiguousarray(inputs[n]) for n in NAMES}
    arrays["consts"], arrays["rope"] = packed, rope
    arrays = {"in_" + n: a for n, a in arrays.items()}
    ins = {n[3:]: nc.dram_tensor(n, a.shape, mybir.dt.float32, kind="ExternalInput").ap() for n, a in arrays.items()}
    out = nc.dram_tensor("out_0_dram", (B, T, D), mybir.dt.float32, kind="ExternalOutput").ap()
    build(nc, ins, where, out)
    r = _run(nc, [arrays], core_ids=[0])
    return r.results[0]["out_0_dram"]
```

```python
import concourse.bass as bass
from concourse import mybir
from contextlib import ExitStack
import numpy as np

STAGE = 4

B, T, D, DV, TAPS = 2, 1024, 256, 4, 4
C = D * DV
N = B * T
TILES = N // 128
KC = D // 128
HEADS, DH = 16, 64
PAIRS = HEADS // 2
SCALE = 8.0
NEG = -1.0e30
EPS = 1e-5
EXPERTS, FF = 8, 1024
SLOT_TILES = TILES + EXPERTS - 1
LHEADS, LDH = 16, 16
GROUPS = D // 4
TOPK = 32


def shape_constants():
    p = np.arange(128)
    parts = {}
    parts["ident"] = np.eye(128)
    parts["causal_add"] = np.where(p[None, :] <= p[:, None], 0.0, NEG)
    parts["causal_mul"] = (p[:, None] <= p[None, :]).astype(float)
    parts["before"] = (p[:, None] < p[None, :]).astype(float)
    parts["ones"] = np.ones((128, 128))
    tile_of, expert = np.arange(128) // 8, np.arange(128) % 8
    parts["expert"] = np.broadcast_to(expert, (128, 128))
    parts["expert_plus"] = np.broadcast_to(expert + EXPERTS, (128, 128))
    parts["k128"] = np.broadcast_to(128 * (np.arange(128) % 16), (128, 128))
    parts["slot_tile"] = np.broadcast_to(np.arange(SLOT_TILES * EXPERTS) // EXPERTS, (128, SLOT_TILES * EXPERTS))
    parts["own_head"] = (p[:, None] // 16 == np.arange(136)[None, :] // 17).astype(float)
    parts["odd_head"] = (p[:, None] // 16 % 2 == np.arange(2)[None, :]).astype(float)
    parts["group4"] = (p[:, None] // 4 == np.arange(32)[None, :]).astype(float)
    arrays, where, at = [], {}, 0
    for name, a in parts.items():
        where[name] = (at, at + a.shape[1])
        at += a.shape[1]
        arrays.append(a)
    s = p % 64
    dim = (s % 32) // 16 * 32 + s // 32 * 16 + s % 16
    f = np.arange(32, dtype=np.float32)
    freq = (np.float32(10000.0) ** (f / np.float32(32))).astype(np.float32)
    angles = (np.arange(T, dtype=np.float32)[None, :] / freq[dim % 32][:, None]).astype(np.float32)
    sign = np.where(dim < 32, -1.0, 1.0)[:, None]
    rope = np.concatenate([np.cos(angles), sign * np.sin(angles)], axis=1)
    return (np.concatenate(arrays, axis=1).astype(np.float32), where, rope.astype(np.float32))


def build(nc, ins, where, out):
    f32, f16, bf16 = mybir.dt.float32, mybir.dt.float16, mybir.dt.bfloat16
    ALU, ACT, AX = mybir.AluOpType, mybir.ActivationFunctionType, mybir.AxisListType
    ctx = ExitStack()
    with ctx:
        def sem(name):
            return ctx.enter_context(nc.semaphore(name))

        def psum(name, cols):
            return ctx.enter_context(nc.psum_tensor(name, [128, cols], f32))

        banks = psum("banks", 8 * 512)

        def bank(b, n=1):
            return banks[:, b * 512:(b + n) * 512]

        def sb(name, shape, dt=f32, stack=ctx):
            return stack.enter_context(nc.sbuf_tensor(name, shape, dt))

        nconst = ins["consts"].shape[1]
        cst = sb("cst", [128, nconst])

        def const(name):
            a, b = where[name]
            return cst[:, a:b]

        H = sb("H", [128, TILES, D])
        mask16 = sb("mask16", [128, 128], bf16)
        ident16 = sb("ident16", [128, 128], bf16)
        eps = sb("eps", [128, 1])
        stats = sb("stats", [128, TILES, 6])
        mv = sb("mv", [128, TILES, 2])
        std = sb("std", [128, TILES])
        rstd = sb("rstd", [128, TILES])
        xn = sb("xn", [128, 2, D])
        XN = sb("XN", [128, TILES, D])
        xnT = sb("xnT", [128, KC, N])

        with ExitStack() as st:
            x_in = sb("x_in", [128, 2, C], stack=st)
            x_hi = sb("x_hi", [128, 2, 8, 131], f16, st)
            x_lo = sb("x_lo", [128, 2, 8, 131], f16, st)
            conv_w = sb("conv_w", [128, 8, TAPS], stack=st)
            conv_b = sb("conv_b", [128, 8], stack=st)
            read = sb("read", [128, 1], stack=st)
            taps32 = sb("taps32", [128, 8, TAPS, 32], stack=st)
            taps_hi = sb("taps_hi", [128, 8, TAPS, 32], f16, st)
            taps_lo = sb("taps_lo", [128, 8, TAPS, 32], f16, st)
            bias32 = sb("bias32", [128, 8, 32], stack=st)
            conv_bias = sb("conv_bias", [128, D], stack=st)
        with ExitStack() as st:
            rope = sb("rope", [128, 2, T], stack=st)
            w_in = sb("w_in", [128, 2, KC, 128], stack=st)
            w_qk = sb("w_qk", [128, 2, KC, 128], stack=st)
            w_v = sb("w_v", [128, KC, 128], stack=st)
            w_o = sb("w_o", [128, D], stack=st)
            b_in = sb("b_in", [128, 2, PAIRS], stack=st)
            b_v = sb("b_v", [128, PAIRS], stack=st)
            b_o = sb("b_o", [128, D], stack=st)
            qf = sb("qf", [128, 2, 512], stack=st)
            q_swap = sb("q_swap", [128, 512], stack=st)
            q_sin = sb("q_sin", [128, 512], stack=st)
            q_cos = sb("q_cos", [128, 2, 512], stack=st)
            q_rot = sb("q_rot", [128, 2, 512], stack=st)
            hi = sb("hi", [128, 2, N], f16, st)
            lo_q = sb("lo_q", [128, N], f16, st)
            lo_k = sb("lo_k", [128, 2, N], f16, st)
            Q2 = sb("Q2", [128, 2, 2, N], f16, st)
            K2 = sb("K2", [128, 2, 2, N], f16, st)
            V = sb("V", [128, 2, TILES, 128], stack=st)
            neg_max = sb("neg_max", [128, 4], stack=st)
            row_sum = sb("row_sum", [128, 4], stack=st)
            inv_sum = sb("inv_sum", [128, 4], stack=st)
            P = sb("P", [128, 2, T], stack=st)
            PT = sb("PT", [128, 4, 512], stack=st)
            z = sb("z", [128, 2, 128], stack=st)
            zT = sb("zT", [128, N], stack=st)

        with ExitStack() as st:
            W1 = sb("W1", [128, EXPERTS, KC, FF], stack=st)
            W2 = sb("W2", [128, EXPERTS, FF // 128, D], stack=st)
            w_r = sb("w_r", [128, KC, EXPERTS], stack=st)
            b_r = sb("b_r", [128, EXPERTS], stack=st)
            b_1 = sb("b_1", [128, EXPERTS * 8], stack=st)
            b_2 = sb("b_2", [1, EXPERTS * D], stack=st)
            logit = sb("logit", [128, TILES, EXPERTS], stack=st)
            top = sb("top", [128, TILES], stack=st)
            pick = sb("pick", [128, TILES, EXPERTS], stack=st)
            cand = sb("cand", [128, TILES, EXPERTS], stack=st)
            gate = sb("gate", [128, TILES], stack=st)
            scan = sb("scan", [128, 2, TILES, EXPERTS], stack=st)
            tot = sb("tot", [128, TILES, EXPERTS], stack=st)
            more = sb("more", [128, EXPERTS, TILES], stack=st)
            ntile = sb("ntile", [128, EXPERTS], stack=st)
            cum = sb("cum", [128, 2, EXPERTS], stack=st)
            start = sb("start", [128, EXPERTS], stack=st)
            past = sb("past", [128, SLOT_TILES, EXPERTS], stack=st)
            posf = sb("posf", [128, TILES], stack=st)
            pos = sb("pos", [128, TILES], mybir.dt.uint32, st)
            expf = sb("expf", [128, SLOT_TILES], stack=st)
            expi = sb("expi", [128, SLOT_TILES], mybir.dt.int32, st)
            xs = sb("xs", [128, 2, D], stack=st)
            xsT = sb("xsT", [128, 2, KC, 128], stack=st)
            hid = xnT[:, 0, 0:FF]
            gelT = xnT[:, 1, 0:FF].rearrange("p (f t) -> p f t", f=8)
            ys = sb("ys", [128, 2, D], stack=st)
        with ExitStack() as st:
            wl_in = sb("wl_in", [128, 4, 2, D], stack=st)
            wlT = sb("wlT", [128, KC, 4, D], stack=st)
            xT = sb("xT", [128, 2, KC, 128], stack=st)
            eT = sb("eT", [128, 512], stack=st)
            ek = sb("ek", [128, D], stack=st)
            qkT = sb("qkT", [128, 2, 4, 128], stack=st)
            kz = sb("kz", [128, 2, 2, KC, 128], stack=st)
            ktok = sb("ktok", [128, 2, D], stack=st)
            vaug = sb("vaug", [128, 2, LHEADS, 17], stack=st)
            AT = sb("AT", [128, LHEADS, 128], stack=st)
            state = sb("state", [128, B, 272], stack=st)
            sdel = sb("sdel", [128, 272], stack=st)
            den = sb("den", [128, LHEADS], stack=st)
            o = sb("o", [128, D], stack=st)
            oT = sb("oT", [128, KC, 128], stack=st)
        with ExitStack() as st:
            wg = sb("wg", [128, KC, D], stack=st)
            cwc = sb("cwc", [128, 2, KC], stack=st)
            gcols = sb("gcols", [128, 3], stack=st)
            lin_in = sb("lin_in", [128, 2, 128], stack=st)
            linT = sb("linT", [128, 2, D], stack=st)
            lin_b = sb("lin_b", [128, 2, D], stack=st)
            bias_g = sb("bias_g", [128, D], stack=st)
            CW = sb("CW", [128, KC, 128], stack=st)
            xc = sb("xc", [128, N], stack=st)
            xa = sb("xa", [128, N], stack=st)
            bst = sb("bst", [128, 4, 6], stack=st)
            bmv = sb("bmv", [128, 2], stack=st)
            bstd = sb("bstd", [128, 1], stack=st)
            bsc = sb("bsc", [128, 3], stack=st)
            xat = sb("xat", [128, 2, 128], stack=st)
            xgt = sb("xgt", [128, 2, KC, 128], stack=st)
            L = sb("L", [128, 2, 2, D], stack=st)
            Lr = sb("Lr", [128, 2, 2, D], stack=st)
            m8 = sb("m8", [128, 2, 2, 4, 8], stack=st)
            nmx = sb("nmx", [128, 2, 2], stack=st)
            ef = sb("ef", [128, 2, 2, D], stack=st)
            er = sb("er", [128, 2, 2, D], stack=st)
            esum = sb("esum", [128, 2, 2], stack=st)
            einv = sb("einv", [128, 2, 2], stack=st)
            ob = sb("ob", [128, 2, D], stack=st)
            xg = sb("xg", [128, 2, D], stack=st)
            xgT = sb("xgT", [128, 2, KC, 128], stack=st)
        sorted_x = nc.dram_tensor("sorted_x", (SLOT_TILES * 128, D), f32, kind="Internal").ap()
        sorted_y = nc.dram_tensor("sorted_y", (SLOT_TILES * 128, D), f32, kind="Internal").ap()

        s_passed = {e.engine: sem("s_passed_" + n) for n, e in
                    (("sp", nc.sync), ("act", nc.scalar), ("dve", nc.vector), ("pe", nc.tensor), ("pool", nc.gpsimd))}
        s_cst = sem("s_cst")
        s_x = [sem("s_x0"), sem("s_x1")]
        s_small = sem("s_small")
        s_taps = sem("s_taps")
        s_cbias = sem("s_cbias")
        s_cb = sem("s_cb")
        s_m16 = sem("s_m16")
        s_xT = sem("s_xT")
        s_xhi = sem("s_xhi")
        s_xlo = sem("s_xlo")
        s_conv = sem("s_conv")
        s_h0 = sem("s_h0")
        s_var = sem("s_var")
        s_std = sem("s_std")
        s_xn = sem("s_xn")
        s_xnt = sem("s_xnt")
        s_xnT = sem("s_xnT")
        s_rope = sem("s_rope")
        s_wqk_in = sem("s_wqk_in")
        s_wv = sem("s_wv")
        s_wo = sem("s_wo")
        s_bias = sem("s_bias")
        s_bq = sem("s_bq")
        s_perm = sem("s_perm")
        s_qk = sem("s_qk")
        s_vp = sem("s_vp")
        s_qf = sem("s_qf")
        s_vev = sem("s_vev")
        s_cos = sem("s_cos")
        s_rot = sem("s_rot")
        s_hi = sem("s_hi")
        s_lo = sem("s_lo")
        s_dup = [sem("s_dup0"), sem("s_dup1")]
        s_S = sem("s_S")
        s_mx = sem("s_mx")
        s_P = sem("s_P")
        s_T = sem("s_T")
        s_evD = sem("s_evD")
        s_evA = sem("s_evA")
        s_PV = sem("s_PV")
        s_zn = sem("s_zn")
        s_zt = sem("s_zt")
        s_zT = sem("s_zT")
        s_WO = sem("s_WO")
        s_h1 = sem("s_h1")
        s_out = sem("s_out")
        s_z0 = sem("s_z0"); s_zd = sem("s_zd"); s_w1 = sem("s_w1"); s_w2 = sem("s_w2"); s_rw = sem("s_rw")
        s_lg = sem("s_lg"); s_lgd = sem("s_lgd"); s_lge = sem("s_lge"); s_oh = sem("s_oh"); s_rk = sem("s_rk")
        s_pos = sem("s_pos"); s_sc = sem("s_sc"); s_xs = [sem("s_xs0"), sem("s_xs1")]; s_xst = sem("s_xst")
        s_xsT = sem("s_xsT"); s_hid = sem("s_hid"); s_he = sem("s_he"); s_ht = sem("s_ht"); s_gel = sem("s_gel")
        s_y = sem("s_y"); s_ye = sem("s_ye"); s_ys = [sem("s_ys0"), sem("s_ys1")]; s_g = sem("s_g"); s_h2 = sem("s_h2")
        l_w = sem("l_w"); l_wt = sem("l_wt"); l_wT = sem("l_wT"); l_xt = sem("l_xt"); l_xT = sem("l_xT"); l_xn = sem("l_xn")
        l_A = sem("l_A"); l_Bk = sem("l_Bk"); l_eA = sem("l_eA"); l_eB = sem("l_eB"); l_mA = sem("l_mA"); l_mB = sem("l_mB")
        l_fA = sem("l_fA"); l_fB = sem("l_fB"); l_kz = sem("l_kz"); l_v = sem("l_v"); l_at = sem("l_at"); l_AT = sem("l_AT")
        l_num = sem("l_num"); l_st = sem("l_st"); l_sd = sem("l_sd"); l_o = sem("l_o"); l_ot = sem("l_ot"); l_oT = sem("l_oT")
        l_y = sem("l_y"); l_h3 = sem("l_h3"); l_ini = sem("l_ini")
        g_w = sem("g_w"); g_cw = sem("g_cw"); g_lt = sem("g_lt"); g_lT = sem("g_lT"); g_xc = sem("g_xc"); g_xce = sem("g_xce")
        g_bv = sem("g_bv"); g_bs = sem("g_bs"); g_sc = sem("g_sc"); g_xa = sem("g_xa"); g_cp = sem("g_cp"); g_lg = sem("g_lg")
        g_L = sem("g_L"); g_tk = [sem("g_tk0"), sem("g_tk1")]; g_nm = sem("g_nm"); g_e = sem("g_e"); g_d = sem("g_d"); g_fu = sem("g_fu"); g_ob = sem("g_ob")
        g_xg = sem("g_xg"); g_xt = sem("g_xt"); g_xT = sem("g_xT"); g_in = sem("g_in"); g_h = sem("g_h")

        x_rows = ins["x"].rearrange("b (i p) d v -> b i p (d v)", p=128)
        out_rows = out.rearrange("b (i p) d -> p (b i) d", p=128)
        wq_d = ins["L0_attn_W_Q"].rearrange("(a h) (c p) k -> a p c h k", h=2, p=128)
        wk_d = ins["L0_attn_W_K"].rearrange("(a h) (c p) k -> a p c h k", h=2, p=128)
        wv_d = ins["L0_attn_W_V"].rearrange("(a h) (c p) k -> a p c h k", h=2, p=128)
        wo_d = ins["L0_attn_W_O"].rearrange("(a h) k m -> a (h k) m", h=2)

        QUERY_TILES = (7, 0, 6, 1, 5, 2, 4, 3)
        STEPS = [(b, qt, h) for b in range(B) for qt in QUERY_TILES for h in range(2)]
        PARTS = []
        for b, qt, h in STEPS:
            f, cuts = len(sum(PARTS, [])), ((0, qt + 1) if qt < 4 else (0, (qt + 2) // 2, qt + 1))
            PARTS.append([(f + j, cuts[j], cuts[j + 1]) for j in range(len(cuts) - 1)])
        NP = len(sum(PARTS, []))
        NS = len(STEPS)
        NQK, NV, FIRST_UNIT = 8, 4, 3
        UNIT_AT = {FIRST_UNIT + 2 * m: m for m in range(NQK + NV)}
        OUT_UNITS = (0, 1, 2, 3, 4, 6, 7, 5)

        def over_pairs(eng, body):
            with eng.Fori(0, PAIRS // 2 - 1) as j:
                for par in range(2):
                    body(2 * j + par, par, False)
            body(PAIRS - 2, 0, False)
            body(PAIRS - 1, 1, True)

        def lin_tile(n, u):
            return (n // 2 if isinstance(n, int) else (n - u) // 2) + 8 * u

        def lin_has(n):
            return not isinstance(n, int) or 0 <= n < TILES

        def lin_loop(eng, step):
            step(0, 0)
            with eng.Fori(0, (TILES - 4) // 2) as i:
                step(2 * i + 1, 1)
                step(2 * i + 2, 0)
            for n in range(TILES - 3, TILES + 1):
                step(n, n % 2)

        def gate_has(n):
            return not isinstance(n, int) or 0 <= n < TILES

        def gate_loop(eng, step):
            step(0, 0)
            step(1, 1)
            with eng.Fori(1, TILES // 2 - 1) as i:
                step(2 * i, 0)
                step(2 * i + 1, 1)
            for n in range(TILES - 2, TILES + 2):
                step(n, n % 2)

        def alone(eng):
            eng.sem_inc(s_passed[eng.engine], 1)

        block = ctx.enter_context(nc.Block())

        @block.sync
        def _(sp):
            sp.dma_start(cst[:], ins["consts"]).then_inc(s_cst, 16)
            sp.dma_start(conv_w[:], ins["L0_tok_conv_w"].rearrange("(c p) j -> p c j", p=128)).then_inc(s_small, 16)
            with nc.allow_non_contiguous_dma(reason="small vectors onto partitions"):
                sp.dma_start(conv_b[:], ins["L0_tok_conv_b"].rearrange("(c p) -> p c", p=128)).then_inc(s_small, 16)
                rd = ins["L0_tok_read"]
                sp.dma_start(read[:], bass.AP(rd.tensor, 0, [[0, 32], [1, 4], [1, 1]])).then_inc(s_small, 16)
            with sp.Fori(0, T // 128) as i:
                for u in range(B):
                    sp.wait_ge(s_xT, 2 * i + u + 1)
                    alone(sp)
                    sp.dma_start(x_in[:, u, :], x_rows[u, i, :, :]).then_inc(s_x[u], 16)
            if STAGE >= 1:
                sp.wait_ge(s_h0, TILES)
                sp.dma_start(rope[:], ins["rope"].rearrange("p (s t) -> p s t", s=2)).then_inc(s_rope, 16)
                with nc.allow_non_contiguous_dma(reason="small vectors onto partitions"):
                    for j, name in enumerate(("L0_attn_b_Q", "L0_attn_b_K")):
                        v = ins[name].rearrange("(a h) (f q r) -> h q f r a", h=2, f=2, q=2)
                        for h in range(2):
                            for q in range(2):
                                for f in range(2):
                                    p0 = h * 64 + q * 32 + f * 16
                                    sp.dma_start(b_in[p0:p0 + 16, j, :], v[h, q, f]).then_inc(s_bias, 16)
                    sp.dma_start(b_v[:], ins["L0_attn_b_V"].rearrange("(a h) k -> (h k) a", h=2)).then_inc(s_bias, 16)
                    bo = ins["L0_attn_b_O"]
                    sp.dma_start(b_o[:], bass.AP(bo.tensor, 0, [[0, 128], [1, D]])).then_inc(s_bias, 16)

                def load_proj(hp):
                    sp.wait_ge(s_perm, hp + 1)
                    alone(sp)
                    for h in range(2):
                        sp.dma_start(w_in[:, 0, :, h * 64:(h + 1) * 64], wq_d[hp, :, :, h, :]).then_inc(s_wqk_in, 16)
                        sp.dma_start(w_in[:, 1, :, h * 64:(h + 1) * 64], wk_d[hp, :, :, h, :]).then_inc(s_wqk_in, 16)
                    sp.wait_ge(s_vp, NV * hp + 1)
                    alone(sp)
                    for h in range(2):
                        sp.dma_start(w_v[:, :, h * 64:(h + 1) * 64], wv_d[hp, :, :, h, :]).then_inc(s_wv, 16)

                def spread(hp, par):
                    sp.wait_ge(s_hi, NQK * hp + NQK)
                    alone(sp)
                    sp.wait_ge(s_lo, NQK * hp + NQK + 1)
                    alone(sp)
                    for h in range(2):
                        own, other = slice(64 * h, 64 * h + 64), slice(64 - 64 * h, 128 - 64 * h)
                        sp.dma_start(Q2[own, par, h, :], hi[own, 0, :]).then_inc(s_dup[par], 16)
                        sp.dma_start(Q2[other, par, h, :], lo_q[own, :]).then_inc(s_dup[par], 16)
                        sp.dma_start(K2[own, par, h, :], hi[own, 1, :]).then_inc(s_dup[par], 16)
                        sp.dma_start(K2[other, par, h, :], hi[own, 1, :]).then_inc(s_dup[par], 16)

                load_proj(0)
                spread(0, 0)

                def pair(hp, par, last):
                    sp.wait_ge(s_WO, NV * 2 * hp + 1)
                    alone(sp)
                    sp.dma_start(w_o[:], wo_d[hp, :, :]).then_inc(s_wo, 16)
                    if not last:
                        load_proj(hp + 1)
                        sp.wait_ge(s_S, NS * hp + 1)
                        alone(sp)
                        spread(hp + 1, 1 - par)

                over_pairs(sp, pair)
                sp.wait_ge(s_h1, 8 * PAIRS + 1)
            if STAGE >= 2:
                with nc.allow_non_contiguous_dma(reason="small vectors onto partitions"):
                    sp.dma_start(w_r[:], ins["L0_ffn_Wr"].rearrange("(c p) e -> p c e", p=128)).then_inc(s_rw, 16)
                    br = ins["L0_ffn_br"]
                    sp.dma_start(b_r[:], bass.AP(br.tensor, 0, [[0, 128], [1, EXPERTS]])).then_inc(s_rw, 16)
                    sp.dma_start(b_1[:].rearrange("p (e f) -> p e f", e=EXPERTS), ins["L0_ffn_b1"].rearrange("e (f p) -> p e f", p=128)).then_inc(s_rw, 16)
                sp.dma_start(b_2[:], ins["L0_ffn_b2"].rearrange("(a e) d -> a (e d)", a=1)).then_inc(s_rw, 16)
                for e in range(EXPERTS):
                    sp.dma_start(W1[:, e, :, :], ins["L0_ffn_W1"][e].rearrange("(c p) f -> p c f", p=128)).then_inc(s_w1, 16)
                for e in range(EXPERTS):
                    sp.dma_start(W2[:, e, :, :], ins["L0_ffn_W2"][e].rearrange("(c p) f -> p c f", p=128)).then_inc(s_w2, 16)
                sp.wait_ge(s_sc, 16 * TILES)

                def load_slots(s, u):
                    sp.wait_ge(s_xst, s + 1)
                    alone(sp)
                    sp.dma_start(xs[:, u, :], sorted_x[bass.ts(s, 128), :]).then_inc(s_xs[u], 16)

                def store_slots(s, u):
                    sp.wait_ge(s_ye, s + 1)
                    alone(sp)
                    sp.dma_start(sorted_y[bass.ts(s, 128), :], ys[:, u, :]).then_inc(s_ys[u], 16)

                load_slots(0, 0)
                load_slots(1, 1)
                with sp.Fori(0, SLOT_TILES // 2 - 1) as i:
                    for u in range(2):
                        load_slots(2 * i + u + 2, u)
                        store_slots(2 * i + u, u)
                load_slots(SLOT_TILES - 1, 0)
                store_slots(SLOT_TILES - 3, 0)
                store_slots(SLOT_TILES - 2, 1)
                store_slots(SLOT_TILES - 1, 0)
                sp.wait_ge(s_h2, TILES)
            if STAGE >= 3:
                for j, name in enumerate(("Wk", "Wv", "Wq", "Wo")):
                    sp.dma_start(wl_in[:, j, :, :], ins["L1_attn_" + name].rearrange("(c p) d -> p c d", p=128)).then_inc(l_w, 16)
                sp.wait_ge(l_h3, TILES + 1)
            if STAGE >= 4:
                sp.dma_start(wg[:], ins["L1_ffn_weight"].rearrange("(c p) d -> p c d", p=128)).then_inc(g_w, 16)
                with nc.allow_non_contiguous_dma(reason="small vectors onto partitions"):
                    for j, n in enumerate(("so", "si")):
                        sp.dma_start(cwc[:, j, :], ins[f"L1_ffn_{n}_conv_w"].rearrange("(c g) f -> (g f) c", c=KC)).then_inc(g_w, 16)
                        for m, v in enumerate(("conv_b", "gamma", "beta")):
                            sp.dma_start(gcols[64 * j:64 * j + 64, m:m + 1], ins[f"L1_ffn_{n}_{v}"].rearrange("(g a) -> g a", a=1)).then_inc(g_w, 16)
                        sp.dma_start(lin_in[:, :, 64 * j:64 * j + 64], ins[f"L1_ffn_{n}_lin_w"].rearrange("(c p) g -> p c g", p=128)).then_inc(g_w, 16)
                        lb = ins[f"L1_ffn_{n}_lin_b"]
                        sp.dma_start(lin_b[:, j, :], bass.AP(lb.tensor, 0, [[0, 128], [1, D]])).then_inc(g_w, 16)
                    bg = ins["L1_ffn_bias"]
                    sp.dma_start(bias_g[:], bass.AP(bg.tensor, 0, [[0, 128], [1, D]])).then_inc(g_w, 16)
                flat = out.rearrange("b (i p) d -> (b i) p d", p=128)
                with sp.Fori(0, TILES // 2) as i:
                    for u in range(2):
                        sp.wait_ge(g_h, 2 * i + u + 1)
                        alone(sp)
                        sp.dma_start(flat[bass.ds(2 * i + u, 1), :, :].rearrange("a p d -> p (a d)"), H[:, 2 * i + u, :]).then_inc(s_out, 16)
                sp.wait_ge(s_out, 16 * TILES)
                return
            if STAGE >= 1:
                pass
            else:
                sp.wait_ge(s_h0, TILES)
            sp.dma_start(out_rows, H[:]).then_inc(s_out, 16)
            sp.wait_ge(s_out, 16)

        @block.gpsimd
        def _(pool):
            pool.wait_ge(s_cst, 16)
            nc.gpsimd.memset(eps[:], EPS)
            nc.gpsimd.memset(x_hi[:, :, :, 0:3], 0.0)
            nc.gpsimd.memset(x_lo[:, :, :, 0:3], 0.0)
            nc.gpsimd.tensor_scalar(ident16[:], const("ident"), 1.0, 0.0, ALU.mult, ALU.add)
            nc.gpsimd.tensor_scalar(mask16[:], const("causal_add"), 1.0, 0.0, ALU.mult, ALU.add).then_inc(s_m16, 1)
            if STAGE < 1:
                return
            pool.wait_ge(s_rope, 16)
            pool.wait_ge(s_bias, 16 * 18)
            nc.gpsimd.tensor_scalar(b_in[:, 0, :], b_in[:, 0, :], 1.0 / SCALE, 0.0, ALU.mult, ALU.add).then_inc(s_bq, 1)

            def permute(hp):
                pool.wait_ge(s_wqk_in, 64 * hp + 64)
                pool.wait_ge(s_qk, NQK * hp + 1)
                alone(pool)
                for j, sc in enumerate((1.0 / SCALE, 1.0)):
                    src = w_in[:, j, :, :].rearrange("p c (h f q r) -> p (c h) f q r", h=2, f=2, q=2)
                    dst = w_qk[:, j, :, :].rearrange("p c (h q f r) -> p (c h) q f r", h=2, f=2, q=2)
                    for f in range(2):
                        last = nc.gpsimd.tensor_scalar(dst[:, :, :, f, :], src[:, :, f, :, :], sc, 0.0, ALU.mult, ALU.add)
                pool.drain()
                last.then_inc(s_perm, 1)

            def rotate(hp):
                for m in range(NQK + 1):
                    if m < NQK:
                        pool.wait_ge(s_qf, NQK * hp + m + 1)
                        if not isinstance(hp, int) or NQK * hp + m > 0:
                            pool.wait_ge(s_rot, NQK * hp + m)
                        nc.gpsimd.tensor_tensor(q_cos[:, m % 2, :], qf[:, m % 2, :],
                                                rope[:, 0, (m // 2) % 2 * 512:(m // 2) % 2 * 512 + 512],
                                                ALU.mult).then_inc(s_cos, 1)
                    if m >= 1:
                        k = m - 1
                        pool.wait_ge(s_rot, NQK * hp + k + 2)
                        alone(pool)
                        nc.gpsimd.tensor_scalar(hi[:, k % 2, k // 2 * 512:k // 2 * 512 + 512], q_rot[:, k % 2, :],
                                                1.0, 0.0, ALU.mult, ALU.add).then_inc(s_hi, 1)

            permute(0)
            rotate(0)

            def pair(hp, par, last):
                if not last:
                    permute(hp + 1)
                    pool.wait_ge(s_dup[par], 64 * (hp - par) + 128)
                    rotate(hp + 1)

            over_pairs(pool, pair)
            if STAGE < 2:
                return
            pool.wait_ge(s_h1, 8 * PAIRS + 1)
            nc.gpsimd.memset(xs[:, 0, :], 0.0).then_inc(s_z0, 1)
            pool.wait_ge(s_z0, 1)
            for s in range(SLOT_TILES):
                pool.dma_start(sorted_x[s * 128:(s + 1) * 128, :], xs[:, 0, :]).then_inc(s_zd, 16)
            pool.wait_ge(s_zd, 16 * SLOT_TILES)
            pool.wait_ge(s_pos, 1)
            for t in range(TILES):
                pool.indirect_dma_start(out=sorted_x, out_offset=bass.IndirectOffsetOnAxis(pos[:, t:t + 1], 0),
                                        in_=XN[:, t, :], in_offset=None).then_inc(s_sc, 16)
            pool.wait_ge(s_ys[0], 16 * ((SLOT_TILES + 1) // 2))
            pool.wait_ge(s_ys[1], 16 * (SLOT_TILES // 2))
            for t in range(TILES):
                pool.indirect_dma_start(out=XN[:, t, :], out_offset=None, in_=sorted_y,
                                        in_offset=bass.IndirectOffsetOnAxis(pos[:, t:t + 1], 0)).then_inc(s_g, 16)
            if STAGE < 3:
                return
            pool.wait_ge(s_h2, TILES)
            nc.gpsimd.memset(state[:], 0.0)
            nc.gpsimd.memset(vaug[:, :, :, 16:17], 1.0).then_inc(l_ini, 1)

            def lin_features(n, u):
                pool.wait_ge(l_eA, n + 1)
                alone(pool)
                nc.gpsimd.tensor_scalar(eT[:], eT[:], 1.0, 0.0, ALU.min, ALU.add).then_inc(l_mA, 1)
                pool.wait_ge(l_eB, n + 1)
                alone(pool)
                nc.gpsimd.tensor_scalar(ek[:], ek[:], 1.0, 0.0, ALU.min, ALU.add).then_inc(l_mB, 1)
                pool.wait_ge(l_fA, n + 1)
                alone(pool)
                for par in range(2):
                    last = nc.gpsimd.tensor_scalar(kz[:, u, par, :, :], qkT[:, u, 2:4, :], const("odd_head")[:, par:par + 1], 0.0,
                                                   ALU.mult, ALU.add)
                last.then_inc(l_kz, 1)

            def lin_step(n, u):
                if lin_has(n + 1):
                    lin_features(n + 1, 1 - u)

            lin_features(0, 0)
            lin_loop(pool, lin_step)
            if STAGE < 4:
                return
            pool.wait_ge(g_w, 16 * 14)
            nc.gpsimd.memset(CW[:], 0.0)
            nc.gpsimd.memset(linT[:], 0.0)
            pool.drain()
            for c in range(KC):
                for j in range(2):
                    last = nc.gpsimd.tensor_scalar(CW[:, c, 64 * j + 32 * c:64 * j + 32 * c + 32], const("group4"), cwc[:, j, c:c + 1], 0.0,
                                                   ALU.mult, ALU.add)
            last.then_inc(g_cw, 1)
            pool.wait_ge(g_xa, 1)

            def gate_fixed(n, u):
                if not isinstance(n, int) or n >= 2:
                    pool.wait_ge(g_fu, n)
                    alone(pool)
                nc.gpsimd.tensor_copy(xat[:, u, :], xa[:, bass.ts(n, 128)])
                nc.gpsimd.tensor_copy(xgt[:, u, :, :], xnT[:, :, bass.ts(n, 128)]).then_inc(g_cp, 1)

            def gate_step(n, u):
                if gate_has(n - 1):
                    pool.wait_ge(g_e, n)
                    nc.gpsimd.tensor_tensor(ef[:, 1 - u, :, :], ef[:, 1 - u, :, :], er[:, 1 - u, :, :], ALU.subtract).then_inc(g_d, 1)
                if gate_has(n + 2):
                    gate_fixed(n + 2, u)

            gate_fixed(0, 0)
            gate_fixed(1, 1)
            gate_loop(pool, gate_step)

        @block.scalar
        def _(act):
            def evac_hi(n, u):
                act.wait_ge(s_xT, n + 3)
                act.wait_ge(s_conv, n + 1)
                nc.scalar.activation(x_hi[:, u, :, 3:131], bank(2 * u, 2).rearrange("p (c t) -> p c t", c=8),
                                     ACT.Copy).then_inc(s_xhi, 1)

            act.sem_inc(s_xT, 2)
            act.sem_inc(s_xnT, 2)
            act.sem_inc(s_qk, 1)
            act.sem_inc(s_perm, 1)
            act.sem_inc(s_vp, 1)
            act.sem_inc(s_rot, 1)
            act.sem_inc(s_lo, 1)
            act.sem_inc(s_S, 1)
            act.sem_inc(s_WO, 1)
            act.sem_inc(s_evD, 1)
            act.sem_inc(s_evA, 1)
            act.sem_inc(s_T, 2)
            act.sem_inc(s_PV, 4)
            act.sem_inc(s_zn, 2)
            act.sem_inc(s_zt, 2)
            act.sem_inc(s_h1, 1)
            act.sem_inc(s_xst, 2)
            act.sem_inc(l_num, 2)
            act.sem_inc(l_at, 1)
            act.sem_inc(l_AT, 2)
            act.sem_inc(l_xt, 2)
            act.sem_inc(l_h3, 1)
            act.sem_inc(l_sd, 2)
            act.sem_inc(l_kz, 2)
            act.sem_inc(l_o, 1)
            act.sem_inc(l_ot, 1)
            act.sem_inc(l_y, 1)
            act.sem_inc(s_he, 1)
            act.sem_inc(s_ye, 0) if False else None
            act.sem_inc(g_fu, 1)
            act.sem_inc(g_in, 2)
            act.sem_inc(g_xt, 1)
            act.sem_inc(g_h, 0) if False else None
            act.sem_inc(s_conv, 2)
            act.wait_ge(s_m16, 1)
            act.drain()
            evac_hi(0, 0)
            def tok(i, u, last):
                act.wait_ge(s_conv, 2 * i + u + 3)
                if not (last):
                    nc.scalar.activation(x_hi[:, u, :, 0:3], x_hi[:, u, :, 128:131], ACT.Copy)
                    act.drain()
            with act.Fori(0, T // 128 - 1) as i:
                evac_hi(2 * i + 1, 1)
                tok(i, 0, False)
                evac_hi(2 * i + 2, 0)
                tok(i, 1, False)
            evac_hi(TILES - 1, 1)
            act.wait_ge(s_var, 1)
            nc.scalar.activation(std[:], mv[:, :, 1], ACT.Sqrt, bias=eps[:, 0:1]).then_inc(s_std, 1)
            if STAGE < 1:
                return

            def evac_tiles(k):
              with act.Fori(0, TILES // 2) as i:
                for u in range(2):
                    act.wait_ge(s_xnt, TILES * (k - 1) + 2 * i + u + 1)
                    alone(act)
                    nc.scalar.activation(xnT[:, :, bass.ts(2 * i + u, 128)],
                                         bank(u)[:, 0:256].rearrange("p (c t) -> p c t", c=KC), ACT.Copy).then_inc(s_xnT, 1)
            evac_tiles(1)
            act.wait_ge(s_bq, 1)

            def evac_qk(hp, m, b):
                act.wait_ge(s_qk, NQK * hp + m + 2)
                if not isinstance(hp, int) or NQK * hp + m > 1:
                    act.wait_ge(s_rot, NQK * hp + m)
                    act.wait_ge(s_cos, NQK * hp + m - 1)
                alone(act)
                nc.scalar.activation(qf[:, m % 2, :], bank(b), ACT.Identity,
                                     bias=b_in[:, m % 2, bass.ds(hp, 1)]).then_inc(s_qf, 1)

            def pair(hp, par, last):
                def exps(g):
                    b, qt, h = STEPS[g]
                    w = (qt + 1) * 128
                    act.wait_ge(s_mx, NS * hp + g + 1)
                    act.wait_ge(s_T, NP * hp + (PARTS[g - 2][-1][0] + 1 if g >= 2 else 0) + 2)
                    nc.scalar.activation(P[:, g % 2, 0:w], bank(2 * (g % 2), 2)[:, 0:w], ACT.Exp,
                                         bias=neg_max[:, g % 4:g % 4 + 1],
                                         accum_out=row_sum[:, g % 4:g % 4 + 1]).then_inc(s_P, 1)

                def evac_PT(g):
                    for f, a, e in PARTS[g]:
                        if f % 2 == 1:
                            act.wait_ge(s_T, NP * hp + f + 3)
                            act.wait_ge(s_PV, NP * hp + f + 1)
                            nc.scalar.activation(PT[:, f % 4, 0:(e - a) * 128], bank(5)[:, 0:(e - a) * 128],
                                                 ACT.Copy).then_inc(s_evA, 1)

                def evac_zT(k):
                    act.wait_ge(s_zt, 16 * hp + k + 3)
                    alone(act)
                    if k == 0:
                        act.wait_ge(s_WO, 8 * hp + 1)
                        alone(act)
                    b, qt, _ = STEPS[2 * k]
                    t = (b * 8 + qt) * 128
                    nc.scalar.activation(zT[:, t:t + 128], bank(7)[:, 0:128], ACT.Identity,
                                         bias=b_v[:, bass.ds(hp, 1)]).then_inc(s_zT, 1)

                exps(0)
                exps(1)
                evac_PT(0)
                for g in range(NS):
                    if g + 2 < NS:
                        exps(g + 2)
                    if g + 1 < NS:
                        evac_PT(g + 1)
                    if g % 2 == 0 and g >= 2:
                        evac_zT(g // 2 - 1)
                    if not last and g in UNIT_AT and UNIT_AT[g] < NQK:
                        evac_qk(hp + 1, UNIT_AT[g], 7)
                evac_zT(NS // 2 - 1)

            for m in range(NQK):
                evac_qk(0, m, m % 4)
            over_pairs(act, pair)
            if STAGE < 2:
                return
            act.wait_ge(s_var, 2)
            nc.scalar.activation(std[:], mv[:, :, 1], ACT.Sqrt, bias=eps[:, 0:1]).then_inc(s_std, 1)
            evac_tiles(2)
            act.wait_ge(s_lgd, 1)
            nc.scalar.activation(cand[:], logit[:], ACT.Exp).then_inc(s_lge, 1)

            def gelu(s, u):
                e = act.value_load(expi[0:1, bass.ds(s, 1)], min_val=0, max_val=EXPERTS - 1)
                act.wait_ge(s_ht, s + 1)
                alone(act)
                for f in range(8):
                    last = nc.scalar.activation(gelT[:, f, :], bank(4, 2)[:, f * 128:(f + 1) * 128], ACT.Gelu, bias=b_1[:, bass.ds(8 * e + f, 1)])
                last.then_inc(s_gel, 1)

            act.wait_ge(s_pos, 1)
            act.wait_ge(s_rw, 64)
            with act.Fori(0, SLOT_TILES // 2) as i:
                gelu(2 * i, 0)
                gelu(2 * i + 1, 1)
            gelu(SLOT_TILES - 1, 0)
            if STAGE < 3:
                return
            act.wait_ge(s_var, 3)
            nc.scalar.activation(std[:], mv[:, :, 1], ACT.Sqrt, bias=eps[:, 0:1]).then_inc(s_std, 1)
            for j in range(4):
                act.wait_ge(l_wt, j + 1)
                nc.scalar.activation(wlT[:, :, j, :], bank(j).rearrange("p (c d) -> p c d", c=KC), ACT.Copy).then_inc(l_wT, 1)
            act.wait_ge(l_ini, 1)

            def lin_xT(n, u):
                act.wait_ge(l_xt, n + 3)
                nc.scalar.activation(xT[:, u, :, :], bank(7)[:, 0:256].rearrange("p (c t) -> p c t", c=KC), ACT.Copy).then_inc(l_xT, 1)

            def lin_exp(n, u):
                act.wait_ge(l_A, n + 1)
                nc.scalar.activation(eT[:], bank(0), ACT.Exp).then_inc(l_eA, 1)
                act.wait_ge(l_Bk, n + 1)
                nc.scalar.activation(ek[:], bank(1)[:, 0:256], ACT.Exp)
                nc.scalar.activation(vaug[:, u, :, 0:16], bank(1)[:, 256:512].rearrange("p (h d) -> p h d", h=LHEADS), ACT.Copy).then_inc(l_eB, 1)

            def lin_oT(n):
                act.wait_ge(l_ot, n + 2)
                nc.scalar.activation(oT[:], bank(5)[:, 0:256].rearrange("p (c t) -> p c t", c=KC), ACT.Copy).then_inc(l_oT, 1)

            def lin_step(n, u):
                if lin_has(n + 2):
                    lin_xT(n + 2, u)
                if lin_has(n - 1):
                    lin_oT(n - 1)
                if lin_has(n + 1):
                    lin_exp(n + 1, 1 - u)

            lin_xT(0, 0)
            lin_xT(1, 1)
            lin_exp(0, 0)
            lin_loop(act, lin_step)
            if STAGE < 4:
                return
            act.wait_ge(s_var, 4)
            nc.scalar.activation(std[:], mv[:, :, 1], ACT.Sqrt, bias=eps[:, 0:1]).then_inc(s_std, 1)
            evac_tiles(3)
            act.wait_ge(g_w, 16 * 14)
            act.wait_ge(g_lt, 1)
            act.wait_ge(g_cw, 1)
            for j in range(2):
                rows = slice(64 * j, 64 * j + 64)
                last = nc.scalar.activation(linT[rows, j, :], bank(2)[rows, 0:256], ACT.Copy)
            last.then_inc(g_lT, 1)
            for m in range(4):
                act.wait_ge(g_xc, m + 1)
                nc.scalar.activation(xc[:, m * 512:(m + 1) * 512], bank(4 + m), ACT.Identity, bias=gcols[:, 0:1]).then_inc(g_xce, 1)
            act.wait_ge(g_bv, 1)
            nc.scalar.activation(bstd[:], bmv[:, 1:2], ACT.Sqrt, bias=eps[:, 0:1]).then_inc(g_bs, 1)
            act.wait_ge(g_sc, 1)
            nc.scalar.activation(xa[:], xc[:], ACT.Gelu, bias=bsc[:, 2:3], scale=bsc[:, 1:2]).then_inc(g_xa, 1)

            def gate_step(n, u):
                if gate_has(n - 1):
                    v = 1 - u
                    act.wait_ge(g_nm, n)
                    for j in range(2):
                        nc.scalar.activation(ef[:, v, j, :], L[:, v, j, :], ACT.Exp, bias=nmx[:, v, j:j + 1], accum_out=esum[:, v, j:j + 1])
                        last = nc.scalar.activation(er[:, v, j, :], Lr[:, v, j, :], ACT.Exp, bias=nmx[:, v, j:j + 1])
                    last.then_inc(g_e, 1)
                    act.wait_ge(g_xt, n + 1)
                    nc.scalar.activation(xgT[:, v, :, :], bank(4 + v)[:, 0:256].rearrange("p (c t) -> p c t", c=KC), ACT.Copy).then_inc(g_xT, 1)

            gate_loop(act, gate_step)

        @block.vector
        def _(dve):
            dve.wait_ge(s_cst, 16)
            dve.wait_ge(s_small, 48)
            for c in range(8):
                for j in range(TAPS):
                    nc.vector.tensor_scalar(taps32[:, c, j, :], const("group4"), conv_w[:, c, j:j + 1], read[:, 0:1],
                                            ALU.mult, ALU.mult)
                last = nc.vector.tensor_scalar(bias32[:, c, :], const("group4"), conv_b[:, c:c + 1], read[:, 0:1],
                                               ALU.mult, ALU.mult)
            last.then_inc(s_cbias, 1)
            dve.drain()
            nc.vector.tensor_copy(taps_hi[:], taps32[:])
            dve.drain()
            nc.vector.tensor_tensor(taps_lo[:], taps32[:], taps_hi[:], ALU.subtract).then_inc(s_taps, 1)
            dve.wait_ge(s_cb, 1)
            nc.vector.tensor_copy(conv_bias[:], bank(4)[:, 0:256]).then_inc(s_taps, 1)
            dve.wait_ge(s_m16, 1)

            def evac_lo(n, u):
                dve.wait_ge(s_xhi, n + 1)
                nc.vector.tensor_tensor(x_lo[:, u, :, 3:131], bank(2 * u, 2).rearrange("p (c t) -> p c t", c=8),
                                        x_hi[:, u, :, 3:131], ALU.subtract).then_inc(s_xlo, 1)

            def tok(i, u, last):
                dve.wait_ge(s_conv, 2 * i + u + 3)
                if not last:
                    nc.vector.tensor_copy(x_lo[:, u, :, 0:3], x_lo[:, u, :, 128:131])
                nc.vector.tensor_tensor(H[:, 8 * u + i, :], bank(4 + u)[:, 0:256], conv_bias[:], ALU.add).then_inc(s_h0, 1)
                dve.drain()

            evac_lo(0, 0)
            with dve.Fori(0, T // 128 - 1) as i:
                evac_lo(2 * i + 1, 1)
                tok(i, 0, False)
                evac_lo(2 * i + 2, 0)
                tok(i, 1, False)
            evac_lo(TILES - 1, 1)
            tok(T // 128 - 1, 0, True)
            tok(T // 128 - 1, 1, True)

            def layernorm_stats(k):
                with dve.Fori(0, TILES // 2) as i:
                    for u in range(2):
                        nc.vector.bn_stats(stats[:, bass.ds(2 * i + u, 1), :].rearrange("p a s -> p (a s)"), H[:, 2 * i + u, :])
                dve.drain()
                for t in range(TILES):
                    nc.vector.bn_aggr(mv[:, t, :], stats[:, t, :])
                dve.drain()
                nc.vector.tensor_copy(stats[:, 0, 0:1], eps[:, 0:1]).then_inc(s_var, 1)
                dve.wait_ge(s_std, k)
                nc.vector.reciprocal(rstd[:], std[:])
                dve.drain()

            layernorm_stats(1)
            if STAGE < 1:
                return

            def normalise(k, keep):
                with dve.Fori(0, TILES // 2) as i:
                    for u in range(2):
                        args = (H[:, 2 * i + u, :], mv[:, 2 * i + u, 0:1], rstd[:, bass.ds(2 * i + u, 1)], ALU.subtract, ALU.mult)
                        dve.wait_ge(s_xnT, TILES * (k - 1) + 2 * i + u + 1)
                        nc.vector.tensor_scalar(xn[:, u, :], *args).then_inc(s_xn, 1)
                        if keep:
                            nc.vector.tensor_scalar(XN[:, 2 * i + u, :], *args)

            normalise(1, False)

            def swap(hp, m):
                dve.wait_ge(s_qf, NQK * hp + m + 1)
                alone(dve)
                nc.vector.stream_shuffle(q_swap[:], qf[:, m % 2, :], [(r + 16) % 32 for r in range(32)])

            def times_sin(hp, m):
                t0 = (m // 2) % 2 * 512
                nc.vector.tensor_tensor(q_sin[:], q_swap[:], rope[:, 1, t0:t0 + 512], ALU.mult)

            def add_cos(hp, m):
                dve.wait_ge(s_cos, NQK * hp + m + 1)
                if m >= 2:
                    dve.wait_ge(s_hi, NQK * hp + m - 1)
                nc.vector.tensor_tensor(q_rot[:, m % 2, :], q_sin[:], q_cos[:, m % 2, :], ALU.add).then_inc(s_rot, 1)

            def low(hp, m, par):
                dve.wait_ge(s_hi, NQK * hp + m + 1)
                dst = lo_q[:] if m % 2 == 0 else lo_k[:, par, :]
                nc.vector.tensor_tensor(dst[:, m // 2 * 512:m // 2 * 512 + 512], q_rot[:, m % 2, :],
                                        hi[:, m % 2, m // 2 * 512:m // 2 * 512 + 512], ALU.subtract).then_inc(s_lo, 1)

            def evac_v(hp, par, m, b):
                dve.wait_ge(s_vp, NV * hp + m + 2)
                nc.vector.tensor_copy(V[:, par, 4 * m:4 * m + 4, :], bank(b).rearrange("p (t d) -> p t d", t=4)).then_inc(s_vev, 1)

            for m in range(NQK + 1):
                if m < NQK:
                    swap(0, m)
                    dve.drain()
                    times_sin(0, m)
                    dve.drain()
                    add_cos(0, m)
                if m >= 1:
                    low(0, m - 1, 0)
            for m in range(NV):
                evac_v(0, 0, m, m % 4)
            nc.vector.tensor_tensor(H[:], H[:], b_o[:].unsqueeze(1).to_broadcast([128, TILES, D]), ALU.add)
            dve.drain()

            def maximum(hp, g):
                b, qt, h = STEPS[g]
                w = (qt + 1) * 128
                dve.wait_ge(s_S, NS * hp + g + 2)
                nc.vector.tensor_reduce(neg_max[:, g % 4:g % 4 + 1], bank(2 * (g % 2), 2)[:, 0:w], AX.X, ALU.max,
                                        negate=True).then_inc(s_mx, 1)

            maximum(0, 0)
            maximum(0, 1)

            def pair(hp, par, last):
                def evac_PT(g):
                    for f, a, e in PARTS[g]:
                        if f % 2 == 0:
                            dve.wait_ge(s_T, NP * hp + f + 3)
                            dve.wait_ge(s_PV, NP * hp + f + 1)
                            nc.vector.tensor_copy(PT[:, f % 4, 0:(e - a) * 128], bank(4)[:, 0:(e - a) * 128]).then_inc(s_evD, 1)

                evac_PT(0)
                maximum(hp, 2)
                for g in range(NS):
                    b, qt, h = STEPS[g]
                    k = g // 2
                    m = (g - 1 - FIRST_UNIT) // 2
                    turning = not last and 0 <= m < NQK
                    if g + 1 < NS:
                        evac_PT(g + 1)
                    dve.wait_ge(s_P, NS * hp + g + 1)
                    nc.vector.reciprocal(inv_sum[:, g % 4:g % 4 + 1], row_sum[:, g % 4:g % 4 + 1])
                    if turning and g % 2 == 0:
                        swap(hp + 1, m)
                    dve.drain()
                    dve.wait_ge(s_PV, NP * hp + PARTS[g][-1][0] + 1 + 4)
                    if h == 0:
                        dve.wait_ge(s_zt, 16 * hp + k + 1)
                    nc.vector.tensor_scalar(z[:, k % 2, 64 * h:64 * h + 64], bank(6)[:, 64 * h:64 * h + 64],
                                            inv_sum[:, g % 4:g % 4 + 1], None, ALU.mult).then_inc(s_zn, 1)
                    if g + 3 < NS:
                        maximum(hp, g + 3)
                    if turning and g % 2 == 0:
                        times_sin(hp + 1, m)
                    if turning and g % 2 == 1:
                        add_cos(hp + 1, m)
                    if not last and g % 2 == 0 and 1 <= m <= NQK:
                        if m == 1:
                            dve.wait_ge(s_dup[par], 64 * (hp - par) + 128)
                        low(hp + 1, m - 1, 1 - par)
                    if not last and NQK <= UNIT_AT.get(g, 0):
                        evac_v(hp + 1, 1 - par, UNIT_AT[g] - NQK, 7)
                if not last:
                    maximum(hp + 1, 0)
                    maximum(hp + 1, 1)
                for n, k in enumerate(OUT_UNITS):
                    dve.wait_ge(s_WO, 8 * hp + n + 2)
                    hh = H[:, 2 * k:2 * k + 2, :]
                    nc.vector.tensor_tensor(hh, bank(4 + n % 2).rearrange("p (t d) -> p t d", t=2), hh, ALU.add).then_inc(s_h1, 1)
                dve.drain()

            over_pairs(dve, pair)
            if STAGE < 2:
                return
            layernorm_stats(2)
            normalise(2, True)
            dve.drain()
            dve.wait_ge(s_lg, 1)
            dve.wait_ge(s_rw, 64)
            flat = lambda a: a[:].rearrange("p t e -> p (t e)")
            over_e = lambda a: a.unsqueeze(2).to_broadcast([128, TILES, EXPERTS])
            nc.vector.tensor_tensor(logit[:], bank(2)[:, 0:128].rearrange("p (t e) -> p t e", e=EXPERTS),
                                    b_r[:].unsqueeze(1).to_broadcast([128, TILES, EXPERTS]), ALU.add)
            dve.drain()
            nc.vector.tensor_reduce(top[:], logit[:], AX.X, ALU.max)
            dve.drain()
            nc.vector.tensor_tensor(logit[:], logit[:], over_e(top[:]), ALU.subtract).then_inc(s_lgd, 1)
            dve.drain()
            nc.vector.tensor_scalar(flat(pick), flat(logit), 0.0, None, ALU.is_equal)
            dve.wait_ge(s_lge, 1)
            nc.vector.tensor_reduce(posf[:], cand[:], AX.X, ALU.add)
            dve.drain()
            nc.vector.reciprocal(gate[:], posf[:])
            nc.vector.scalar_tensor_tensor(flat(cand), flat(pick), -float(EXPERTS), const("expert_plus"), ALU.mult, ALU.add)
            dve.drain()
            nc.vector.tensor_reduce(top[:], cand[:], AX.X, ALU.min)
            dve.drain()
            nc.vector.tensor_tensor(pick[:], const("expert").rearrange("p (t e) -> p t e", e=EXPERTS), over_e(top[:]), ALU.is_equal).then_inc(s_oh, 1)
            dve.wait_ge(s_rk, 1)
            nc.vector.tensor_copy(flat(tot), bank(4)[:, 0:128])
            nc.vector.tensor_copy(scan[:, 0, :, :].rearrange("p t e -> p (t e)"), bank(4)[:, 0:128])
            dve.drain()
            a, sh = 0, 1
            while sh < TILES:
                nc.vector.tensor_copy(scan[:, 1 - a, 0:sh, :], scan[:, a, 0:sh, :])
                nc.vector.tensor_tensor(scan[:, 1 - a, sh:TILES, :], scan[:, a, sh:TILES, :], scan[:, a, 0:TILES - sh, :], ALU.add)
                dve.drain()
                a, sh = 1 - a, 2 * sh
            count = scan[:, a, TILES - 1, :]
            nc.vector.tensor_tensor(more[:], count.unsqueeze(2).to_broadcast([128, EXPERTS, TILES]),
                                    const("k128").rearrange("p (e k) -> p e k", e=EXPERTS), ALU.is_gt)
            dve.drain()
            nc.vector.tensor_reduce(ntile[:], more[:], AX.X, ALU.add)
            dve.drain()
            nc.vector.tensor_copy(cum[:, 0, :], ntile[:])
            dve.drain()
            c, sh = 0, 1
            while sh < EXPERTS:
                nc.vector.tensor_copy(cum[:, 1 - c, 0:sh], cum[:, c, 0:sh])
                nc.vector.tensor_tensor(cum[:, 1 - c, sh:EXPERTS], cum[:, c, sh:EXPERTS], cum[:, c, 0:EXPERTS - sh], ALU.add)
                dve.drain()
                c, sh = 1 - c, 2 * sh
            nc.vector.tensor_tensor(start[:], cum[:, c, :], ntile[:], ALU.subtract)
            nc.vector.tensor_tensor(past[:], cum[:, c, :].unsqueeze(1).to_broadcast([128, SLOT_TILES, EXPERTS]),
                                    const("slot_tile").rearrange("p (s e) -> p s e", e=EXPERTS), ALU.is_le)
            nc.vector.tensor_tensor(cand[:], scan[:, a, :, :], tot[:], ALU.subtract)
            dve.drain()
            nc.vector.tensor_scalar(start[:], start[:], 128.0, None, ALU.mult)
            nc.vector.tensor_reduce(expf[:], past[:], AX.X, ALU.add)
            nc.vector.tensor_tensor(flat(cand), bank(3)[:, 0:128], flat(cand), ALU.add)
            dve.drain()
            nc.vector.tensor_scalar(expi[:], expf[:], float(EXPERTS - 1), None, ALU.min)
            nc.vector.tensor_tensor(cand[:], cand[:], start[:].unsqueeze(1).to_broadcast([128, TILES, EXPERTS]), ALU.add)
            dve.drain()
            nc.vector.tensor_tensor(cand[:], cand[:], pick[:], ALU.mult)
            dve.drain()
            nc.vector.tensor_reduce(posf[:], cand[:], AX.X, ALU.add)
            dve.drain()
            nc.vector.tensor_copy(pos[:], posf[:])
            dve.drain()
            dve.sem_inc(s_pos, 1)

            def evac_hid(s, u):
                dve.wait_ge(s_hid, s + 1)
                nc.vector.tensor_copy(hid, bank(2, 2)).then_inc(s_he, 1)

            def evac_y(s, u, i):
                dve.wait_ge(s_y, s + 1)
                if not isinstance(i, int) or i >= 1:
                    dve.wait_ge(s_ys[u], 16 * i)
                nc.vector.tensor_copy(ys[:, u, :], bank(6 + u)[:, 0:256]).then_inc(s_ye, 1)

            def evac_xs(s, u):
                dve.wait_ge(s_xst, s + 3)
                nc.vector.tensor_copy(xsT[:, u, :, :], bank(u)[:, 0:256].rearrange("p (c t) -> p c t", c=KC)).then_inc(s_xsT, 1)

            evac_xs(0, 0)
            evac_hid(0, 0)
            evac_xs(1, 1)
            evac_hid(1, 1)
            evac_xs(2, 0)
            evac_y(0, 0, 0)
            evac_hid(2, 0)
            evac_xs(3, 1)
            evac_y(1, 1, 0)
            with dve.Fori(1, SLOT_TILES // 2 - 1) as i:
                evac_hid(2 * i + 1, 1)
                evac_xs(2 * i + 2, 0)
                evac_y(2 * i, 0, i)
                evac_hid(2 * i + 2, 0)
                evac_xs(2 * i + 3, 1)
                evac_y(2 * i + 1, 1, i)
            evac_hid(SLOT_TILES - 2, 1)
            evac_xs(SLOT_TILES - 1, 0)
            evac_y(SLOT_TILES - 3, 0, SLOT_TILES // 2 - 1)
            evac_hid(SLOT_TILES - 1, 0)
            evac_y(SLOT_TILES - 2, 1, SLOT_TILES // 2 - 1)
            evac_y(SLOT_TILES - 1, 0, SLOT_TILES // 2)
            for t in range(TILES):
                if t == 0:
                    dve.wait_ge(s_g, 16 * TILES)
                last = nc.vector.scalar_tensor_tensor(H[:, t, :], XN[:, t, :], gate[:, t:t + 1], H[:, t, :], ALU.mult, ALU.add)
                last.then_inc(s_h2, 1)
            dve.drain()
            if STAGE < 3:
                return
            layernorm_stats(3)
            dve.wait_ge(l_ini, 1)

            def lin_norm(n, u):
                dve.wait_ge(l_xt, n + 1)
                nc.vector.tensor_scalar(xn[:, u, :], H[:, lin_tile(n, u), :], mv[:, lin_tile(n, u), 0:1],
                                        rstd[:, bass.ds(lin_tile(n, u), 1)], ALU.subtract, ALU.mult).then_inc(l_xn, 1)

            def lin_features(n, u):
                dve.wait_ge(l_mA, n + 1)
                dve.wait_ge(l_kz, n + 1)
                nc.vector.scalar_tensor_tensor(qkT[:, u, :, :].rearrange("p a t -> p (a t)"), bank(0), 0.0, eT[:], ALU.max, ALU.add).then_inc(l_fA, 1)
                dve.wait_ge(l_mB, n + 1)
                nc.vector.scalar_tensor_tensor(ktok[:, u, :], bank(1)[:, 0:256], 0.0, ek[:], ALU.max, ALU.add).then_inc(l_fB, 1)

            def lin_mask(n, r):
                dve.wait_ge(l_at, 4 * n + r + 2)
                nc.vector.tensor_tensor(AT[:].rearrange("p (c x) t -> p c x t", c=KC)[:, :, 2 * r:2 * r + 2, :],
                                        bank(2 + r % 2).rearrange("p (c h t) -> p c h t", c=KC, h=2),
                                        const("causal_mul").unsqueeze(1).unsqueeze(1).to_broadcast([128, KC, 2, 128]),
                                        ALU.mult).then_inc(l_AT, 1)

            def lin_divide(n):
                dve.wait_ge(l_num, n + 3)
                num = bank(6)[:, 0:272].rearrange("p (h x) -> p h x", x=17)
                nc.vector.tensor_scalar(den[:], num[:, :, 16], 1e-8, None, ALU.add)
                dve.drain()
                nc.vector.reciprocal(den[:], den[:])
                dve.drain()
                nc.vector.tensor_tensor(o[:].rearrange("p (h x) -> p h x", x=16), num[:, :, 0:16],
                                        den[:].unsqueeze(2).to_broadcast([128, LHEADS, 16]), ALU.mult).then_inc(l_o, 1)

            def lin_own(n):
                dve.wait_ge(l_st, n + 1)
                nc.vector.tensor_tensor(sdel[:].rearrange("p (c x) -> p c x", c=2), bank(4)[:, 0:272].rearrange("p (c x) -> p c x", c=2),
                                        const("own_head").unsqueeze(1).to_broadcast([128, 2, 136]), ALU.mult)

            def lin_state(u):
                nc.vector.tensor_tensor(state[:, u, :], state[:, u, :], sdel[:], ALU.add).then_inc(l_sd, 1)

            def lin_add(n, u):
                dve.wait_ge(l_y, n + 2)
                hh = H[:, lin_tile(n, u), :]
                nc.vector.tensor_tensor(hh, bank(5)[:, 256:512], hh, ALU.add).then_inc(l_h3, 1)

            def lin_step(n, u):
                if lin_has(n - 1):
                    lin_divide(n - 1)
                if lin_has(n):
                    lin_mask(n, 0)
                    lin_mask(n, 1)
                if lin_has(n - 1):
                    lin_own(n - 1)
                if lin_has(n):
                    lin_mask(n, 2)
                dve.drain()
                if lin_has(n - 1):
                    lin_state(1 - u)
                if lin_has(n):
                    lin_mask(n, 3)
                if lin_has(n + 1):
                    lin_features(n + 1, 1 - u)
                if lin_has(n - 1):
                    lin_add(n - 1, 1 - u)
                if lin_has(n + 3):
                    lin_norm(n + 3, 1 - u)

            lin_norm(0, 0)
            lin_norm(1, 1)
            lin_norm(2, 0)
            lin_features(0, 0)
            lin_loop(dve, lin_step)
            dve.drain()
            if STAGE < 4:
                return
            layernorm_stats(4)
            normalise(3, True)
            dve.drain()
            dve.wait_ge(g_w, 16 * 14)
            nc.vector.tensor_tensor(H[:], H[:], bias_g[:].unsqueeze(1).to_broadcast([128, TILES, D]), ALU.add)
            for m in range(4):
                dve.wait_ge(g_xce, m + 1)
                nc.vector.bn_stats(bst[:, m, :], xc[:, m * 512:(m + 1) * 512])
            dve.drain()
            nc.vector.bn_aggr(bmv[:], bst[:].rearrange("p a b -> p (a b)")).then_inc(g_bv, 1)
            dve.wait_ge(g_bs, 1)
            nc.vector.reciprocal(bsc[:, 0:1], bstd[:])
            dve.drain()
            nc.vector.tensor_tensor(bsc[:, 1:2], bsc[:, 0:1], gcols[:, 1:2], ALU.mult)
            dve.drain()
            nc.vector.tensor_tensor(bsc[:, 0:1], bsc[:, 1:2], bmv[:, 0:1], ALU.mult)
            dve.drain()
            nc.vector.tensor_tensor(bsc[:, 2:3], gcols[:, 2:3], bsc[:, 0:1], ALU.subtract).then_inc(g_sc, 1)

            def gate_top(n, u, r):
                src = L if r == 0 else Lr
                for j in range(2):
                    if r == 0:
                        dve.wait_ge(g_L, n + 1)
                    else:
                        dve.wait_ge(g_tk[j], 8 * n + 2 * r)
                    alone(dve)
                    nc.vector.max(m8[:, u, j, r, :], src[:, u, j, :]).then_inc(g_tk[j], 1)
                for j in range(2):
                    dve.wait_ge(g_tk[j], 8 * n + 2 * r + 1)
                    alone(dve)
                    nc.vector.match_replace(Lr[:, u, j, :], m8[:, u, j, r, :], src[:, u, j, :], NEG).then_inc(g_tk[j], 1)
                if r == 0:
                    nc.vector.tensor_scalar(nmx[:, u, :], m8[:, u, :, 0, 0], -1.0, None, ALU.mult)

            def gate_step(n, u):
                v = 1 - u
                if gate_has(n):
                    dve.wait_ge(g_lg, n + 1)
                    nc.vector.tensor_tensor(L[:, u, :, :], bank(u).rearrange("p (j d) -> p j d", j=2), lin_b[:], ALU.add).then_inc(g_L, 1)
                if gate_has(n - 2):
                    dve.wait_ge(g_in, n + 1)
                    nc.vector.tensor_tensor(H[:, n - 2, :], bank(6 + u)[:, 0:256], H[:, n - 2, :], ALU.add).then_inc(g_h, 1)
                if gate_has(n):
                    gate_top(n, u, 0)
                    gate_top(n, u, 1)
                if gate_has(n - 1):
                    dve.wait_ge(g_e, n)
                    nc.vector.reciprocal(einv[:, v, :], esum[:, v, :])
                    dve.drain()
                    dve.wait_ge(g_d, n)
                    nc.vector.scalar_tensor_tensor(xg[:, v, :], ef[:, v, 1, :], einv[:, v, 1:2], XN[:, n - 1, :], ALU.mult, ALU.mult).then_inc(g_xg, 1)
                    dve.wait_ge(g_fu, n + 1)
                    nc.vector.scalar_tensor_tensor(ob[:, v, :], ef[:, v, 0, :], einv[:, v, 0:1], bank(2 + v)[:, 0:256], ALU.mult, ALU.mult).then_inc(g_ob, 1)
                if gate_has(n):
                    gate_top(n, u, 2)
                    gate_top(n, u, 3)
                dve.drain()
                if gate_has(n):
                    dve.sem_inc(g_nm, 1)
                if gate_has(n - 1):
                    nc.vector.tensor_tensor(H[:, n - 1, :], H[:, n - 1, :], ob[:, v, :], ALU.add)
                    dve.drain()

            gate_loop(dve, gate_step)

        @block.tensor
        def _(pe):
            pe.wait_ge(s_cst, 16)
            pe.wait_ge(s_cbias, 1)
            for c in range(8):
                last = nc.tensor.matmul(bank(4)[:, 32 * c:32 * c + 32], const("ones"), bias32[:, c, :], start=True, stop=True)
            last.then_inc(s_cb, 1)
            pe.wait_ge(s_taps, 2)

            def transpose_x(n, i, u):
                pe.wait_ge(s_x[u], 16 * i + 16)
                pe.wait_ge(s_xlo, n - 1) if isinstance(n, int) and n >= 2 else (None if isinstance(n, int) else pe.wait_ge(s_xlo, n - 1))
                for c in range(8):
                    last = nc.tensor.transpose(bank(2 * u, 2)[:, c * 128:(c + 1) * 128], x_in[:, u, c * 128:(c + 1) * 128], const("ident"))
                last.then_inc(s_xT, 1)

            def conv(n, u):
                pe.wait_ge(s_xhi, n + 1)
                pe.wait_ge(s_xlo, n + 1)
                if not isinstance(n, int) or n >= 2:
                    pe.wait_ge(s_h0, n - 1)
                first = True
                for c in range(8):
                    for xs, ws in ((x_hi, taps_hi), (x_hi, taps_lo), (x_lo, taps_hi)):
                        for j in range(TAPS):
                            last = nc.tensor.matmul(bank(4 + u)[:, 32 * c:32 * c + 32], xs[:, u, c, j:j + 128], ws[:, c, j, :],
                                                    start=first, stop=True, skip_group_check=True)
                            first = False
                last.then_inc(s_conv, 1)

            transpose_x(0, 0, 0)
            transpose_x(1, 0, 1)
            conv(0, 0)
            transpose_x(2, 1, 0)
            conv(1, 1)
            with pe.Fori(1, T // 128 - 1) as i:
                transpose_x(2 * i + 1, i, 1)
                conv(2 * i, 0)
                transpose_x(2 * i + 2, i + 1, 0)
                conv(2 * i + 1, 1)
            transpose_x(TILES - 1, T // 128 - 1, 1)
            conv(TILES - 2, 0)
            conv(TILES - 1, 1)
            if STAGE < 1:
                return
            pe.wait_ge(s_h0, TILES)

            def transpose_tiles(k):
                with pe.Fori(0, TILES // 2) as i:
                    for u in range(2):
                        pe.wait_ge(s_xn, TILES * (k - 1) + 2 * i + u + 1)
                        for c in range(KC):
                            last = nc.tensor.transpose(bank(u)[:, c * 128:(c + 1) * 128], xn[:, u, c * 128:(c + 1) * 128], const("ident"))
                        last.then_inc(s_xnt, 1)
            transpose_tiles(1)

            def project_qk(hp, m, b):
                for c in range(KC):
                    last = nc.tensor.matmul(bank(b), w_qk[:, m % 2, c, :], xnT[:, c, m // 2 * 512:m // 2 * 512 + 512],
                                            start=(c == 0), stop=(c == KC - 1))
                last.then_inc(s_qk, 1)

            def project_v(hp, m, b):
                for t in range(4):
                    tok = (4 * m + t) * 128
                    for c in range(KC):
                        last = nc.tensor.matmul(bank(b)[:, t * 128:(t + 1) * 128], xnT[:, c, tok:tok + 128], w_v[:, c, :],
                                                start=(c == 0), stop=(c == KC - 1))
                last.then_inc(s_vp, 1)

            pe.wait_ge(s_xnT, TILES + 2)
            pe.wait_ge(s_perm, 2)
            for m in range(NQK):
                if m >= 4:
                    pe.wait_ge(s_qf, m - 3)
                project_qk(0, m, m % 4)
            pe.wait_ge(s_wv, 32)
            for m in range(NV):
                pe.wait_ge(s_qf, m + 5)
                project_v(0, m, m % 4)
            pe.wait_ge(s_vev, NV)

            def scores(hp, par, g):
                b, qt, h = STEPS[g]
                q0, w = b * T + qt * 128, (qt + 1) * 128
                own = slice(64 * h, 64 * h + 64)
                if g == 0:
                    pe.wait_ge(s_dup[par], 64 * (hp - par) + 128)
                    pe.wait_ge(s_lo, NQK * hp + NQK + 1)
                if g >= 2:
                    pe.wait_ge(s_P, NS * hp + g - 1)
                for a in range(0, w, 512):
                    e = min(a + 512, w)
                    dst = bank(2 * (g % 2), 2)[:, a:e]
                    nc.tensor.matmul(dst, Q2[:, par, h, q0:q0 + 128], K2[:, par, h, b * T + a:b * T + e], start=True, stop=False)
                    last = nc.tensor.matmul(dst, Q2[own, par, h, q0:q0 + 128], lo_k[own, par, b * T + a:b * T + e],
                                            start=False, stop=True)
                    if e == w:
                        last = nc.tensor.matmul(bank(2 * (g % 2), 2)[:, w - 128:w], ident16[:], mask16[:], start=False, stop=True,
                                                skip_group_check=True)
                last.then_inc(s_S, 1)

            scores(0, 0, 0)
            scores(0, 0, 1)

            def pair(hp, par, last_pair):
                def transpose_P(part, g):
                    f, a, e = part
                    pe.wait_ge(s_evD if f % 2 == 0 else s_evA, NP // 2 * hp + f // 2 + 1)
                    for j in range(a, e):
                        last = nc.tensor.transpose(bank(4 + f % 2)[:, (j - a) * 128:(j - a + 1) * 128],
                                                   P[:, g % 2, j * 128:(j + 1) * 128], const("ident"))
                    last.then_inc(s_T, 1)

                def times_V(part, g):
                    b, qt, h = STEPS[g]
                    f, a, e = part
                    pe.wait_ge(s_evD if f % 2 == 0 else s_evA, NP // 2 * hp + f // 2 + 2)
                    for j in range(a, e):
                        last = nc.tensor.matmul(bank(6)[:, 64 * h:64 * h + 64], PT[:, f % 4, (j - a) * 128:(j - a + 1) * 128],
                                                V[:, par, b * 8 + j, 64 * h:64 * h + 64], start=(j == 0), stop=(j == qt))
                    last.then_inc(s_PV, 1)

                def transpose_z(k, units):
                    pe.wait_ge(s_zn, NS * hp + 2 * k + 4)
                    pe.wait_ge(s_zT, 16 * hp + k) if k else None
                    if 0 < units <= NQK:
                        pe.wait_ge(s_qf, NQK * hp + NQK + units)
                    elif units:
                        pe.wait_ge(s_vev, NV * hp + NV + units - NQK)
                    nc.tensor.transpose(bank(7)[:, 0:128], z[:, k % 2, :], const("ident")).then_inc(s_zt, 1)

                def unit(m, k):
                    if m == 0:
                        pe.wait_ge(s_perm, hp + 3)
                    if m == NQK:
                        pe.wait_ge(s_wv, 32 * hp + 64)
                    pe.wait_ge(s_zT, 16 * hp + k + 1)
                    if m < NQK:
                        project_qk(hp + 1, m, 7)
                    else:
                        project_v(hp + 1, m - NQK, 7)

                pe.wait_ge(s_P, NS * hp + 1)
                for part in PARTS[0]:
                    transpose_P(part, 0)
                scores(hp, par, 2)
                for g in range(NS):
                    ahead = PARTS[g + 1] if g + 1 < NS else []
                    for n in range(2):
                        if n < len(ahead):
                            if n == 0:
                                pe.wait_ge(s_P, NS * hp + g + 2)
                            transpose_P(ahead[n], g + 1)
                        if n < len(PARTS[g]):
                            if n == 0:
                                pe.wait_ge(s_zn, NS * hp + g + 2)
                            times_V(PARTS[g][n], g)
                    if g + 3 < NS:
                        scores(hp, par, g + 3)
                    if g % 2 == 0 and g >= 2:
                        units = 0 if last_pair else sum(1 for at in UNIT_AT if at < g)
                        transpose_z(g // 2 - 1, units)
                    if not last_pair and g in UNIT_AT:
                        unit(UNIT_AT[g], (g - 1) // 2 - 1)
                if not last_pair:
                    pe.wait_ge(s_vev, NV * hp + 2 * NV)
                    scores(hp + 1, 1 - par, 0)
                    scores(hp + 1, 1 - par, 1)
                transpose_z(NS // 2 - 1, 0)
                pe.wait_ge(s_wo, 16 * hp + 16)
                for n, k in enumerate(OUT_UNITS):
                    pe.wait_ge(s_zT, 16 * hp + (15 if n < 7 else 16))
                    if n >= 2:
                        pe.wait_ge(s_h1, 8 * hp + n)
                    for t in range(2):
                        last = nc.tensor.matmul(bank(4 + n % 2)[:, t * 256:(t + 1) * 256], zT[:, (2 * k + t) * 128:(2 * k + t + 1) * 128],
                                                w_o[:], start=True, stop=True)
                    last.then_inc(s_WO, 1)
                pe.wait_ge(s_h1, 8 * hp + 9)

            over_pairs(pe, pair)
            if STAGE < 2:
                return
            transpose_tiles(2)
            pe.wait_ge(s_xnT, 2 * TILES + 2)
            pe.wait_ge(s_rw, 64)
            for t in range(TILES):
                for c in range(KC):
                    last = nc.tensor.matmul(bank(2)[:, t * 8:(t + 1) * 8], xnT[:, c, t * 128:(t + 1) * 128], w_r[:, c, :],
                                            start=(c == 0), stop=(c == KC - 1))
            last.then_inc(s_lg, 1)
            pe.wait_ge(s_oh, 1)
            nc.tensor.matmul(bank(3)[:, 0:128], const("before"), pick[:].rearrange("p t e -> p (t e)"), start=True, stop=True)
            nc.tensor.matmul(bank(4)[:, 0:128], const("ones"), pick[:].rearrange("p t e -> p (t e)"), start=True, stop=True).then_inc(s_rk, 1)
            pe.wait_ge(s_pos, 1)

            def tr_xs(s, u, i):
                pe.wait_ge(s_xs[u], 16 * i + 16)
                for c in range(KC):
                    last = nc.tensor.transpose(bank(u)[:, c * 128:(c + 1) * 128], xs[:, u, c * 128:(c + 1) * 128], const("ident"))
                last.then_inc(s_xst, 1)

            def up(s, u):
                e = pe.value_load(expi[0:1, bass.ds(s, 1)], min_val=0, max_val=EXPERTS - 1)
                pe.wait_ge(s_xsT, s + 1)
                pe.wait_ge(s_he, s + 1)
                for a in range(2):
                    for c in range(KC):
                        last = nc.tensor.matmul(bank(2 + a), xsT[:, u, c, :], W1[:, bass.ds(e, 1), c, a * 512:(a + 1) * 512].rearrange("p a f -> p (a f)"),
                                                start=(c == 0), stop=(c == KC - 1))
                last.then_inc(s_hid, 1)

            def tr_hid(s, u):
                pe.wait_ge(s_he, s + 2)
                if not isinstance(s, int) or s >= 1:
                    pe.wait_ge(s_gel, s)
                for f in range(8):
                    last = nc.tensor.transpose(bank(4, 2)[:, f * 128:(f + 1) * 128], hid[:, f * 128:(f + 1) * 128], const("ident"))
                last.then_inc(s_ht, 1)

            def down(s, u):
                e = pe.value_load(expi[0:1, bass.ds(s, 1)], min_val=0, max_val=EXPERTS - 1)
                pe.wait_ge(s_gel, s + 1)
                if not isinstance(s, int) or s >= 2:
                    pe.wait_ge(s_ye, s - 1)
                for f in range(8):
                    nc.tensor.matmul(bank(6 + u)[:, 0:256], gelT[:, f, :], W2[:, bass.ds(e, 1), f, :].rearrange("p a f -> p (a f)"), start=(f == 0), stop=False)
                nc.tensor.matmul(bank(6 + u)[:, 0:256], const("ones")[0:1, :], b_2[0:1, bass.ds(e * D, D)], start=False, stop=True).then_inc(s_y, 1)

            pe.wait_ge(s_w1, 128)
            tr_xs(0, 0, 0)
            up(0, 0)
            pe.wait_ge(s_w2, 128)

            def slot(s, u, i, iu):
                tr_hid(s, u)
                up(s + 1, 1 - u)
                if i is not None:
                    tr_xs(s + 2, u, i)
                down(s, u)

            tr_xs(1, 1, 0)
            slot(0, 0, 1, 0)
            slot(1, 1, 1, 0)
            with pe.Fori(1, SLOT_TILES // 2 - 1) as i:
                slot(2 * i, 0, i + 1, 0)
                slot(2 * i + 1, 1, i + 1, 0)
            slot(SLOT_TILES - 3, 0, SLOT_TILES // 2, 0)
            slot(SLOT_TILES - 2, 1, None, 0)
            tr_hid(SLOT_TILES - 1, 0)
            down(SLOT_TILES - 1, 0)
            if STAGE < 3:
                return
            pe.wait_ge(s_ye, SLOT_TILES)
            pe.wait_ge(l_w, 64)
            for j in range(4):
                for c in range(KC):
                    for oc in range(2):
                        last = nc.tensor.transpose(bank(j)[:, c * 256 + oc * 128:c * 256 + oc * 128 + 128], wl_in[:, j, oc, c * 128:(c + 1) * 128], const("ident"))
                last.then_inc(l_wt, 1)
            pe.wait_ge(l_wT, 4)

            def lin_xt(n, u):
                pe.wait_ge(l_xn, n + 1)
                if not isinstance(n, int) or n >= 1:
                    pe.wait_ge(l_xT, n)
                for c in range(KC):
                    last = nc.tensor.transpose(bank(7)[:, c * 128:(c + 1) * 128], xn[:, u, c * 128:(c + 1) * 128], const("ident"))
                last.then_inc(l_xt, 1)

            def lin_project(n, u):
                pe.wait_ge(l_xT, n + 1)
                if not isinstance(n, int) or n >= 1:
                    pe.wait_ge(l_fA, n)
                    pe.wait_ge(l_fB, n)
                for a in range(4):
                    w = (2, 2, 0, 0)[a]
                    for c in range(KC):
                        last = nc.tensor.matmul(bank(0)[:, a * 128:(a + 1) * 128], wlT[:, c, w, a % 2 * 128:a % 2 * 128 + 128], xT[:, u, c, :],
                                                start=(c == 0), stop=(c == KC - 1))
                last.then_inc(l_A, 1)
                for c in range(KC):
                    last = nc.tensor.matmul(bank(1), xT[:, u, c, :], wlT[:, c, 0:2, :].rearrange("p a d -> p (a d)"),
                                            start=(c == 0), stop=(c == KC - 1))
                last.then_inc(l_Bk, 1)

            def lin_kq(n, u, r):
                pe.wait_ge(l_AT, 4 * n + r + 1)
                rows = slice(32 * r, 32 * r + 32)
                for k in range(4):
                    c, par = k // 2, k % 2
                    last = nc.tensor.matmul(bank(2 + r % 2)[:, k * 128:k * 128 + 128], kz[rows, u, par, c, :], qkT[rows, u, c, :],
                                            start=True, stop=True, tile_position=(32 * r, 0))
                last.then_inc(l_at, 1)

            def lin_num(n, u):
                pe.wait_ge(l_sd, n + 1)
                pe.wait_ge(l_o, n + 1)
                for c in range(KC):
                    nc.tensor.matmul(bank(6)[:, c * 136:(c + 1) * 136], qkT[:, u, c, :], state[:, u, c * 136:(c + 1) * 136], start=(c == 0), stop=True, skip_group_check=True)
                pe.wait_ge(l_AT, 4 * n + 6)
                pe.wait_ge(l_eB, n + 1)
                for h in range(LHEADS):
                    last = nc.tensor.matmul(bank(6)[:, h * 17:(h + 1) * 17], AT[:, h, :], vaug[:, u, h, :], start=False, stop=True, skip_group_check=True)
                last.then_inc(l_num, 1)

            def lin_kv(n, u):
                pe.wait_ge(l_sd, n + 2)
                pe.wait_ge(l_fB, n + 1)
                for c in range(KC):
                    last = nc.tensor.matmul(bank(4)[:, c * 136:(c + 1) * 136], ktok[:, u, c * 128:(c + 1) * 128],
                                            vaug[:, u, 8 * c:8 * c + 8, :].rearrange("p h x -> p (h x)"), start=True, stop=True)
                last.then_inc(l_st, 1)

            def lin_ot(n):
                pe.wait_ge(l_o, n + 2)
                pe.wait_ge(l_h3, n + 1)
                for c in range(KC):
                    last = nc.tensor.transpose(bank(5)[:, c * 128:(c + 1) * 128], o[:, c * 128:(c + 1) * 128], const("ident"))
                last.then_inc(l_ot, 1)

            def lin_out(n):
                pe.wait_ge(l_oT, n + 1)
                for c in range(KC):
                    last = nc.tensor.matmul(bank(5)[:, 256:512], oT[:, c, :], wlT[:, c, 3, :], start=(c == 0), stop=(c == KC - 1))
                last.then_inc(l_y, 1)

            def lin_step(n, u):
                if lin_has(n + 2):
                    lin_xt(n + 2, u)
                if lin_has(n):
                    pe.wait_ge(l_kz, n + 3)
                    lin_kq(n, u, 0)
                    lin_kq(n, u, 1)
                if lin_has(n - 1):
                    lin_ot(n - 1)
                if lin_has(n):
                    lin_kq(n, u, 2)
                    lin_kq(n, u, 3)
                if lin_has(n + 1):
                    lin_project(n + 1, 1 - u)
                if lin_has(n - 1):
                    lin_out(n - 1)
                if lin_has(n):
                    lin_num(n, u)
                    lin_kv(n, u)

            lin_xt(0, 0)
            lin_xt(1, 1)
            lin_project(0, 0)
            lin_loop(pe, lin_step)
            if STAGE < 4:
                return
            pe.wait_ge(l_h3, TILES + 1)
            transpose_tiles(3)
            pe.wait_ge(g_w, 16 * 14)
            for c in range(2):
                last = nc.tensor.transpose(bank(2)[:, c * 128:(c + 1) * 128], lin_in[:, c, :], const("ident"))
            last.then_inc(g_lt, 1)
            pe.wait_ge(g_cw, 1)
            pe.wait_ge(s_xnT, 3 * TILES + 2)
            for m in range(4):
                for c in range(KC):
                    last = nc.tensor.matmul(bank(4 + m), CW[:, c, :], xnT[:, c, m * 512:(m + 1) * 512], start=(c == 0), stop=(c == KC - 1))
                last.then_inc(g_xc, 1)
            pe.wait_ge(g_lT, 1)
            pe.wait_ge(g_xce, 4)

            def gate_logits(n, u):
                pe.wait_ge(g_cp, n + 1)
                if not isinstance(n, int) or n >= 2:
                    pe.wait_ge(g_L, n - 1)
                nc.tensor.matmul(bank(u), xat[:, u, :], linT[:].rearrange("p j d -> p (j d)"), start=True, stop=True).then_inc(g_lg, 1)

            def gate_full(n, u):
                if not isinstance(n, int) or n >= 2:
                    pe.wait_ge(g_ob, n - 1)
                for c in range(KC):
                    last = nc.tensor.matmul(bank(2 + u)[:, 0:256], xgt[:, u, c, :], wg[:, c, :], start=(c == 0), stop=(c == KC - 1))
                last.then_inc(g_fu, 1)

            def gate_step(n, u):
                v = 1 - u
                if gate_has(n + 1):
                    gate_logits(n + 1, v)
                if gate_has(n - 1):
                    pe.wait_ge(g_xg, n)
                    for c in range(KC):
                        last = nc.tensor.transpose(bank(4 + v)[:, c * 128:(c + 1) * 128], xg[:, v, c * 128:(c + 1) * 128], const("ident"))
                    last.then_inc(g_xt, 1)
                if gate_has(n + 1):
                    gate_full(n + 1, v)
                if gate_has(n - 1):
                    pe.wait_ge(g_xT, n)
                    for c in range(KC):
                        last = nc.tensor.matmul(bank(6 + v)[:, 0:256], xgT[:, v, c, :], wg[:, c, :], start=(c == 0), stop=(c == KC - 1))
                    last.then_inc(g_in, 1)

            gate_logits(0, 0)
            gate_full(0, 0)
            gate_loop(pe, gate_step)


NAMES = ['x', 'L0_tok_conv_w', 'L0_tok_conv_b', 'L0_tok_read', 'L0_attn_W_Q', 'L0_attn_b_Q', 'L0_attn_W_K', 'L0_attn_b_K', 'L0_attn_W_V', 'L0_attn_b_V', 'L0_attn_W_O', 'L0_attn_b_O',
         'L0_ffn_W1', 'L0_ffn_b1', 'L0_ffn_W2', 'L0_ffn_b2', 'L0_ffn_Wr', 'L0_ffn_br', 'L1_attn_Wq', 'L1_attn_Wk', 'L1_attn_Wv', 'L1_attn_Wo',
         'L1_ffn_weight', 'L1_ffn_bias', 'L1_ffn_so_conv_w', 'L1_ffn_so_conv_b', 'L1_ffn_so_gamma', 'L1_ffn_so_beta', 'L1_ffn_so_lin_w',
         'L1_ffn_so_lin_b', 'L1_ffn_si_conv_w', 'L1_ffn_si_conv_b', 'L1_ffn_si_gamma', 'L1_ffn_si_beta', 'L1_ffn_si_lin_w', 'L1_ffn_si_lin_b']


def kernel(**inputs):
    import concourse.bacc as _bacc
    from concourse.bass_utils import run_bass_kernel_spmd as _run
    nc = _bacc.Bacc("TRN2", target_bir_lowering=False, num_devices=1)
    packed, where, rope = shape_constants()
    arrays = {n: np.ascontiguousarray(inputs[n]) for n in NAMES}
    arrays["consts"], arrays["rope"] = packed, rope
    arrays = {"in_" + n: a for n, a in arrays.items()}
    ins = {n[3:]: nc.dram_tensor(n, a.shape, mybir.dt.float32, kind="ExternalInput").ap() for n, a in arrays.items()}
    out = nc.dram_tensor("out_0_dram", (B, T, D), mybir.dt.float32, kind="ExternalOutput").ap()
    build(nc, ins, where, out)
    r = _run(nc, [arrays], core_ids=[0])
    return r.results[0]["out_0_dram"]
```

```python
import concourse.bass as bass
from concourse import mybir
from contextlib import ExitStack
import numpy as np


B, T, D, DV, TAPS = 2, 1024, 256, 4, 4
C = D * DV
N = B * T
TILES = N // 128
KC = D // 128
HEADS, DH = 16, 64
PAIRS = HEADS // 2
SCALE = 8.0
NEG = -1.0e30
EPS = 1e-5
EXPERTS, FF = 8, 1024
SLOT_TILES = TILES + EXPERTS - 1
LHEADS = 16
TOPK = 32


def shape_constants():
    p = np.arange(128)
    parts = {}
    parts["ident"] = np.eye(128)
    parts["causal_add"] = np.where(p[None, :] <= p[:, None], 0.0, NEG)
    parts["causal_mul"] = (p[:, None] <= p[None, :]).astype(float)
    parts["before"] = (p[:, None] < p[None, :]).astype(float)
    parts["ones"] = np.ones((128, 128))
    tile_of, expert = np.arange(128) // 8, np.arange(128) % 8
    parts["expert"] = np.broadcast_to(expert, (128, 128))
    parts["expert_plus"] = np.broadcast_to(expert + EXPERTS, (128, 128))
    parts["k128"] = np.broadcast_to(128 * (np.arange(128) % 16), (128, 128))
    parts["slot_tile"] = np.broadcast_to(np.arange(SLOT_TILES * EXPERTS) // EXPERTS, (128, SLOT_TILES * EXPERTS))
    parts["own_head"] = (p[:, None] // 16 == np.arange(136)[None, :] // 17).astype(float)
    parts["group4"] = (p[:, None] // 4 == np.arange(32)[None, :]).astype(float)
    arrays, where, at = [], {}, 0
    for name, a in parts.items():
        where[name] = (at, at + a.shape[1])
        at += a.shape[1]
        arrays.append(a)
    s = p % 64
    dim = (s % 32) // 16 * 32 + s // 32 * 16 + s % 16
    f = np.arange(32, dtype=np.float32)
    freq = (np.float32(10000.0) ** (f / np.float32(32))).astype(np.float32)
    angles = (np.arange(T, dtype=np.float32)[None, :] / freq[dim % 32][:, None]).astype(np.float32)
    sign = np.where(dim < 32, -1.0, 1.0)[:, None]
    rope = np.concatenate([np.cos(angles), sign * np.sin(angles)], axis=1)
    return (np.concatenate(arrays, axis=1).astype(np.float32), where, rope.astype(np.float32))


def build(nc, ins, where, out):
    f32, f16, bf16 = mybir.dt.float32, mybir.dt.float16, mybir.dt.bfloat16
    ALU, ACT, AX = mybir.AluOpType, mybir.ActivationFunctionType, mybir.AxisListType
    ctx = ExitStack()
    with ctx:
        def sem(name):
            return ctx.enter_context(nc.semaphore(name))

        def psum(name, cols):
            return ctx.enter_context(nc.psum_tensor(name, [128, cols], f32))

        banks = psum("banks", 8 * 512)

        def bank(b, n=1):
            return banks[:, b * 512:(b + n) * 512]

        def sb(name, shape, dt=f32, stack=ctx):
            return stack.enter_context(nc.sbuf_tensor(name, shape, dt))

        nconst = ins["consts"].shape[1]
        cst = sb("cst", [128, nconst])

        def const(name):
            a, b = where[name]
            return cst[:, a:b]

        H = sb("H", [128, TILES, D])
        mask16 = sb("mask16", [128, 128], bf16)
        ident16 = sb("ident16", [128, 128], bf16)
        eps = sb("eps", [128, 1])
        stats = sb("stats", [128, TILES, 6])
        mv = sb("mv", [128, TILES, 2])
        std = sb("std", [128, TILES])
        rstd = sb("rstd", [128, TILES])
        xn = sb("xn", [128, 4, D])
        zeros = sb("zeros", [128, D])
        XN = sb("XN", [128, TILES, D])
        xnT = sb("xnT", [128, KC, N])

        with ExitStack() as st:
            x_in = sb("x_in", [128, 2, C], stack=st)
            x_hi = sb("x_hi", [128, 2, 8, 131], f16, st)
            x_lo = sb("x_lo", [128, 2, 8, 131], f16, st)
            conv_w = sb("conv_w", [128, 8, TAPS], stack=st)
            conv_b = sb("conv_b", [128, 8], stack=st)
            read = sb("read", [128, 1], stack=st)
            taps32 = sb("taps32", [128, 8, TAPS, 32], stack=st)
            taps16 = sb("taps16", [128, 8, TAPS, 2, 32], f16, st)
            bias32 = sb("bias32", [128, 8, 32], stack=st)
            conv_bias = sb("conv_bias", [128, D], stack=st)
        with ExitStack() as st:
            rope = sb("rope", [128, 2, T], stack=st)
            w_in = sb("w_in", [128, 2, KC, 128], stack=st)
            w_qk = sb("w_qk", [128, 2, KC, 128], stack=st)
            w_v = sb("w_v", [128, KC, 128], stack=st)
            w_o = sb("w_o", [128, D], stack=st)
            b_in = sb("b_in", [128, 2, PAIRS], stack=st)
            b_v = sb("b_v", [128, PAIRS], stack=st)
            b_o = sb("b_o", [128, D], stack=st)
            qf = sb("qf", [128, 2, 512], stack=st)
            q_swap = sb("q_swap", [128, 2, 512], stack=st)
            q_sin = sb("q_sin", [128, 2, 512], stack=st)
            q_cos = sb("q_cos", [128, 2, 512], stack=st)
            q_rot = sb("q_rot", [128, 2, 512], stack=st)
            hi = sb("hi", [128, 2, N], f16, st)
            lo_q = sb("lo_q", [128, N], f16, st)
            lo_k = sb("lo_k", [128, 2, N], f16, st)
            Q2 = sb("Q2", [128, 2, 2, N], f16, st)
            K2 = sb("K2", [128, 2, 2, N], f16, st)
            V_hi = sb("V_hi", [128, 2, TILES, 128], f16, st)
            V_lo = sb("V_lo", [128, 2, TILES, 128], f16, st)
            neg_max = sb("neg_max", [128, 4], stack=st)
            row_sum = sb("row_sum", [128, 4], stack=st)
            inv_sum = sb("inv_sum", [128, 4], stack=st)
            P = sb("P", [128, 2, T], stack=st)
            PT_hi = sb("PT_hi", [128, 4, 512], f16, st)
            PT_lo = sb("PT_lo", [128, 4, 512], f16, st)
            z = sb("z", [128, 2, 128], stack=st)
            zT = sb("zT", [128, N], stack=st)

        with ExitStack() as st:
            W1_hi = sb("W1_hi", [128, EXPERTS, KC, FF], f16, st)
            W1_lo = sb("W1_lo", [128, EXPERTS, KC, FF], f16, st)
            W2 = sb("W2", [128, EXPERTS, FF // 128, D], stack=st)
            w_r = sb("w_r", [128, KC, EXPERTS], stack=st)
            b_r = sb("b_r", [128, EXPERTS], stack=st)
            b_1 = sb("b_1", [128, EXPERTS * 8], stack=st)
            b_2 = sb("b_2", [1, EXPERTS * D], stack=st)
            logit = sb("logit", [128, TILES, EXPERTS], stack=st)
            top = sb("top", [128, TILES], stack=st)
            pick = sb("pick", [128, TILES, EXPERTS], stack=st)
            cand = sb("cand", [128, TILES, EXPERTS], stack=st)
            gate = sb("gate", [128, TILES], stack=st)
            scan = sb("scan", [128, 2, TILES, EXPERTS], stack=st)
            tot = sb("tot", [128, TILES, EXPERTS], stack=st)
            more = sb("more", [128, EXPERTS, TILES], stack=st)
            ntile = sb("ntile", [128, EXPERTS], stack=st)
            cum = sb("cum", [128, 2, EXPERTS], stack=st)
            start = sb("start", [128, EXPERTS], stack=st)
            past = sb("past", [128, SLOT_TILES, EXPERTS], stack=st)
            posf = sb("posf", [128, TILES], stack=st)
            pos = sb("pos", [128, TILES], mybir.dt.uint32, st)
            expf = sb("expf", [128, SLOT_TILES], stack=st)
            expi = sb("expi", [128, SLOT_TILES], mybir.dt.int32, st)
            xs = sb("xs", [128, 2, D], stack=st)
            xs_hi = sb("xs_hi", [128, 2, KC, 128], f16, st)
            xs_lo = sb("xs_lo", [128, 2, KC, 128], f16, st)
            gelT = xnT[:, :, 0:FF].rearrange("p u (f t) -> p u f t", f=8)
            ys = sb("ys", [128, 2, D], stack=st)
        with ExitStack() as st:
            wl_in = sb("wl_in", [128, 4, 2, D], stack=st)
            wlT = sb("wlT", [128, KC, 4, D], stack=st)
            xT = sb("xT", [128, 2, KC, 128], stack=st)
            eT = sb("eT", [128, 512], stack=st)
            ek = sb("ek", [128, D], stack=st)
            qkT = sb("qkT", [128, 2, 4, 128], stack=st)
            qz = sb("qz", [128, 2, KC, 8, 128], stack=st)
            ktok = sb("ktok", [128, 2, D], stack=st)
            vaug = sb("vaug", [128, 2, LHEADS, 17], stack=st)
            AT = sb("AT", [128, LHEADS, 128], stack=st)
            AT_hi = sb("AT_hi", [128, LHEADS, 128], f16, st)
            AT_lo = sb("AT_lo", [128, LHEADS, 128], f16, st)
            v_hi = sb("v_hi", [128, 2, LHEADS, 17], f16, st)
            v_lo = sb("v_lo", [128, 2, LHEADS, 17], f16, st)
            state = sb("state", [128, B, 272], stack=st)
            sdel = sb("sdel", [128, 272], stack=st)
            den = sb("den", [128, LHEADS], stack=st)
            o = sb("o", [128, D], stack=st)
            oT = sb("oT", [128, KC, 128], stack=st)
            wg = sb("wg", [128, KC, D], stack=st)
            cwc = sb("cwc", [128, 2, KC], stack=st)
            gcols = sb("gcols", [128, 3], stack=st)
            lin_in = sb("lin_in", [128, 2, 128], stack=st)
            linT = sb("linT", [128, 2, D], stack=st)
            lin_b = sb("lin_b", [128, 2, D], stack=st)
            bias_g = sb("bias_g", [1, D], stack=st)
            CW = sb("CW", [128, KC, 128], stack=st)
            xc = sb("xc", [128, N], stack=st)
            xa = sb("xa", [128, N], stack=st)
            bst = sb("bst", [128, 4, 6], stack=st)
            bmv = sb("bmv", [128, 2], stack=st)
            bstd = sb("bstd", [128, 1], stack=st)
            bsc = sb("bsc", [128, 3], stack=st)
            xat = sb("xat", [128, 2, 128], stack=st)
            xgt = sb("xgt", [128, 2, KC, 128], stack=st)
            L = sb("L", [128, 2, 2, D], stack=st)
            Lr = sb("Lr", [128, 2, 2, D], stack=st)
            m8 = sb("m8", [128, 2, 2, 4, 8], stack=st)
            nmx = sb("nmx", [128, 2, 2], stack=st)
            ef = sb("ef", [128, 2, 2, D], stack=st)
            er = sb("er", [128, 2, 2, D], stack=st)
            esum = sb("esum", [128, 2, 2], stack=st)
            einv = sb("einv", [128, 2, 2], stack=st)
            ob = sb("ob", [128, 2, D], stack=st)
            xg = sb("xg", [128, 2, D], stack=st)
            xgT = sb("xgT", [128, 2, KC, 128], stack=st)

        def W1_in(e):
            return W2[:, e, :, :].rearrange("p f d -> p (f d)").rearrange("p (c f) -> p c f", c=KC)

        sorted_x = nc.dram_tensor("sorted_x", (SLOT_TILES * 128, D), f32, kind="Internal").ap()
        sorted_y = nc.dram_tensor("sorted_y", (SLOT_TILES * 128, D), f32, kind="Internal").ap()

        passed = {e.engine: sem("passed_" + n) for n, e in
                    (("sp", nc.sync), ("act", nc.scalar), ("dve", nc.vector), ("pe", nc.tensor), ("pool", nc.gpsimd))}
        consts_in = sem("consts_in")
        x_in_ready = [sem(f"x_in_ready{k}") for k in range(2)]
        taps_in = sem("taps_in")
        taps_ready = sem("taps_ready")
        tap_bias_ready = sem("tap_bias_ready")
        bias_sum_ready = sem("bias_sum_ready")
        fp16_consts_ready = sem("fp16_consts_ready")
        x_transposed = sem("x_transposed")
        x_hi_ready = sem("x_hi_ready")
        x_lo_ready = sem("x_lo_ready")
        conv_done = sem("conv_done")
        h_mixed = sem("h_mixed")
        moments_ready = sem("moments_ready")
        std_ready = sem("std_ready")
        xn_ready = sem("xn_ready")
        xn_transposed = sem("xn_transposed")
        xnT_ready = sem("xnT_ready")
        rope_in = sem("rope_in")
        wqk_in = sem("wqk_in")
        wv_in = sem("wv_in")
        wo_in = sem("wo_in")
        biases_in = sem("biases_in")
        bq_scaled = sem("bq_scaled")
        wqk_permuted = sem("wqk_permuted")
        qk_projected = sem("qk_projected")
        v_projected = sem("v_projected")
        qk_biased = sem("qk_biased")
        v_hi_ready = sem("v_hi_ready")
        v_split = sem("v_split")
        partners_swapped = sem("partners_swapped")
        rope_terms_ready = sem("rope_terms_ready")
        qk_rotated = sem("qk_rotated")
        qk_hi_ready = sem("qk_hi_ready")
        qk_lo_ready = sem("qk_lo_ready")
        operands_stacked = [sem(f"operands_stacked{k}") for k in range(2)]
        scores_ready = sem("scores_ready")
        max_ready = sem("max_ready")
        probs_ready = sem("probs_ready")
        probs_transposed = sem("probs_transposed")
        PT_hi_ready = sem("PT_hi_ready")
        PT_lo_ready = sem("PT_lo_ready")
        PV_done = sem("PV_done")
        inverse_sum_ready = sem("inverse_sum_ready")
        z_divided = sem("z_divided")
        z_transposed = sem("z_transposed")
        zT_ready = sem("zT_ready")
        out_projected = sem("out_projected")
        h_attended = sem("h_attended")
        out_stored = sem("out_stored")
        zeros_ready = sem("zeros_ready")
        zeros_stored = sem("zeros_stored")
        w1_in = [sem(f"w1_in{k}") for k in range(8)]
        w1_hi_ready = sem("w1_hi_ready")
        w1_lo_ready = [sem(f"w1_lo_ready{k}") for k in range(2)]
        w2_in = sem("w2_in")
        router_in = sem("router_in")
        logits_done = sem("logits_done")
        logits_shifted = sem("logits_shifted")
        logits_exp = sem("logits_exp")
        picks_ready = sem("picks_ready")
        ranks_done = sem("ranks_done")
        places_ready = sem("places_ready")
        rows_scattered = sem("rows_scattered")
        slot_in = [sem(f"slot_in{k}") for k in range(2)]
        slot_transposed = sem("slot_transposed")
        slot_split = sem("slot_split")
        hidden_done = sem("hidden_done")
        gelu_done = sem("gelu_done")
        slot_product_done = sem("slot_product_done")
        ys_ready = sem("ys_ready")
        ys_stored = [sem(f"ys_stored{k}") for k in range(2)]
        rows_gathered = [sem(f"rows_gathered{k}") for k in range(4)]
        h_expert_added = sem("h_expert_added")
        lin_weights_in = sem("lin_weights_in")
        lin_weights_transposed = sem("lin_weights_transposed")
        lin_wT_ready = sem("lin_wT_ready")
        lin_xn_ready = sem("lin_xn_ready")
        lin_x_transposed = sem("lin_x_transposed")
        lin_xT_ready = sem("lin_xT_ready")
        lin_qkT_projected = sem("lin_qkT_projected")
        lin_kv_projected = sem("lin_kv_projected")
        lin_expT_ready = sem("lin_expT_ready")
        lin_exp_v_ready = sem("lin_exp_v_ready")
        lin_qkT_ready = sem("lin_qkT_ready")
        lin_k_v_ready = sem("lin_k_v_ready")
        lin_qz_ready = sem("lin_qz_ready")
        lin_kq_done = sem("lin_kq_done")
        lin_kq_masked = sem("lin_kq_masked")
        lin_AT_hi_ready = sem("lin_AT_hi_ready")
        lin_AT_lo_ready = sem("lin_AT_lo_ready")
        lin_sums_done = sem("lin_sums_done")
        lin_kv_done = sem("lin_kv_done")
        lin_state_updated = sem("lin_state_updated")
        lin_o_ready = sem("lin_o_ready")
        lin_o_transposed = sem("lin_o_transposed")
        lin_oT_ready = sem("lin_oT_ready")
        lin_out_done = sem("lin_out_done")
        h_lin_added = sem("h_lin_added")
        late_buffers_set = sem("late_buffers_set")
        gate_weights_in = sem("gate_weights_in")
        gate_conv_ready = sem("gate_conv_ready")
        gate_lin_transposed = sem("gate_lin_transposed")
        gate_lin_ready = sem("gate_lin_ready")
        gate_conv_done = sem("gate_conv_done")
        gate_xc_ready = sem("gate_xc_ready")
        batch_var_ready = sem("batch_var_ready")
        batch_std_ready = sem("batch_std_ready")
        batch_scale_ready = sem("batch_scale_ready")
        gate_xa_ready = sem("gate_xa_ready")
        gate_tile_copied = sem("gate_tile_copied")
        gate_logits_done = sem("gate_logits_done")
        gate_logits_ready = sem("gate_logits_ready")
        gate_top_step = [sem(f"gate_top_step{k}") for k in range(2)]
        gate_top_done = sem("gate_top_done")
        gate_exp_ready = sem("gate_exp_ready")
        gate_kept_ready = sem("gate_kept_ready")
        gate_full_done = sem("gate_full_done")
        gate_out_ready = sem("gate_out_ready")
        gate_xg_ready = sem("gate_xg_ready")
        gate_xg_transposed = sem("gate_xg_transposed")
        gate_xgT_ready = sem("gate_xgT_ready")
        gate_in_done = sem("gate_in_done")
        h_gated = sem("h_gated")

        x_rows = ins["x"].rearrange("b (i p) d v -> b i p (d v)", p=128)
        wq_d = ins["L0_attn_W_Q"].rearrange("(a h) (c p) k -> a p c h k", h=2, p=128)
        wk_d = ins["L0_attn_W_K"].rearrange("(a h) (c p) k -> a p c h k", h=2, p=128)
        wv_d = ins["L0_attn_W_V"].rearrange("(a h) (c p) k -> a p c h k", h=2, p=128)
        wo_d = ins["L0_attn_W_O"].rearrange("(a h) k m -> a (h k) m", h=2)

        QUERY_TILES = (1, 0, 2, 3, 4, 5, 6, 7)
        STEPS = [(b, qt, h) for b in range(B) for qt in QUERY_TILES for h in range(2)]
        PARTS = []
        for b, qt, h in STEPS:
            f, cuts = len(sum(PARTS, [])), ((0, qt + 1) if qt < 4 else (0, (qt + 2) // 2, qt + 1))
            PARTS.append([(f + j, cuts[j], cuts[j + 1]) for j in range(len(cuts) - 1)])
        NP = len(sum(PARTS, []))
        NS = len(STEPS)
        NQK, NV, FIRST_UNIT = 8, 4, 3
        UNIT_AT = {FIRST_UNIT + 2 * m: m for m in range(NQK + NV)}
        OUT_UNITS = (0, 1, 2, 3, 4, 5, 6, 7)

        def over_pairs(eng, body):
            with eng.Fori(0, PAIRS // 2 - 1) as j:
                for par in range(2):
                    body(2 * j + par, par, False)
            body(PAIRS - 2, 0, False)
            body(PAIRS - 1, 1, True)

        def lin_tile(n, u):
            return (n // 2 if isinstance(n, int) else (n - u) // 2) + 8 * u

        def heads(r):
            first = 8 * (r % 2) + 4 * (r // 2)
            return slice(first, first + 4)

        def lin_has(n):
            return not isinstance(n, int) or 0 <= n < TILES

        def lin_loop(eng, step):
            step(0, 0)
            with eng.Fori(0, (TILES - 4) // 2) as i:
                step(2 * i + 1, 1)
                step(2 * i + 2, 0)
            for n in range(TILES - 3, TILES + 1):
                step(n, n % 2)

        def gate_has(n):
            return not isinstance(n, int) or 0 <= n < TILES

        def gate_loop(eng, step):
            step(0, 0)
            step(1, 1)
            with eng.Fori(1, TILES // 2 - 1) as i:
                step(2 * i, 0)
                step(2 * i + 1, 1)
            for n in range(TILES - 2, TILES + 2):
                step(n, n % 2)

        def alone(eng):
            eng.sem_inc(passed[eng.engine], 1)

        block = ctx.enter_context(nc.Block())

        @block.sync
        def _(sp):
            sp.dma_start(conv_w[:], ins["L0_tok_conv_w"].rearrange("(c p) j -> p c j", p=128)).then_inc(taps_in, 16)
            with nc.allow_non_contiguous_dma(reason="small vectors onto partitions"):
                sp.dma_start(conv_b[:], ins["L0_tok_conv_b"].rearrange("(c p) -> p c", p=128)).then_inc(taps_in, 16)
                rd = ins["L0_tok_read"]
                sp.dma_start(read[:], bass.AP(rd.tensor, 0, [[0, 32], [1, 4], [1, 1]])).then_inc(taps_in, 16)
            sp.dma_start(cst[:], ins["consts"]).then_inc(consts_in, 16)
            with sp.Fori(0, T // 128) as i:
                for u in range(B):
                    sp.wait_ge(x_transposed, 2 * i + u + 1)
                    alone(sp)
                    sp.dma_start(x_in[:, u, :], x_rows[u, i, :, :]).then_inc(x_in_ready[u], 16)
            sp.wait_ge(h_mixed, TILES)
            def load_proj(hp):
                sp.wait_ge(wqk_permuted, hp + 1)
                alone(sp)
                for h in range(2):
                    sp.dma_start(w_in[:, 0, :, h * 64:(h + 1) * 64], wq_d[hp, :, :, h, :]).then_inc(wqk_in, 16)
                    sp.dma_start(w_in[:, 1, :, h * 64:(h + 1) * 64], wk_d[hp, :, :, h, :]).then_inc(wqk_in, 16)
                sp.wait_ge(v_projected, NV * hp + 1)
                alone(sp)
                for h in range(2):
                    sp.dma_start(w_v[:, :, h * 64:(h + 1) * 64], wv_d[hp, :, :, h, :]).then_inc(wv_in, 16)

            load_proj(0)
            with nc.allow_non_contiguous_dma(reason="small vectors onto partitions"):
                for j, name in enumerate(("L0_attn_b_Q", "L0_attn_b_K")):
                    v = ins[name].rearrange("(a h) (f q r) -> h q f r a", h=2, f=2, q=2)
                    for h in range(2):
                        for q in range(2):
                            for f in range(2):
                                p0 = h * 64 + q * 32 + f * 16
                                sp.dma_start(b_in[p0:p0 + 16, j, :], v[h, q, f]).then_inc(biases_in, 16)
                sp.dma_start(b_v[:], ins["L0_attn_b_V"].rearrange("(a h) k -> (h k) a", h=2)).then_inc(biases_in, 16)
                bo = ins["L0_attn_b_O"]
                sp.dma_start(b_o[:], bass.AP(bo.tensor, 0, [[0, 128], [1, D]])).then_inc(biases_in, 16)
            sp.dma_start(rope[:], ins["rope"].rearrange("p (s t) -> p s t", s=2)).then_inc(rope_in, 16)

            def spread(hp, par):
                sp.wait_ge(qk_hi_ready, NQK * hp + NQK)
                alone(sp)
                sp.wait_ge(qk_lo_ready, NQK * hp + NQK + 1)
                alone(sp)
                for h in range(2):
                    own, other = slice(64 * h, 64 * h + 64), slice(64 - 64 * h, 128 - 64 * h)
                    sp.dma_start(Q2[own, par, h, :], hi[own, 0, :]).then_inc(operands_stacked[par], 16)
                    sp.dma_start(Q2[other, par, h, :], lo_q[own, :]).then_inc(operands_stacked[par], 16)
                    sp.dma_start(K2[own, par, h, :], hi[own, 1, :]).then_inc(operands_stacked[par], 16)
                    sp.dma_start(K2[other, par, h, :], hi[own, 1, :]).then_inc(operands_stacked[par], 16)

            spread(0, 0)

            def pair(hp, par, last):
                sp.wait_ge(out_projected, NV * 2 * hp + 1)
                alone(sp)
                sp.dma_start(w_o[:], wo_d[hp, :, :]).then_inc(wo_in, 16)
                if not last:
                    load_proj(hp + 1)
                    sp.wait_ge(scores_ready, NS * hp + 1)
                    alone(sp)
                    spread(hp + 1, 1 - par)

            over_pairs(sp, pair)
            sp.wait_ge(h_attended, 8 * PAIRS + 1)
            with nc.allow_non_contiguous_dma(reason="small vectors onto partitions"):
                sp.dma_start(w_r[:], ins["L0_ffn_Wr"].rearrange("(c p) e -> p c e", p=128)).then_inc(router_in, 16)
                br = ins["L0_ffn_br"]
                sp.dma_start(b_r[:], bass.AP(br.tensor, 0, [[0, 128], [1, EXPERTS]])).then_inc(router_in, 16)
                sp.dma_start(b_1[:].rearrange("p (e f) -> p e f", e=EXPERTS), ins["L0_ffn_b1"].rearrange("e (f p) -> p e f", p=128)).then_inc(router_in, 16)
            sp.dma_start(b_2[:], ins["L0_ffn_b2"].rearrange("(a e) d -> a (e d)", a=1)).then_inc(router_in, 16)
            for e in range(EXPERTS):
                sp.dma_start(W1_in(e), ins["L0_ffn_W1"][e].rearrange("(c p) f -> p c f", p=128)).then_inc(w1_in[e], 16)
            for e in range(EXPERTS):
                if e == EXPERTS // 2:
                    sp.wait_ge(places_ready, 1)
                sp.wait_ge(w1_lo_ready[e % 2], e // 2 + 1)
                sp.dma_start(W2[:, e, :, :], ins["L0_ffn_W2"][e].rearrange("(c p) f -> p c f", p=128)).then_inc(w2_in, 16)
            sp.wait_ge(rows_scattered, 16 * TILES)

            def load_slots(s, u):
                sp.wait_ge(slot_transposed, s + 1)
                alone(sp)
                sp.dma_start(xs[:, u, :], sorted_x[bass.ts(s, 128), :]).then_inc(slot_in[u], 16)

            def store_slots(s, u):
                sp.wait_ge(ys_ready, s + 1)
                alone(sp)
                sp.dma_start(sorted_y[bass.ts(s, 128), :], ys[:, u, :]).then_inc(ys_stored[u], 16)

            load_slots(0, 0)
            load_slots(1, 1)
            load_slots(2, 0)
            with sp.Fori(0, SLOT_TILES // 2 - 2) as i:
                for u in range(2):
                    load_slots(2 * i + u + 3, 1 - u)
                    store_slots(2 * i + u, u)
            load_slots(SLOT_TILES - 2, 1)
            store_slots(SLOT_TILES - 5, 0)
            load_slots(SLOT_TILES - 1, 0)
            for n in range(SLOT_TILES - 4, SLOT_TILES):
                store_slots(n, n % 2)
            for j, name in enumerate(("Wk", "Wv", "Wq", "Wo")):
                sp.dma_start(wl_in[:, j, :, :], ins["L1_attn_" + name].rearrange("(c p) d -> p c d", p=128)).then_inc(lin_weights_in, 16)
            sp.dma_start(wg[:], ins["L1_ffn_weight"].rearrange("(c p) d -> p c d", p=128)).then_inc(gate_weights_in, 16)
            with nc.allow_non_contiguous_dma(reason="small vectors onto partitions"):
                for j, n in enumerate(("so", "si")):
                    sp.dma_start(cwc[:, j, :], ins[f"L1_ffn_{n}_conv_w"].rearrange("(c g) f -> (g f) c", c=KC)).then_inc(gate_weights_in, 16)
                    for m, v in enumerate(("conv_b", "gamma", "beta")):
                        sp.dma_start(gcols[64 * j:64 * j + 64, m:m + 1], ins[f"L1_ffn_{n}_{v}"].rearrange("(g a) -> g a", a=1)).then_inc(gate_weights_in, 16)
                    sp.dma_start(lin_in[:, :, 64 * j:64 * j + 64], ins[f"L1_ffn_{n}_lin_w"].rearrange("(c p) g -> p c g", p=128)).then_inc(gate_weights_in, 16)
                    lb = ins[f"L1_ffn_{n}_lin_b"]
                    sp.dma_start(lin_b[:, j, :], bass.AP(lb.tensor, 0, [[0, 128], [1, D]])).then_inc(gate_weights_in, 16)
                bg = ins["L1_ffn_bias"]
                sp.dma_start(bias_g[:], bass.AP(bg.tensor, 0, [[0, 1], [1, D]])).then_inc(gate_weights_in, 16)
            flat = out.rearrange("b (i p) d -> (b i) p d", p=128)
            with sp.Fori(0, TILES // 2) as i:
                for u in range(2):
                    sp.wait_ge(h_gated, 2 * i + u + 1)
                    alone(sp)
                    sp.dma_start(flat[bass.ds(2 * i + u, 1), :, :].rearrange("a p d -> p (a d)"), H[:, 2 * i + u, :]).then_inc(out_stored, 16)
            sp.wait_ge(out_stored, 16 * TILES)

        @block.gpsimd
        def _(pool):
            pool.wait_ge(consts_in, 16)
            nc.gpsimd.memset(eps[:], EPS)
            nc.gpsimd.memset(x_hi[:, :, :, 0:3], 0.0)
            nc.gpsimd.memset(x_lo[:, :, :, 0:3], 0.0)
            nc.gpsimd.tensor_scalar(ident16[:], const("ident"), 1.0, 0.0, ALU.mult, ALU.add)
            nc.gpsimd.tensor_scalar(mask16[:], const("causal_add"), 1.0, 0.0, ALU.mult, ALU.add).then_inc(fp16_consts_ready, 1)
            nc.gpsimd.memset(zeros[:], 0.0).then_inc(zeros_ready, 1)
            pool.wait_ge(zeros_ready, 1)
            for s in range(SLOT_TILES):
                pool.dma_start(sorted_x[s * 128:(s + 1) * 128, :], zeros[:]).then_inc(zeros_stored, 16)
            def permute(hp):
                pool.wait_ge(wqk_in, 64 * hp + 64)
                pool.wait_ge(qk_projected, NQK * hp + 1)
                alone(pool)
                for j, sc in enumerate((1.0 / SCALE, 1.0)):
                    src = w_in[:, j, :, :].rearrange("p c (h f q r) -> p (c h) f q r", h=2, f=2, q=2)
                    dst = w_qk[:, j, :, :].rearrange("p c (h q f r) -> p (c h) q f r", h=2, f=2, q=2)
                    for f in range(2):
                        last = nc.gpsimd.tensor_scalar(dst[:, :, :, f, :], src[:, :, f, :, :], sc, 0.0, ALU.mult, ALU.add)
                pool.drain()
                last.then_inc(wqk_permuted, 1)

            def rotate(hp, par, first=False):
                for m in range(NQK + 1):
                    if m < NQK:
                        t0 = (m // 2) % 2 * 512
                        pool.wait_ge(qk_biased, NQK * hp + m + 1)
                        if not isinstance(hp, int) or NQK * hp + m > 0:
                            pool.wait_ge(qk_rotated, NQK * hp + m)
                        last = nc.gpsimd.tensor_tensor(q_cos[:, m % 2, :], qf[:, m % 2, :], rope[:, 0, t0:t0 + 512], ALU.mult)
                        if not first:
                            pool.wait_ge(partners_swapped, NQK * hp + m + 1)
                            last = nc.gpsimd.tensor_tensor(q_sin[:, m % 2, :], q_swap[:, m % 2, :], rope[:, 1, t0:t0 + 512], ALU.mult)
                        last.then_inc(rope_terms_ready, 1)
                    if m >= 1:
                        k = m - 1
                        part = hi[:, k % 2, k // 2 * 512:k // 2 * 512 + 512]
                        dst = lo_q[:] if k % 2 == 0 else lo_k[:, par, :]
                        pool.wait_ge(qk_rotated, NQK * hp + k + 2)
                        alone(pool)
                        nc.gpsimd.tensor_scalar(part, q_rot[:, k % 2, :], 1.0, 0.0, ALU.mult, ALU.add).then_inc(qk_hi_ready, 1)
                        if first:
                            continue
                        pool.wait_ge(qk_hi_ready, NQK * hp + k + 1)
                        nc.gpsimd.tensor_tensor(dst[:, k // 2 * 512:k // 2 * 512 + 512], q_rot[:, k % 2, :], part, ALU.subtract).then_inc(qk_lo_ready, 1)

            permute(0)
            pool.wait_ge(rope_in, 16)
            pool.wait_ge(biases_in, 16 * 18)
            nc.gpsimd.tensor_scalar(b_in[:, 0, :], b_in[:, 0, :], 1.0 / SCALE, 0.0, ALU.mult, ALU.add).then_inc(bq_scaled, 1)
            rotate(0, 0, True)

            def pair(hp, par, last):
                if not last:
                    permute(hp + 1)
                    pool.wait_ge(operands_stacked[par], 64 * (hp - par) + 128)
                    rotate(hp + 1, 1 - par)

            over_pairs(pool, pair)
            for e in range(0, EXPERTS, 2):
                pool.wait_ge(w1_hi_ready, e + 1)
                nc.gpsimd.tensor_tensor(W1_lo[:, e, :, :], W1_in(e), W1_hi[:, e, :, :], ALU.subtract).then_inc(w1_lo_ready[0], 1)
            pool.wait_ge(zeros_stored, 16 * SLOT_TILES)
            pool.wait_ge(places_ready, 1)
            for t in range(TILES):
                pool.indirect_dma_start(out=sorted_x, out_offset=bass.IndirectOffsetOnAxis(pos[:, t:t + 1], 0),
                                        in_=XN[:, t, :], in_offset=None).then_inc(rows_scattered, 16)
            pool.wait_ge(ys_ready, SLOT_TILES)
            nc.gpsimd.memset(state[:], 0.0)
            nc.gpsimd.memset(vaug[:, :, :, 16:17], 1.0)
            nc.gpsimd.memset(v_hi[:, :, :, 16:17], 1.0)
            nc.gpsimd.memset(v_lo[:, :, :, 16:17], 0.0)
            nc.gpsimd.memset(CW[:], 0.0)
            nc.gpsimd.memset(linT[:], 0.0)
            pool.drain()
            pool.sem_inc(late_buffers_set, 1)
            pool.wait_ge(ys_stored[0], 16 * ((SLOT_TILES + 1) // 2))
            pool.wait_ge(ys_stored[1], 16 * (SLOT_TILES // 2))
            for t in range(TILES):
                pool.indirect_dma_start(out=XN[:, t, :], out_offset=None, in_=sorted_y,
                                        in_offset=bass.IndirectOffsetOnAxis(pos[:, t:t + 1], 0)).then_inc(rows_gathered[t // 4], 16)
            pool.wait_ge(gate_weights_in, 16 * 14)
            for c in range(KC):
                for j in range(2):
                    last = nc.gpsimd.tensor_scalar(CW[:, c, 64 * j + 32 * c:64 * j + 32 * c + 32], const("group4"), cwc[:, j, c:c + 1], 0.0,
                                                   ALU.mult, ALU.add)
            last.then_inc(gate_conv_ready, 1)

            def lin_features(n, u):
                pool.wait_ge(lin_qkT_ready, n + 1)
                alone(pool)
                for j in range(8):
                    last = nc.gpsimd.tensor_scalar(qz[:, u, :, j, :], qkT[:, u, 0:2, :], const("own_head")[:, 17 * j:17 * j + 1], 0.0,
                                                   ALU.mult, ALU.add)
                    if j % 4 == 3:
                        last.then_inc(lin_qz_ready, 1)

            def lin_step(n, u):
                if lin_has(n + 1):
                    lin_features(n + 1, 1 - u)

            lin_features(0, 0)
            lin_loop(pool, lin_step)
            pool.wait_ge(gate_xa_ready, 1)

            def gate_fixed(n, u):
                if not isinstance(n, int) or n >= 2:
                    pool.wait_ge(gate_full_done, n)
                    alone(pool)
                nc.gpsimd.tensor_copy(xat[:, u, :], xa[:, bass.ts(n, 128)])
                nc.gpsimd.tensor_copy(xgt[:, u, :, :], xnT[:, :, bass.ts(n, 128)]).then_inc(gate_tile_copied, 1)

            def gate_step(n, u):
                if gate_has(n - 1):
                    pool.wait_ge(gate_exp_ready, n)
                    nc.gpsimd.tensor_tensor(ef[:, 1 - u, :, :], ef[:, 1 - u, :, :], er[:, 1 - u, :, :], ALU.subtract).then_inc(gate_kept_ready, 1)
                if gate_has(n + 2):
                    gate_fixed(n + 2, u)

            gate_fixed(0, 0)
            gate_fixed(1, 1)
            gate_loop(pool, gate_step)

        @block.scalar
        def _(act):
            def evac_hi(n, u):
                act.wait_ge(x_transposed, n + 3)
                act.wait_ge(conv_done, n + 1)
                nc.scalar.activation(x_hi[:, u, :, 3:131], bank(2 * u, 2).rearrange("p (c t) -> p c t", c=8),
                                     ACT.Copy).then_inc(x_hi_ready, 1)

            act.sem_inc(x_transposed, 2)
            act.sem_inc(xnT_ready, 4)
            act.sem_inc(qk_projected, 1)
            act.sem_inc(wqk_permuted, 1)
            act.sem_inc(v_projected, 1)
            act.sem_inc(qk_rotated, 1)
            act.sem_inc(qk_lo_ready, 1)
            act.sem_inc(scores_ready, 1)
            act.sem_inc(out_projected, 1)
            act.sem_inc(PT_lo_ready, 2)
            act.sem_inc(probs_transposed, 2)
            act.sem_inc(PV_done, 4)
            act.sem_inc(z_divided, 2)
            act.sem_inc(z_transposed, 2)
            act.sem_inc(h_attended, 1)
            act.sem_inc(slot_transposed, 2)
            act.sem_inc(lin_sums_done, 2)
            act.sem_inc(lin_kq_done, 1)
            act.sem_inc(lin_kq_masked, 2)
            act.sem_inc(lin_x_transposed, 2)
            act.sem_inc(h_lin_added, 1)
            act.sem_inc(lin_state_updated, 2)
            act.sem_inc(lin_qz_ready, 4)
            act.sem_inc(lin_o_ready, 1)
            act.sem_inc(lin_o_transposed, 1)
            act.sem_inc(lin_out_done, 1)
            act.sem_inc(slot_product_done, 2)
            act.sem_inc(gelu_done, 2)
            act.sem_inc(gate_full_done, 1)
            act.sem_inc(gate_in_done, 2)
            act.sem_inc(gate_xg_transposed, 1)
            act.sem_inc(conv_done, 2)
            act.wait_ge(fp16_consts_ready, 1)
            act.drain()
            evac_hi(0, 0)

            def tok(i, u, last):
                act.wait_ge(conv_done, 2 * i + u + 3)
                if not last:
                    nc.scalar.activation(x_hi[:, u, :, 0:3], x_hi[:, u, :, 128:131], ACT.Copy)
                    act.drain()

            with act.Fori(0, T // 128 - 1) as i:
                evac_hi(2 * i + 1, 1)
                tok(i, 0, False)
                evac_hi(2 * i + 2, 0)
                tok(i, 1, False)
            evac_hi(TILES - 1, 1)
            act.wait_ge(moments_ready, 1)
            nc.scalar.activation(std[:], mv[:, :, 1], ACT.Sqrt, bias=eps[:, 0:1]).then_inc(std_ready, 1)

            def evac_tiles(k):
                with act.Fori(0, TILES // 4) as i:
                    for u in range(4):
                        act.wait_ge(xn_transposed, TILES * (k - 1) + 4 * i + u + 1)
                        alone(act)
                        nc.scalar.activation(xnT[:, :, bass.ts(4 * i + u, 128)],
                                             bank(u)[:, 0:256].rearrange("p (c t) -> p c t", c=KC), ACT.Copy).then_inc(xnT_ready, 1)
            evac_tiles(1)
            act.wait_ge(bq_scaled, 1)

            def evac_qk(hp, m, b):
                act.wait_ge(qk_projected, NQK * hp + m + 2)
                if not isinstance(hp, int) or NQK * hp + m > 1:
                    act.wait_ge(qk_rotated, NQK * hp + m)
                    act.wait_ge(rope_terms_ready, NQK * hp + m - 1)
                alone(act)
                nc.scalar.activation(qf[:, m % 2, :], bank(b), ACT.Identity,
                                     bias=b_in[:, m % 2, bass.ds(hp, 1)]).then_inc(qk_biased, 1)

            def evac_v(hp, par, m, b):
                act.wait_ge(v_projected, NV * hp + m + 2)
                nc.scalar.activation(V_hi[:, par, 4 * m:4 * m + 4, :], bank(b).rearrange("p (t d) -> p t d", t=4), ACT.Copy).then_inc(v_hi_ready, 1)

            def pair(hp, par, last):
                def exps(g):
                    b, qt, h = STEPS[g]
                    w = (qt + 1) * 128
                    act.wait_ge(max_ready, NS * hp + g + 1)
                    act.wait_ge(probs_transposed, NP * hp + (PARTS[g - 2][-1][0] + 1 if g >= 2 else 0) + 2)
                    nc.scalar.activation(P[:, g % 2, 0:w], bank(2 * (g % 2), 2)[:, 0:w], ACT.Exp,
                                         bias=neg_max[:, g % 4:g % 4 + 1],
                                         accum_out=row_sum[:, g % 4:g % 4 + 1]).then_inc(probs_ready, 1)

                def evac_PT(g):
                    for f, a, e in PARTS[g]:
                        act.wait_ge(probs_transposed, NP * hp + f + 3)
                        act.wait_ge(PV_done, NP * hp + f + 1)
                        nc.scalar.activation(PT_hi[:, f % 4, 0:(e - a) * 128], bank(4 + f % 2)[:, 0:(e - a) * 128],
                                             ACT.Copy).then_inc(PT_hi_ready, 1)

                def divide(g):
                    b, qt, h = STEPS[g]
                    k = g // 2
                    act.wait_ge(inverse_sum_ready, NS * hp + g + 1)
                    act.wait_ge(PV_done, NP * hp + PARTS[g][-1][0] + 1 + 4)
                    if h == 0:
                        act.wait_ge(z_transposed, 16 * hp + k + 1)
                    nc.scalar.activation(z[:, k % 2, 64 * h:64 * h + 64], bank(6)[:, 64 * h:64 * h + 64],
                                         ACT.Identity, scale=inv_sum[:, g % 4:g % 4 + 1]).then_inc(z_divided, 1)

                def evac_zT(k):
                    act.wait_ge(z_transposed, 16 * hp + k + 3)
                    alone(act)
                    if k == 0:
                        act.wait_ge(out_projected, 8 * hp + 1)
                        alone(act)
                    b, qt, _ = STEPS[2 * k]
                    t = (b * 8 + qt) * 128
                    nc.scalar.activation(zT[:, t:t + 128], bank(7)[:, 0:128], ACT.Identity,
                                         bias=b_v[:, bass.ds(hp, 1)]).then_inc(zT_ready, 1)

                exps(0)
                exps(1)
                evac_PT(0)
                for g in range(NS):
                    if g + 1 < NS:
                        evac_PT(g + 1)
                    if g + 2 < NS:
                        exps(g + 2)
                    divide(g)
                    if g % 2 == 0 and g >= 2:
                        evac_zT(g // 2 - 1)
                    if not last and g in UNIT_AT and UNIT_AT[g] < NQK:
                        evac_qk(hp + 1, UNIT_AT[g], 7)
                    if not last and NQK <= UNIT_AT.get(g, 0):
                        evac_v(hp + 1, 1 - par, UNIT_AT[g] - NQK, 7)
                evac_zT(NS // 2 - 1)

            for m in range(NQK):
                evac_qk(0, m, m % 4)
            for m in range(NV):
                evac_v(0, 0, m, m % 4)
            over_pairs(act, pair)
            act.wait_ge(moments_ready, 2)
            nc.scalar.activation(std[:], mv[:, :, 1], ACT.Sqrt, bias=eps[:, 0:1]).then_inc(std_ready, 1)
            evac_tiles(2)

            def w1_high(e):
                act.wait_ge(w1_in[e], 16)
                nc.scalar.activation(W1_hi[:, e, :, :], W1_in(e), ACT.Copy).then_inc(w1_hi_ready, 1)

            for e in range(EXPERTS // 2):
                w1_high(e)
            act.wait_ge(logits_shifted, 1)
            nc.scalar.activation(cand[:], logit[:], ACT.Exp).then_inc(logits_exp, 1)
            for e in range(EXPERTS // 2, EXPERTS):
                w1_high(e)

            def gelu(s, u):
                e = act.value_load(expi[0:1, bass.ds(s, 1)], min_val=0, max_val=EXPERTS - 1)
                act.wait_ge(hidden_done, s + 1)
                alone(act)
                act.wait_ge(slot_product_done, s + 1)
                alone(act)
                for f in range(8):
                    last = nc.scalar.activation(gelT[:, u, f, :], bank(2 + 2 * u, 2)[:, f * 128:(f + 1) * 128], ACT.Gelu, bias=b_1[:, bass.ds(8 * e + f, 1)])
                last.then_inc(gelu_done, 1)

            act.wait_ge(places_ready, 1)
            act.wait_ge(router_in, 64)
            with act.Fori(0, SLOT_TILES // 2) as i:
                gelu(2 * i, 0)
                gelu(2 * i + 1, 1)
            gelu(SLOT_TILES - 1, 0)
            for j in range(4):
                act.wait_ge(lin_weights_transposed, j + 1)
                nc.scalar.activation(wlT[:, :, j, :], bank(j).rearrange("p (c d) -> p c d", c=KC), ACT.Copy).then_inc(lin_wT_ready, 1)
            act.wait_ge(gate_lin_transposed, 1)
            act.wait_ge(late_buffers_set, 1)
            for j in range(2):
                rows = slice(64 * j, 64 * j + 64)
                last = nc.scalar.activation(linT[rows, j, :], bank(4)[rows, 0:256], ACT.Copy)
            last.then_inc(gate_lin_ready, 1)
            act.wait_ge(moments_ready, 3)
            nc.scalar.activation(std[:], mv[:, :, 1], ACT.Sqrt, bias=eps[:, 0:1]).then_inc(std_ready, 1)

            def lin_xT(n, u):
                act.wait_ge(lin_x_transposed, n + 3)
                nc.scalar.activation(xT[:, u, :, :], bank(7)[:, 0:256].rearrange("p (c t) -> p c t", c=KC), ACT.Copy).then_inc(lin_xT_ready, 1)

            def lin_exp(n, u):
                act.wait_ge(lin_qkT_projected, n + 1)
                nc.scalar.activation(eT[:], bank(0), ACT.Exp).then_inc(lin_expT_ready, 1)
                act.wait_ge(lin_kv_projected, n + 1)
                nc.scalar.activation(ek[:], bank(1)[:, 0:256], ACT.Exp)
                nc.scalar.activation(vaug[:, u, :, 0:16], bank(1)[:, 256:512].rearrange("p (h d) -> p h d", h=LHEADS), ACT.Copy)
                nc.scalar.activation(v_hi[:, u, :, 0:16], bank(1)[:, 256:512].rearrange("p (h d) -> p h d", h=LHEADS), ACT.Copy).then_inc(lin_exp_v_ready, 1)

            def lin_high(n, r):
                act.wait_ge(lin_kq_masked, 4 * n + r + 3)
                nc.scalar.activation(AT_hi[:, heads(r), :], AT[:, heads(r), :], ACT.Copy).then_inc(lin_AT_hi_ready, 1)

            def lin_oT(n):
                act.wait_ge(lin_o_transposed, n + 2)
                nc.scalar.activation(oT[:], bank(5)[:, 0:256].rearrange("p (c t) -> p c t", c=KC), ACT.Copy).then_inc(lin_oT_ready, 1)

            def lin_step(n, u):
                if lin_has(n + 2):
                    lin_xT(n + 2, u)
                if lin_has(n - 1):
                    lin_oT(n - 1)
                if lin_has(n):
                    for r in range(4):
                        lin_high(n, r)
                if lin_has(n + 1):
                    lin_exp(n + 1, 1 - u)

            lin_xT(0, 0)
            lin_xT(1, 1)
            lin_exp(0, 0)
            lin_loop(act, lin_step)
            act.wait_ge(moments_ready, 4)
            nc.scalar.activation(std[:], mv[:, :, 1], ACT.Sqrt, bias=eps[:, 0:1]).then_inc(std_ready, 1)
            evac_tiles(3)
            for m in range(4):
                act.wait_ge(gate_conv_done, m + 1)
                nc.scalar.activation(xc[:, m * 512:(m + 1) * 512], bank(4 + m), ACT.Identity, bias=gcols[:, 0:1]).then_inc(gate_xc_ready, 1)
            act.wait_ge(batch_var_ready, 1)
            nc.scalar.activation(bstd[:], bmv[:, 1:2], ACT.Sqrt, bias=eps[:, 0:1]).then_inc(batch_std_ready, 1)
            act.wait_ge(batch_scale_ready, 1)
            nc.scalar.activation(xa[:], xc[:], ACT.Gelu, bias=bsc[:, 2:3], scale=bsc[:, 1:2]).then_inc(gate_xa_ready, 1)

            def gate_step(n, u):
                if gate_has(n - 1):
                    v = 1 - u
                    act.wait_ge(gate_top_done, n)
                    for j in range(2):
                        nc.scalar.activation(ef[:, v, j, :], L[:, v, j, :], ACT.Exp, bias=nmx[:, v, j:j + 1], accum_out=esum[:, v, j:j + 1])
                        last = nc.scalar.activation(er[:, v, j, :], Lr[:, v, j, :], ACT.Exp, bias=nmx[:, v, j:j + 1])
                    last.then_inc(gate_exp_ready, 1)
                    act.wait_ge(gate_xg_transposed, n + 1)
                    nc.scalar.activation(xgT[:, v, :, :], bank(4 + v)[:, 0:256].rearrange("p (c t) -> p c t", c=KC), ACT.Copy).then_inc(gate_xgT_ready, 1)

            gate_loop(act, gate_step)

        @block.vector
        def _(dve):
            dve.wait_ge(consts_in, 16)
            dve.wait_ge(taps_in, 48)
            nc.vector.tensor_scalar(conv_w[:], conv_w[:], read[:, 0:1], None, ALU.mult)
            nc.vector.tensor_scalar(conv_b[:], conv_b[:], read[:, 0:1], None, ALU.mult)
            dve.drain()
            nc.vector.tensor_tensor(bias32[:], const("group4").unsqueeze(1).to_broadcast([128, 8, 32]),
                                    conv_b[:].unsqueeze(2).to_broadcast([128, 8, 32]), ALU.mult).then_inc(tap_bias_ready, 1)
            nc.vector.tensor_tensor(taps32[:].rearrange("p c j g -> p (c j) g"), const("group4").unsqueeze(1).to_broadcast([128, 8 * TAPS, 32]),
                                    conv_w[:].rearrange("p c j -> p (c j)").unsqueeze(2).to_broadcast([128, 8 * TAPS, 32]), ALU.mult)
            dve.drain()
            nc.vector.tensor_copy(taps16[:, :, :, 0, :], taps32[:])
            dve.drain()
            nc.vector.tensor_tensor(taps16[:, :, :, 1, :], taps32[:], taps16[:, :, :, 0, :], ALU.subtract).then_inc(taps_ready, 1)
            dve.wait_ge(bias_sum_ready, 1)
            nc.vector.tensor_copy(conv_bias[:], bank(4)[:, 0:256]).then_inc(taps_ready, 1)
            dve.wait_ge(fp16_consts_ready, 1)

            def row_statistics(t):
                nc.vector.bn_stats(stats[:, bass.ds(t, 1), :].rearrange("p a s -> p (a s)"), H[:, t, :])

            def evac_lo(n, u):
                dve.wait_ge(x_hi_ready, n + 1)
                nc.vector.tensor_tensor(x_lo[:, u, :, 3:131], bank(2 * u, 2).rearrange("p (c t) -> p c t", c=8),
                                        x_hi[:, u, :, 3:131], ALU.subtract).then_inc(x_lo_ready, 1)

            def tok(i, u, last):
                dve.wait_ge(conv_done, 2 * i + u + 3)
                if not last:
                    nc.vector.tensor_copy(x_lo[:, u, :, 0:3], x_lo[:, u, :, 128:131])
                h = H[:, 8 * u + i, :].rearrange("p (c g) -> p c g", c=8)
                product = bank(4 + u).rearrange("p (c k g) -> p c k g", c=8, k=2)
                nc.vector.tensor_tensor(h, product[:, :, 1, :], conv_bias[:].rearrange("p (c g) -> p c g", c=8), ALU.add)
                dve.drain()
                nc.vector.tensor_tensor(h, product[:, :, 0, :], h, ALU.add).then_inc(h_mixed, 1)
                dve.drain()
                row_statistics(8 * u + i)

            evac_lo(0, 0)
            with dve.Fori(0, T // 128 - 1) as i:
                evac_lo(2 * i + 1, 1)
                tok(i, 0, False)
                evac_lo(2 * i + 2, 0)
                tok(i, 1, False)
            evac_lo(TILES - 1, 1)
            tok(T // 128 - 1, 0, True)
            tok(T // 128 - 1, 1, True)

            def layernorm_stats(k):
                dve.drain()
                for t in range(TILES):
                    nc.vector.bn_aggr(mv[:, t, :], stats[:, t, :])
                dve.drain()
                dve.sem_inc(moments_ready, 1)
                dve.wait_ge(std_ready, k)
                nc.vector.reciprocal(rstd[:], std[:])
                dve.drain()

            layernorm_stats(1)
            def normalise(k, keep):
                with dve.Fori(0, TILES // 4) as i:
                    for u in range(4):
                        t = 4 * i + u
                        args = (H[:, t, :], mv[:, t, 0:1], rstd[:, bass.ds(t, 1)], ALU.subtract, ALU.mult)
                        dve.wait_ge(xnT_ready, TILES * (k - 1) + t + 1)
                        nc.vector.tensor_scalar(xn[:, u, :], *args).then_inc(xn_ready, 1)
                        if keep:
                            nc.vector.tensor_scalar(XN[:, t, :], *args)

            normalise(1, False)

            def swap(hp, m):
                dve.wait_ge(qk_biased, NQK * hp + m + 1)
                alone(dve)
                nc.vector.stream_shuffle(q_swap[:, m % 2, :], qf[:, m % 2, :], [(r + 16) % 32 for r in range(32)]).then_inc(partners_swapped, 1)

            def rotated(hp, m):
                dve.wait_ge(rope_terms_ready, NQK * hp + m + 1)
                if not isinstance(hp, int) or NQK * hp + m > 0:
                    dve.wait_ge(qk_lo_ready, NQK * hp + m)
                nc.vector.tensor_tensor(q_rot[:, m % 2, :], q_sin[:, m % 2, :], q_cos[:, m % 2, :], ALU.add).then_inc(qk_rotated, 1)

            def split_v(hp, par, m, b):
                dve.wait_ge(v_hi_ready, NV * hp + m + 1)
                nc.vector.tensor_tensor(V_lo[:, par, 4 * m:4 * m + 4, :], bank(b).rearrange("p (t d) -> p t d", t=4),
                                        V_hi[:, par, 4 * m:4 * m + 4, :], ALU.subtract).then_inc(v_split, 1)

            for m in range(NQK + 1):
                if m < NQK:
                    swap(0, m)
                    dve.drain()
                    t0 = (m // 2) % 2 * 512
                    nc.vector.tensor_tensor(q_sin[:, m % 2, :], q_swap[:, m % 2, :], rope[:, 1, t0:t0 + 512], ALU.mult)
                    dve.drain()
                    rotated(0, m)
                if m >= 1:
                    k = m - 1
                    dve.wait_ge(qk_hi_ready, k + 1)
                    dst = lo_q[:] if k % 2 == 0 else lo_k[:, 0, :]
                    nc.vector.tensor_tensor(dst[:, k // 2 * 512:k // 2 * 512 + 512], q_rot[:, k % 2, :],
                                            hi[:, k % 2, k // 2 * 512:k // 2 * 512 + 512], ALU.subtract).then_inc(qk_lo_ready, 1)
            for m in range(NV):
                split_v(0, 0, m, m % 4)
            dve.wait_ge(bq_scaled, 1)
            nc.vector.tensor_tensor(H[:], H[:], b_o[:].unsqueeze(1).to_broadcast([128, TILES, D]), ALU.add)
            dve.drain()

            def maximum(hp, g):
                b, qt, h = STEPS[g]
                w = (qt + 1) * 128
                dve.wait_ge(scores_ready, NS * hp + g + 2)
                nc.vector.tensor_reduce(neg_max[:, g % 4:g % 4 + 1], bank(2 * (g % 2), 2)[:, 0:w], AX.X, ALU.max,
                                        negate=True).then_inc(max_ready, 1)

            maximum(0, 0)
            maximum(0, 1)

            def pair(hp, par, last):
                def split_PT(g):
                    for f, a, e in PARTS[g]:
                        dve.wait_ge(PT_hi_ready, NP * hp + f + 1)
                        nc.vector.tensor_tensor(PT_lo[:, f % 4, 0:(e - a) * 128], bank(4 + f % 2)[:, 0:(e - a) * 128],
                                                PT_hi[:, f % 4, 0:(e - a) * 128], ALU.subtract).then_inc(PT_lo_ready, 1)

                split_PT(0)
                maximum(hp, 2)
                for g in range(NS):
                    b, qt, h = STEPS[g]
                    k = g // 2
                    m = (g - 1 - FIRST_UNIT) // 2
                    turning = not last and 0 <= m < NQK
                    if g + 1 < NS:
                        split_PT(g + 1)
                    dve.wait_ge(probs_ready, NS * hp + g + 1)
                    nc.vector.reciprocal(inv_sum[:, g % 4:g % 4 + 1], row_sum[:, g % 4:g % 4 + 1]).then_inc(inverse_sum_ready, 1)
                    if g + 3 < NS:
                        maximum(hp, g + 3)
                    if turning and g % 2 == 0:
                        swap(hp + 1, m)
                    if not last and g % 2 == 0 and 1 <= m <= NQK:
                        rotated(hp + 1, m - 1)
                    if not last and NQK <= UNIT_AT.get(g, 0):
                        split_v(hp + 1, 1 - par, UNIT_AT[g] - NQK, 7)
                if not last:
                    maximum(hp + 1, 0)
                    maximum(hp + 1, 1)
                for n, k in enumerate(OUT_UNITS):
                    dve.wait_ge(out_projected, 8 * hp + n + 2)
                    hh = H[:, 2 * k:2 * k + 2, :]
                    nc.vector.tensor_tensor(hh, bank(4 + n % 2).rearrange("p (t d) -> p t d", t=2), hh, ALU.add).then_inc(h_attended, 1)
                    if last and n >= 1:
                        dve.wait_ge(h_attended, 8 * hp + n + 1)
                        row_statistics(2 * OUT_UNITS[n - 1])
                        row_statistics(2 * OUT_UNITS[n - 1] + 1)
                dve.drain()
                if last:
                    row_statistics(2 * OUT_UNITS[7])
                    row_statistics(2 * OUT_UNITS[7] + 1)

            over_pairs(dve, pair)
            layernorm_stats(2)
            normalise(2, True)
            dve.drain()

            def w1_low(e):
                dve.wait_ge(w1_hi_ready, e + 1)
                nc.vector.tensor_tensor(W1_lo[:, e, :, :], W1_in(e), W1_hi[:, e, :, :], ALU.subtract).then_inc(w1_lo_ready[1], 1)

            w1_low(1)
            dve.wait_ge(logits_done, 1)
            dve.wait_ge(router_in, 64)
            flat = lambda a: a[:].rearrange("p t e -> p (t e)")
            over_e = lambda a: a.unsqueeze(2).to_broadcast([128, TILES, EXPERTS])
            nc.vector.tensor_tensor(logit[:], bank(4)[:, 0:128].rearrange("p (t e) -> p t e", e=EXPERTS),
                                    b_r[:].unsqueeze(1).to_broadcast([128, TILES, EXPERTS]), ALU.add)
            dve.drain()
            nc.vector.tensor_reduce(top[:], logit[:], AX.X, ALU.max)
            dve.drain()
            nc.vector.tensor_tensor(logit[:], logit[:], over_e(top[:]), ALU.subtract).then_inc(logits_shifted, 1)
            dve.drain()
            nc.vector.tensor_scalar(flat(pick), flat(logit), 0.0, None, ALU.is_equal)
            dve.wait_ge(logits_exp, 1)
            nc.vector.tensor_reduce(posf[:], cand[:], AX.X, ALU.add)
            dve.drain()
            nc.vector.reciprocal(gate[:], posf[:])
            nc.vector.scalar_tensor_tensor(flat(cand), flat(pick), -float(EXPERTS), const("expert_plus"), ALU.mult, ALU.add)
            dve.drain()
            nc.vector.tensor_reduce(top[:], cand[:], AX.X, ALU.min)
            dve.drain()
            nc.vector.tensor_tensor(pick[:], const("expert").rearrange("p (t e) -> p t e", e=EXPERTS), over_e(top[:]), ALU.is_equal).then_inc(picks_ready, 1)
            dve.wait_ge(ranks_done, 1)
            nc.vector.tensor_copy(flat(tot), bank(6)[:, 0:128])
            nc.vector.tensor_copy(scan[:, 0, :, :].rearrange("p t e -> p (t e)"), bank(6)[:, 0:128])
            dve.drain()
            a, sh = 0, 1
            while sh < TILES:
                nc.vector.tensor_copy(scan[:, 1 - a, 0:sh, :], scan[:, a, 0:sh, :])
                nc.vector.tensor_tensor(scan[:, 1 - a, sh:TILES, :], scan[:, a, sh:TILES, :], scan[:, a, 0:TILES - sh, :], ALU.add)
                dve.drain()
                a, sh = 1 - a, 2 * sh
            count = scan[:, a, TILES - 1, :]
            nc.vector.tensor_tensor(more[:], count.unsqueeze(2).to_broadcast([128, EXPERTS, TILES]),
                                    const("k128").rearrange("p (e k) -> p e k", e=EXPERTS), ALU.is_gt)
            dve.drain()
            nc.vector.tensor_reduce(ntile[:], more[:], AX.X, ALU.add)
            dve.drain()
            nc.vector.tensor_copy(cum[:, 0, :], ntile[:])
            dve.drain()
            c, sh = 0, 1
            while sh < EXPERTS:
                nc.vector.tensor_copy(cum[:, 1 - c, 0:sh], cum[:, c, 0:sh])
                nc.vector.tensor_tensor(cum[:, 1 - c, sh:EXPERTS], cum[:, c, sh:EXPERTS], cum[:, c, 0:EXPERTS - sh], ALU.add)
                dve.drain()
                c, sh = 1 - c, 2 * sh
            nc.vector.tensor_tensor(start[:], cum[:, c, :], ntile[:], ALU.subtract)
            nc.vector.tensor_tensor(past[:], cum[:, c, :].unsqueeze(1).to_broadcast([128, SLOT_TILES, EXPERTS]),
                                    const("slot_tile").rearrange("p (s e) -> p s e", e=EXPERTS), ALU.is_le)
            nc.vector.tensor_tensor(cand[:], scan[:, a, :, :], tot[:], ALU.subtract)
            dve.drain()
            nc.vector.tensor_scalar(start[:], start[:], 128.0, None, ALU.mult)
            nc.vector.tensor_reduce(expf[:], past[:], AX.X, ALU.add)
            nc.vector.tensor_tensor(flat(cand), bank(5)[:, 0:128], flat(cand), ALU.add)
            dve.drain()
            nc.vector.tensor_scalar(expi[:], expf[:], float(EXPERTS - 1), None, ALU.min)
            nc.vector.tensor_tensor(cand[:], cand[:], start[:].unsqueeze(1).to_broadcast([128, TILES, EXPERTS]), ALU.add)
            dve.drain()
            nc.vector.tensor_tensor(cand[:], cand[:], pick[:], ALU.mult)
            dve.drain()
            nc.vector.tensor_reduce(posf[:], cand[:], AX.X, ALU.add)
            dve.drain()
            nc.vector.tensor_copy(pos[:], posf[:])
            dve.drain()
            dve.sem_inc(places_ready, 1)

            w1_low(3)
            w1_low(5)
            w1_low(7)

            def evac_y(s, u, i):
                dve.wait_ge(slot_product_done, s + 3)
                if not isinstance(i, int) or i >= 1:
                    dve.wait_ge(ys_stored[u], 16 * i)
                nc.vector.tensor_copy(ys[:, u, :], bank(6 + u)[:, 0:256]).then_inc(ys_ready, 1)

            def split_xs(s, u):
                dve.wait_ge(slot_transposed, s + 3)
                x = bank(u)[:, 0:256].rearrange("p (c t) -> p c t", c=KC)
                nc.vector.tensor_copy(xs_hi[:, u, :, :], x)
                dve.drain()
                nc.vector.tensor_tensor(xs_lo[:, u, :, :], x, xs_hi[:, u, :, :], ALU.subtract).then_inc(slot_split, 1)

            split_xs(0, 0)
            split_xs(1, 1)
            split_xs(2, 0)
            evac_y(0, 0, 0)
            split_xs(3, 1)
            evac_y(1, 1, 0)
            with dve.Fori(1, SLOT_TILES // 2 - 1) as i:
                split_xs(2 * i + 2, 0)
                evac_y(2 * i, 0, i)
                split_xs(2 * i + 3, 1)
                evac_y(2 * i + 1, 1, i)
            split_xs(SLOT_TILES - 1, 0)
            evac_y(SLOT_TILES - 3, 0, SLOT_TILES // 2 - 1)
            evac_y(SLOT_TILES - 2, 1, SLOT_TILES // 2 - 1)
            evac_y(SLOT_TILES - 1, 0, SLOT_TILES // 2)
            for t in range(TILES + 1):
                if t < TILES:
                    if t % 4 == 0:
                        dve.wait_ge(rows_gathered[t // 4], 64)
                    nc.vector.scalar_tensor_tensor(H[:, t, :], XN[:, t, :], gate[:, t:t + 1], H[:, t, :], ALU.mult, ALU.add).then_inc(h_expert_added, 1)
                if t >= 1:
                    dve.wait_ge(h_expert_added, t)
                    row_statistics(t - 1)
            layernorm_stats(3)
            dve.wait_ge(late_buffers_set, 1)

            def lin_norm(n, u):
                dve.wait_ge(lin_x_transposed, n + 1)
                nc.vector.tensor_scalar(xn[:, u, :], H[:, lin_tile(n, u), :], mv[:, lin_tile(n, u), 0:1],
                                        rstd[:, bass.ds(lin_tile(n, u), 1)], ALU.subtract, ALU.mult).then_inc(lin_xn_ready, 1)

            def lin_features(n, u):
                dve.wait_ge(lin_expT_ready, n + 1)
                nc.vector.tensor_scalar(eT[:], eT[:], 1.0, None, ALU.min)
                dve.drain()
                dve.wait_ge(lin_qz_ready, 2 * n + 2)
                nc.vector.scalar_tensor_tensor(qkT[:, u, :, :].rearrange("p a t -> p (a t)"), bank(0), 0.0, eT[:], ALU.max, ALU.add).then_inc(lin_qkT_ready, 1)
                dve.wait_ge(lin_exp_v_ready, n + 1)
                nc.vector.tensor_scalar(ek[:], ek[:], 1.0, None, ALU.min)
                dve.drain()
                nc.vector.tensor_tensor(v_lo[:, u, :, 0:16], bank(1)[:, 256:512].rearrange("p (h d) -> p h d", h=LHEADS),
                                        v_hi[:, u, :, 0:16], ALU.subtract)
                nc.vector.scalar_tensor_tensor(ktok[:, u, :], bank(1)[:, 0:256], 0.0, ek[:], ALU.max, ALU.add).then_inc(lin_k_v_ready, 1)

            def lin_mask(n, r):
                dve.wait_ge(lin_kq_done, 4 * n + r + 2)
                nc.vector.tensor_tensor(AT[:, heads(r), :], bank(2 + r % 2).rearrange("p (h t) -> p h t", h=4),
                                        const("causal_mul").unsqueeze(1).to_broadcast([128, 4, 128]),
                                        ALU.mult).then_inc(lin_kq_masked, 1)

            def lin_low(n, r):
                dve.wait_ge(lin_AT_hi_ready, 4 * n + r + 1)
                nc.vector.tensor_tensor(AT_lo[:, heads(r), :], AT[:, heads(r), :], AT_hi[:, heads(r), :],
                                        ALU.subtract).then_inc(lin_AT_lo_ready, 1)

            def lin_divide(n):
                dve.wait_ge(lin_sums_done, n + 3)
                num = bank(6)[:, 0:272].rearrange("p (h x) -> p h x", x=17)
                nc.vector.tensor_scalar(den[:], num[:, :, 16], 1e-8, None, ALU.add)
                dve.drain()
                nc.vector.reciprocal(den[:], den[:])
                dve.drain()
                nc.vector.tensor_tensor(o[:].rearrange("p (h x) -> p h x", x=16), num[:, :, 0:16],
                                        den[:].unsqueeze(2).to_broadcast([128, LHEADS, 16]), ALU.mult).then_inc(lin_o_ready, 1)

            def lin_own(n):
                dve.wait_ge(lin_kv_done, n + 1)
                nc.vector.tensor_tensor(sdel[:].rearrange("p (c x) -> p c x", c=2), bank(4)[:, 0:272].rearrange("p (c x) -> p c x", c=2),
                                        const("own_head").unsqueeze(1).to_broadcast([128, 2, 136]), ALU.mult)

            def lin_state(u):
                nc.vector.tensor_tensor(state[:, u, :], state[:, u, :], sdel[:], ALU.add).then_inc(lin_state_updated, 1)

            def lin_add(n, u):
                dve.wait_ge(lin_out_done, n + 2)
                hh = H[:, lin_tile(n, u), :]
                nc.vector.tensor_tensor(hh, bank(5)[:, 256:512], hh, ALU.add).then_inc(h_lin_added, 1)

            def lin_step(n, u):
                if lin_has(n - 1):
                    lin_divide(n - 1)
                if lin_has(n):
                    lin_mask(n, 0)
                    lin_mask(n, 1)
                if lin_has(n - 1):
                    lin_own(n - 1)
                if lin_has(n):
                    lin_low(n, 0)
                    lin_mask(n, 2)
                    lin_low(n, 1)
                dve.drain()
                if lin_has(n - 2):
                    row_statistics(lin_tile(n - 2, u))
                if lin_has(n - 1):
                    lin_state(1 - u)
                if lin_has(n):
                    lin_mask(n, 3)
                    lin_low(n, 2)
                    lin_low(n, 3)
                if lin_has(n + 1):
                    lin_features(n + 1, 1 - u)
                if lin_has(n - 1):
                    lin_add(n - 1, 1 - u)
                if lin_has(n + 3):
                    lin_norm(n + 3, 1 - u)

            lin_norm(0, 0)
            lin_norm(1, 1)
            lin_norm(2, 0)
            lin_features(0, 0)
            lin_loop(dve, lin_step)
            dve.drain()
            row_statistics(TILES - 1)
            layernorm_stats(4)
            normalise(3, True)
            dve.drain()
            dve.wait_ge(gate_weights_in, 16 * 14)
            for m in range(4):
                dve.wait_ge(gate_xc_ready, m + 1)
                nc.vector.bn_stats(bst[:, m, :], xc[:, m * 512:(m + 1) * 512])
            dve.drain()
            nc.vector.bn_aggr(bmv[:], bst[:].rearrange("p a b -> p (a b)")).then_inc(batch_var_ready, 1)
            dve.wait_ge(batch_std_ready, 1)
            nc.vector.reciprocal(bsc[:, 0:1], bstd[:])
            dve.drain()
            nc.vector.tensor_tensor(bsc[:, 1:2], bsc[:, 0:1], gcols[:, 1:2], ALU.mult)
            dve.drain()
            nc.vector.tensor_tensor(bsc[:, 0:1], bsc[:, 1:2], bmv[:, 0:1], ALU.mult)
            dve.drain()
            nc.vector.tensor_tensor(bsc[:, 2:3], gcols[:, 2:3], bsc[:, 0:1], ALU.subtract).then_inc(batch_scale_ready, 1)

            def gate_top(n, u, r):
                src = L if r == 0 else Lr
                for j in range(2):
                    if r == 0:
                        dve.wait_ge(gate_logits_ready, n + 1)
                    else:
                        dve.wait_ge(gate_top_step[j], 8 * n + 2 * r)
                    alone(dve)
                    nc.vector.max(m8[:, u, j, r, :], src[:, u, j, :]).then_inc(gate_top_step[j], 1)
                for j in range(2):
                    dve.wait_ge(gate_top_step[j], 8 * n + 2 * r + 1)
                    alone(dve)
                    nc.vector.match_replace(Lr[:, u, j, :], m8[:, u, j, r, :], src[:, u, j, :], NEG).then_inc(gate_top_step[j], 1)
                if r == 0:
                    nc.vector.tensor_scalar(nmx[:, u, :], m8[:, u, :, 0, 0], -1.0, None, ALU.mult)

            def gate_step(n, u):
                v = 1 - u
                if gate_has(n):
                    dve.wait_ge(gate_logits_done, n + 1)
                    nc.vector.tensor_tensor(L[:, u, :, :], bank(u).rearrange("p (j d) -> p j d", j=2), lin_b[:], ALU.add).then_inc(gate_logits_ready, 1)
                if gate_has(n - 2):
                    dve.wait_ge(gate_in_done, n + 1)
                    nc.vector.tensor_tensor(H[:, n - 2, :], bank(6 + u)[:, 0:256], H[:, n - 2, :], ALU.add).then_inc(h_gated, 1)
                if gate_has(n):
                    gate_top(n, u, 0)
                    gate_top(n, u, 1)
                if gate_has(n - 1):
                    dve.wait_ge(gate_exp_ready, n)
                    nc.vector.reciprocal(einv[:, v, :], esum[:, v, :])
                    dve.drain()
                    dve.wait_ge(gate_kept_ready, n)
                    nc.vector.scalar_tensor_tensor(xg[:, v, :], ef[:, v, 1, :], einv[:, v, 1:2], XN[:, n - 1, :], ALU.mult, ALU.mult).then_inc(gate_xg_ready, 1)
                    dve.wait_ge(gate_full_done, n + 1)
                    nc.vector.scalar_tensor_tensor(ob[:, v, :], ef[:, v, 0, :], einv[:, v, 0:1], bank(2 + v)[:, 0:256], ALU.mult, ALU.mult).then_inc(gate_out_ready, 1)
                if gate_has(n):
                    gate_top(n, u, 2)
                    gate_top(n, u, 3)
                dve.drain()
                if gate_has(n):
                    dve.sem_inc(gate_top_done, 1)
                if gate_has(n - 1):
                    nc.vector.tensor_tensor(H[:, n - 1, :], H[:, n - 1, :], ob[:, v, :], ALU.add)
                    dve.drain()

            gate_loop(dve, gate_step)

        @block.tensor
        def _(pe):
            pe.wait_ge(consts_in, 16)
            def transpose_x(n, i, u):
                pe.wait_ge(x_in_ready[u], 16 * i + 16)
                if not isinstance(n, int) or n >= 2:
                    pe.wait_ge(x_lo_ready, n - 1)
                for c in range(8):
                    last = nc.tensor.transpose(bank(2 * u, 2)[:, c * 128:(c + 1) * 128], x_in[:, u, c * 128:(c + 1) * 128], const("ident"))
                last.then_inc(x_transposed, 1)

            transpose_x(0, 0, 0)
            transpose_x(1, 0, 1)
            pe.wait_ge(tap_bias_ready, 1)
            for c in range(8):
                last = nc.tensor.matmul(bank(4)[:, 32 * c:32 * c + 32], const("ones"), bias32[:, c, :], start=True, stop=True)
            last.then_inc(bias_sum_ready, 1)
            pe.wait_ge(taps_ready, 2)

            def conv(n, u):
                pe.wait_ge(x_hi_ready, n + 1)
                pe.wait_ge(x_lo_ready, n + 1)
                if not isinstance(n, int) or n >= 2:
                    pe.wait_ge(h_mixed, n - 1)
                first = True
                for c in range(8):
                    for j in range(TAPS):
                        nc.tensor.matmul(bank(4 + u)[:, 64 * c:64 * c + 64], x_hi[:, u, c, j:j + 128],
                                         taps16[:, c, j, :, :].rearrange("p k g -> p (k g)"),
                                         start=(c == 0 and j == 0), stop=True, skip_group_check=True)
                        last = nc.tensor.matmul(bank(4 + u)[:, 64 * c:64 * c + 32], x_lo[:, u, c, j:j + 128], taps16[:, c, j, 0, :],
                                                start=False, stop=True, skip_group_check=True)
                last.then_inc(conv_done, 1)

            conv(0, 0)
            transpose_x(2, 1, 0)
            conv(1, 1)
            with pe.Fori(1, T // 128 - 1) as i:
                transpose_x(2 * i + 1, i, 1)
                conv(2 * i, 0)
                transpose_x(2 * i + 2, i + 1, 0)
                conv(2 * i + 1, 1)
            transpose_x(TILES - 1, T // 128 - 1, 1)
            conv(TILES - 2, 0)
            conv(TILES - 1, 1)
            pe.wait_ge(h_mixed, TILES)

            def transpose_tiles(k):
                with pe.Fori(0, TILES // 4) as i:
                    for u in range(4):
                        pe.wait_ge(xn_ready, TILES * (k - 1) + 4 * i + u + 1)
                        for c in range(KC):
                            last = nc.tensor.transpose(bank(u)[:, c * 128:(c + 1) * 128], xn[:, u, c * 128:(c + 1) * 128], const("ident"))
                        last.then_inc(xn_transposed, 1)
            transpose_tiles(1)

            def project_qk(hp, m, b):
                for c in range(KC):
                    last = nc.tensor.matmul(bank(b), w_qk[:, m % 2, c, :], xnT[:, c, m // 2 * 512:m // 2 * 512 + 512],
                                            start=(c == 0), stop=(c == KC - 1))
                last.then_inc(qk_projected, 1)

            def project_v(hp, m, b):
                for t in range(4):
                    tok = (4 * m + t) * 128
                    for c in range(KC):
                        last = nc.tensor.matmul(bank(b)[:, t * 128:(t + 1) * 128], xnT[:, c, tok:tok + 128], w_v[:, c, :],
                                                start=(c == 0), stop=(c == KC - 1))
                last.then_inc(v_projected, 1)

            pe.wait_ge(xnT_ready, TILES + 4)
            pe.wait_ge(wqk_permuted, 2)
            for m in range(NQK):
                if m >= 4:
                    pe.wait_ge(qk_biased, m - 3)
                project_qk(0, m, m % 4)
            pe.wait_ge(wv_in, 32)
            for m in range(NV):
                pe.wait_ge(qk_biased, m + 5)
                project_v(0, m, m % 4)
            pe.wait_ge(v_split, NV)

            def scores(hp, par, g):
                b, qt, h = STEPS[g]
                q0, w = b * T + qt * 128, (qt + 1) * 128
                own = slice(64 * h, 64 * h + 64)
                if g == 0:
                    pe.wait_ge(operands_stacked[par], 64 * (hp - par) + 128)
                    pe.wait_ge(qk_lo_ready, NQK * hp + NQK + 1)
                if g >= 2:
                    pe.wait_ge(probs_ready, NS * hp + g - 1)
                for a in range(0, w, 512):
                    e = min(a + 512, w)
                    dst = bank(2 * (g % 2), 2)[:, a:e]
                    nc.tensor.matmul(dst, Q2[:, par, h, q0:q0 + 128], K2[:, par, h, b * T + a:b * T + e], start=True, stop=False)
                    last = nc.tensor.matmul(dst, Q2[own, par, h, q0:q0 + 128], lo_k[own, par, b * T + a:b * T + e],
                                            start=False, stop=True)
                    if e == w:
                        last = nc.tensor.matmul(bank(2 * (g % 2), 2)[:, w - 128:w], ident16[:], mask16[:], start=False, stop=True,
                                                skip_group_check=True)
                last.then_inc(scores_ready, 1)

            scores(0, 0, 0)
            scores(0, 0, 1)

            def pair(hp, par, last_pair):
                def transpose_P(part, g):
                    f, a, e = part
                    pe.wait_ge(PT_lo_ready, NP * hp + f + 1)
                    for j in range(a, e):
                        last = nc.tensor.transpose(bank(4 + f % 2)[:, (j - a) * 128:(j - a + 1) * 128],
                                                   P[:, g % 2, j * 128:(j + 1) * 128], const("ident"))
                    last.then_inc(probs_transposed, 1)

                def times_V(part, g):
                    b, qt, h = STEPS[g]
                    f, a, e = part
                    for high in (True, False):
                        pe.wait_ge(PT_hi_ready if high else PT_lo_ready, NP * hp + f + (1 if high else 3))
                        for j in range(a, e):
                            PT = (PT_hi if high else PT_lo)[:, f % 4, (j - a) * 128:(j - a + 1) * 128]
                            for V in ((V_hi, V_lo) if high else (V_hi,)):
                                last = nc.tensor.matmul(bank(6)[:, 64 * h:64 * h + 64], PT, V[:, par, b * 8 + j, 64 * h:64 * h + 64],
                                                        start=(high and j == 0 and V is V_hi), stop=(not high and j == qt))
                    last.then_inc(PV_done, 1)

                def transpose_z(k, units):
                    pe.wait_ge(z_divided, NS * hp + 2 * k + 4)
                    if k:
                        pe.wait_ge(zT_ready, 16 * hp + k)
                    if 0 < units <= NQK:
                        pe.wait_ge(qk_biased, NQK * hp + NQK + units)
                    elif units:
                        pe.wait_ge(v_split, NV * hp + NV + units - NQK)
                    nc.tensor.transpose(bank(7)[:, 0:128], z[:, k % 2, :], const("ident")).then_inc(z_transposed, 1)

                def unit(m, k):
                    if m == 0:
                        pe.wait_ge(wqk_permuted, hp + 3)
                    if m == NQK:
                        pe.wait_ge(wv_in, 32 * hp + 64)
                    pe.wait_ge(zT_ready, 16 * hp + k + 1)
                    if m < NQK:
                        project_qk(hp + 1, m, 7)
                    else:
                        project_v(hp + 1, m - NQK, 7)

                pe.wait_ge(probs_ready, NS * hp + 1)
                for part in PARTS[0]:
                    transpose_P(part, 0)
                scores(hp, par, 2)
                for g in range(NS):
                    if g + 1 < NS:
                        pe.wait_ge(probs_ready, NS * hp + g + 2)
                        for part in PARTS[g + 1]:
                            transpose_P(part, g + 1)
                    if g + 3 < NS:
                        scores(hp, par, g + 3)
                    pe.wait_ge(z_divided, NS * hp + g + 2)
                    for part in PARTS[g]:
                        times_V(part, g)
                    if g % 2 == 0 and g >= 2:
                        units = 0 if last_pair else sum(1 for at in UNIT_AT if at < g)
                        transpose_z(g // 2 - 1, units)
                    if not last_pair and g in UNIT_AT:
                        unit(UNIT_AT[g], (g - 1) // 2 - 1)
                if not last_pair:
                    pe.wait_ge(v_split, NV * hp + 2 * NV)
                    scores(hp + 1, 1 - par, 0)
                    scores(hp + 1, 1 - par, 1)
                transpose_z(NS // 2 - 1, 0)
                pe.wait_ge(wo_in, 16 * hp + 16)
                for n, k in enumerate(OUT_UNITS):
                    pe.wait_ge(zT_ready, 16 * hp + (15 if n < 7 else 16))
                    if n >= 2:
                        pe.wait_ge(h_attended, 8 * hp + n)
                    for t in range(2):
                        last = nc.tensor.matmul(bank(4 + n % 2)[:, t * 256:(t + 1) * 256], zT[:, (2 * k + t) * 128:(2 * k + t + 1) * 128],
                                                w_o[:], start=True, stop=True)
                    last.then_inc(out_projected, 1)
                pe.wait_ge(h_attended, 8 * hp + 9)

            over_pairs(pe, pair)
            pe.wait_ge(router_in, 64)
            for n in range(TILES + 4):
                if n < TILES:
                    pe.wait_ge(xn_ready, TILES + n + 1)
                    for c in range(KC):
                        last = nc.tensor.transpose(bank(n % 4)[:, c * 128:(c + 1) * 128], xn[:, n % 4, c * 128:(c + 1) * 128], const("ident"))
                    last.then_inc(xn_transposed, 1)
                t = n - 4
                if t >= 0:
                    pe.wait_ge(xnT_ready, TILES + t + 1 + 4)
                    for c in range(KC):
                        last = nc.tensor.matmul(bank(4)[:, t * 8:(t + 1) * 8], xnT[:, c, t * 128:(t + 1) * 128], w_r[:, c, :],
                                                start=(c == 0), stop=(c == KC - 1))
            last.then_inc(logits_done, 1)
            pe.wait_ge(picks_ready, 1)
            nc.tensor.matmul(bank(5)[:, 0:128], const("before"), pick[:].rearrange("p t e -> p (t e)"), start=True, stop=True)
            nc.tensor.matmul(bank(6)[:, 0:128], const("ones"), pick[:].rearrange("p t e -> p (t e)"), start=True, stop=True).then_inc(ranks_done, 1)
            pe.wait_ge(places_ready, 1)

            def tr_xs(s, u, i):
                pe.wait_ge(slot_in[u], 16 * i + 16)
                for c in range(KC):
                    last = nc.tensor.transpose(bank(u)[:, c * 128:(c + 1) * 128], xs[:, u, c * 128:(c + 1) * 128], const("ident"))
                last.then_inc(slot_transposed, 1)

            def up(s, u):
                e = pe.value_load(expi[0:1, bass.ds(s, 1)], min_val=0, max_val=EXPERTS - 1)
                pe.wait_ge(slot_split, s + 1)
                pe.wait_ge(gelu_done, s + 1)
                for f in range(8):
                    for c in range(KC):
                        for W, x in ((W1_hi, xs_hi), (W1_hi, xs_lo), (W1_lo, xs_hi)):
                            last = nc.tensor.matmul(bank(2 + 2 * u, 2)[:, f * 128:(f + 1) * 128],
                                                    W[:, bass.ds(e, 1), c, f * 128:(f + 1) * 128].rearrange("p a f -> p (a f)"), x[:, u, c, :],
                                                    start=(c == 0 and W is W1_hi and x is xs_hi), stop=(c == KC - 1 and W is W1_lo))
                last.then_inc(hidden_done, 1)

            def down(s, u):
                e = pe.value_load(expi[0:1, bass.ds(s, 1)], min_val=0, max_val=EXPERTS - 1)
                pe.wait_ge(gelu_done, s + 3)
                if not isinstance(s, int) or s >= 2:
                    pe.wait_ge(ys_ready, s - 1)
                for f in range(8):
                    nc.tensor.matmul(bank(6 + u)[:, 0:256], gelT[:, u, f, :], W2[:, bass.ds(e, 1), f, :].rearrange("p a f -> p (a f)"), start=(f == 0), stop=False)
                nc.tensor.matmul(bank(6 + u)[:, 0:256], const("ones")[0:1, :], b_2[0:1, bass.ds(e * D, D)], start=False, stop=True).then_inc(slot_product_done, 1)

            pe.wait_ge(w1_lo_ready[0], EXPERTS // 2)
            pe.wait_ge(w1_lo_ready[1], EXPERTS // 2)
            tr_xs(0, 0, 0)
            tr_xs(1, 1, 0)
            up(0, 0)

            def slot(s, u, i):
                up(s + 1, 1 - u)
                if i is not None:
                    tr_xs(s + 2, u, i)
                down(s, u)

            up(1, 1)
            tr_xs(2, 0, 1)
            pe.wait_ge(w2_in, 128)
            down(0, 0)
            slot(1, 1, 1)
            with pe.Fori(1, SLOT_TILES // 2 - 1) as i:
                slot(2 * i, 0, i + 1)
                slot(2 * i + 1, 1, i + 1)
            slot(SLOT_TILES - 3, 0, SLOT_TILES // 2)
            slot(SLOT_TILES - 2, 1, None)
            down(SLOT_TILES - 1, 0)
            pe.wait_ge(ys_ready, SLOT_TILES)
            pe.wait_ge(lin_weights_in, 64)
            for j in range(4):
                for c in range(KC):
                    for oc in range(2):
                        last = nc.tensor.transpose(bank(j)[:, c * 256 + oc * 128:c * 256 + oc * 128 + 128], wl_in[:, j, oc, c * 128:(c + 1) * 128], const("ident"))
                last.then_inc(lin_weights_transposed, 1)
            pe.wait_ge(gate_weights_in, 16 * 14)
            for c in range(2):
                last = nc.tensor.transpose(bank(4)[:, c * 128:(c + 1) * 128], lin_in[:, c, :], const("ident"))
            last.then_inc(gate_lin_transposed, 1)
            pe.wait_ge(lin_wT_ready, 4)
            pe.wait_ge(gate_lin_ready, 1)

            def lin_xt(n, u):
                pe.wait_ge(lin_xn_ready, n + 1)
                if not isinstance(n, int) or n >= 1:
                    pe.wait_ge(lin_xT_ready, n)
                for c in range(KC):
                    last = nc.tensor.transpose(bank(7)[:, c * 128:(c + 1) * 128], xn[:, u, c * 128:(c + 1) * 128], const("ident"))
                last.then_inc(lin_x_transposed, 1)

            def lin_project(n, u):
                pe.wait_ge(lin_xT_ready, n + 1)
                if not isinstance(n, int) or n >= 1:
                    pe.wait_ge(lin_qkT_ready, n)
                    pe.wait_ge(lin_k_v_ready, n)
                for a in range(4):
                    w = (2, 2, 0, 0)[a]
                    for c in range(KC):
                        last = nc.tensor.matmul(bank(0)[:, a * 128:(a + 1) * 128], wlT[:, c, w, a % 2 * 128:a % 2 * 128 + 128], xT[:, u, c, :],
                                                start=(c == 0), stop=(c == KC - 1))
                last.then_inc(lin_qkT_projected, 1)
                for c in range(KC):
                    last = nc.tensor.matmul(bank(1), xT[:, u, c, :], wlT[:, c, 0:2, :].rearrange("p a d -> p (a d)"),
                                            start=(c == 0), stop=(c == KC - 1))
                last.then_inc(lin_kv_projected, 1)

            def lin_kq(n, u, r):
                pe.wait_ge(lin_kq_masked, 4 * n + r + 1)
                c, j = r % 2, r // 2 * 4
                if c == 0:
                    pe.wait_ge(lin_qz_ready, 2 * n + 5 + r // 2)
                nc.tensor.matmul(bank(2 + r % 2), qkT[:, u, 2 + c, :], qz[:, u, c, j:j + 4, :].rearrange("p h t -> p (h t)"),
                                 start=True, stop=True).then_inc(lin_kq_done, 1)

            def lin_num(n, u):
                pe.wait_ge(lin_state_updated, n + 1)
                pe.wait_ge(lin_o_ready, n + 1)
                for c in range(KC):
                    nc.tensor.matmul(bank(6)[:, c * 136:(c + 1) * 136], qkT[:, u, c, :], state[:, u, c * 136:(c + 1) * 136], start=(c == 0), stop=True, skip_group_check=True)
                pe.wait_ge(lin_AT_lo_ready, 4 * n + 4)
                pe.wait_ge(lin_k_v_ready, n + 1)
                for h in range(LHEADS):
                    for A, v in ((AT_hi, v_hi), (AT_hi, v_lo), (AT_lo, v_hi)):
                        last = nc.tensor.matmul(bank(6)[:, h * 17:(h + 1) * 17], A[:, h, :], v[:, u, h, :], start=False, stop=True, skip_group_check=True)
                last.then_inc(lin_sums_done, 1)

            def lin_kv(n, u):
                pe.wait_ge(lin_state_updated, n + 2)
                pe.wait_ge(lin_k_v_ready, n + 1)
                for c in range(KC):
                    last = nc.tensor.matmul(bank(4)[:, c * 136:(c + 1) * 136], ktok[:, u, c * 128:(c + 1) * 128],
                                            vaug[:, u, 8 * c:8 * c + 8, :].rearrange("p h x -> p (h x)"), start=True, stop=True)
                last.then_inc(lin_kv_done, 1)

            def lin_ot(n):
                pe.wait_ge(lin_o_ready, n + 2)
                pe.wait_ge(h_lin_added, n + 1)
                for c in range(KC):
                    last = nc.tensor.transpose(bank(5)[:, c * 128:(c + 1) * 128], o[:, c * 128:(c + 1) * 128], const("ident"))
                last.then_inc(lin_o_transposed, 1)

            def lin_out(n):
                pe.wait_ge(lin_oT_ready, n + 1)
                for c in range(KC):
                    last = nc.tensor.matmul(bank(5)[:, 256:512], oT[:, c, :], wlT[:, c, 3, :], start=(c == 0), stop=(c == KC - 1))
                last.then_inc(lin_out_done, 1)

            def lin_step(n, u):
                if lin_has(n + 2):
                    lin_xt(n + 2, u)
                if lin_has(n):
                    lin_kq(n, u, 0)
                    lin_kq(n, u, 1)
                if lin_has(n - 1):
                    lin_ot(n - 1)
                if lin_has(n):
                    lin_kq(n, u, 2)
                    lin_kq(n, u, 3)
                if lin_has(n + 1):
                    lin_project(n + 1, 1 - u)
                if lin_has(n - 1):
                    lin_out(n - 1)
                if lin_has(n):
                    lin_num(n, u)
                    lin_kv(n, u)

            lin_xt(0, 0)
            lin_xt(1, 1)
            lin_project(0, 0)
            lin_loop(pe, lin_step)
            pe.wait_ge(h_lin_added, TILES + 1)
            transpose_tiles(3)
            pe.wait_ge(gate_conv_ready, 1)
            for m in range(4):
                pe.wait_ge(xnT_ready, 2 * TILES + 4 * m + 8)
                for c in range(KC):
                    last = nc.tensor.matmul(bank(4 + m), CW[:, c, :], xnT[:, c, m * 512:(m + 1) * 512], start=(c == 0), stop=(c == KC - 1))
                last.then_inc(gate_conv_done, 1)
            pe.wait_ge(gate_xc_ready, 4)

            def gate_logits(n, u):
                pe.wait_ge(gate_tile_copied, n + 1)
                if not isinstance(n, int) or n >= 2:
                    pe.wait_ge(gate_logits_ready, n - 1)
                nc.tensor.matmul(bank(u), xat[:, u, :], linT[:].rearrange("p j d -> p (j d)"), start=True, stop=True).then_inc(gate_logits_done, 1)

            def gate_full(n, u):
                if not isinstance(n, int) or n >= 2:
                    pe.wait_ge(gate_out_ready, n - 1)
                for c in range(KC):
                    last = nc.tensor.matmul(bank(2 + u)[:, 0:256], xgt[:, u, c, :], wg[:, c, :], start=(c == 0), stop=(c == KC - 1))
                last.then_inc(gate_full_done, 1)

            def gate_step(n, u):
                v = 1 - u
                if gate_has(n + 1):
                    gate_logits(n + 1, v)
                if gate_has(n - 1):
                    pe.wait_ge(gate_xg_ready, n)
                    for c in range(KC):
                        last = nc.tensor.transpose(bank(4 + v)[:, c * 128:(c + 1) * 128], xg[:, v, c * 128:(c + 1) * 128], const("ident"))
                    last.then_inc(gate_xg_transposed, 1)
                if gate_has(n + 1):
                    gate_full(n + 1, v)
                if gate_has(n - 1):
                    pe.wait_ge(gate_xgT_ready, n)
                    for c in range(KC):
                        nc.tensor.matmul(bank(6 + v)[:, 0:256], xgT[:, v, c, :], wg[:, c, :], start=(c == 0), stop=False)
                    nc.tensor.matmul(bank(6 + v)[:, 0:256], const("ones")[0:1, :], bias_g[0:1, :], start=False, stop=True).then_inc(gate_in_done, 1)

            gate_logits(0, 0)
            gate_full(0, 0)
            gate_loop(pe, gate_step)


NAMES = ['x', 'L0_tok_conv_w', 'L0_tok_conv_b', 'L0_tok_read', 'L0_attn_W_Q', 'L0_attn_b_Q', 'L0_attn_W_K', 'L0_attn_b_K', 'L0_attn_W_V', 'L0_attn_b_V', 'L0_attn_W_O', 'L0_attn_b_O',
         'L0_ffn_W1', 'L0_ffn_b1', 'L0_ffn_W2', 'L0_ffn_b2', 'L0_ffn_Wr', 'L0_ffn_br', 'L1_attn_Wq', 'L1_attn_Wk', 'L1_attn_Wv', 'L1_attn_Wo',
         'L1_ffn_weight', 'L1_ffn_bias', 'L1_ffn_so_conv_w', 'L1_ffn_so_conv_b', 'L1_ffn_so_gamma', 'L1_ffn_so_beta', 'L1_ffn_so_lin_w',
         'L1_ffn_so_lin_b', 'L1_ffn_si_conv_w', 'L1_ffn_si_conv_b', 'L1_ffn_si_gamma', 'L1_ffn_si_beta', 'L1_ffn_si_lin_w', 'L1_ffn_si_lin_b']


def kernel(**inputs):
    import concourse.bacc as _bacc
    from concourse.bass_utils import run_bass_kernel_spmd as _run
    nc = _bacc.Bacc("TRN2", target_bir_lowering=False, num_devices=1)
    packed, where, rope = shape_constants()
    arrays = {n: np.ascontiguousarray(inputs[n]) for n in NAMES}
    arrays["consts"], arrays["rope"] = packed, rope
    arrays = {"in_" + n: a for n, a in arrays.items()}
    ins = {n[3:]: nc.dram_tensor(n, a.shape, mybir.dt.float32, kind="ExternalInput").ap() for n, a in arrays.items()}
    out = nc.dram_tensor("out_0_dram", (B, T, D), mybir.dt.float32, kind="ExternalOutput").ap()
    build(nc, ins, where, out)
    r = _run(nc, [arrays], core_ids=[0])
    return r.results[0]["out_0_dram"]
```
